# Optimizing a Trainium2 kernel written in Bass

```python
import numpy as np
import jax
import jax.numpy as jnp

def _softmax(x, axis=-1):
    return jax.nn.softmax(x, axis=axis)

def _gelu(x):
    return jax.nn.gelu(x, approximate=True)

def _silu(x):
    return jax.nn.silu(x)

def _sigmoid(x):
    return jax.nn.sigmoid(x)

def _layernorm(x, axis=-1, eps=1e-05):
    m = jnp.mean(x, axis=axis, keepdims=True)
    v = jnp.var(x, axis=axis, keepdims=True)
    return (x - m) / jnp.sqrt(v + eps)

def _scatter_add(tgt, idx, src, axis=0):
    return tgt.at[idx].add(src)

def _segment_sum(src, seg, n):
    return jax.ops.segment_sum(src, seg, n)
kernel_name = 'mk_gps_d1_gnn_r32_1e6ff2'

def setup_inputs(seed: int=0):
    np.random.seed(seed)
    _w = jnp.asarray

    def _rec_inputs():
        import jax
        import jax.numpy as jnp
        _gk = jax.random.key(seed)
        x = -0.0003713 + 1 * jax.random.normal(jax.random.fold_in(_gk, 1), (3125, 256), jnp.float32)
        _s = jax.random.randint(jax.random.fold_in(_gk, 2), (25000,), 0, 3125, jnp.int32)
        _d = jax.random.randint(jax.random.fold_in(_gk, 3), (25000,), 0, 3125, jnp.int32)
        _loop = jnp.arange(3125, dtype=jnp.int32)
        src = jnp.concatenate([_s, _d, _loop])
        dst = jnp.concatenate([_d, _s, _loop])
        _o = jnp.argsort(dst, stable=True)
        src = src[_o]
        dst = dst[_o]
        edge_attr_64 = 0.000189758 + 1.00013 * jax.random.normal(jax.random.fold_in(_gk, 12), (53125, 64), jnp.float32)
        return (x, src, dst, edge_attr_64)
    x, src, dst, edge_attr_64 = _rec_inputs()

    def _L0_gnn_setup():
        import jax, jax.numpy as jnp
        import numpy as np
        N_NODES = 50000
        N_EDGES = 25000
        NODE_IN = 256
        EDGE_OUT = 64
        GLOBAL_IN = 128
        NODE_OUT = 256
        HIDDEN = 512
        N_GRAPHS = 64
        key = jax.random.key(seed)
        ks = jax.random.split(key, 8)
        x = jax.random.normal(ks[0], (N_NODES, NODE_IN), dtype=jnp.float32)
        edge_index = jax.random.randint(ks[1], (2, N_EDGES), 0, N_NODES, dtype=jnp.int64)
        edge_attr = jax.random.normal(ks[2], (N_EDGES, EDGE_OUT), dtype=jnp.float32)
        u = jax.random.normal(ks[3], (N_GRAPHS, GLOBAL_IN), dtype=jnp.float32)
        batch = jnp.sort(jax.random.randint(ks[4], (N_NODES,), 0, N_GRAPHS, dtype=jnp.int64))
        in_dim = NODE_IN + EDGE_OUT + GLOBAL_IN
        b1s = 1.0 / np.sqrt(in_dim)
        b2s = 1.0 / np.sqrt(HIDDEN)
        W1 = jax.random.uniform(ks[5], (in_dim, HIDDEN), dtype=jnp.float32, minval=-b1s, maxval=b1s)
        b1 = jnp.zeros((HIDDEN,), dtype=jnp.float32)
        W2 = jax.random.uniform(ks[6], (HIDDEN, NODE_OUT), dtype=jnp.float32, minval=-b2s, maxval=b2s)
        b2 = jnp.zeros((NODE_OUT,), dtype=jnp.float32)
        return {'x': x, 'edge_index': edge_index, 'edge_attr': edge_attr, 'u': u, 'batch': batch, 'W1': W1, 'b1': b1, 'W2': W2, 'b2': b2}
    _L0_gnn_all = _L0_gnn_setup()
    _L0_gnn_in = {k: v for k, v in _L0_gnn_all.items() if k in ('u', 'W1', 'b1', 'W2', 'b2')}
    del _L0_gnn_all

    def _L0_mix_setup():
        import jax, jax.numpy as jnp
        import numpy as np
        A, Bc, Cc = (0.5, 1.0, 1.0)
        H = 8
        EPS = 1e-12

        def _normalize(t):
            n = jnp.linalg.norm(t, axis=-1, keepdims=True)
            return t / jnp.maximum(n, EPS)
        key = jax.random.key(seed)
        ks = jax.random.split(key, 5)
        B, N, C = (8, 64, 256)
        D = C // H
        x = jax.random.normal(ks[0], (B, N, C), dtype=jnp.float32)
        Wqkv = jax.random.normal(ks[1], (3 * H * D, C), dtype=jnp.float32) * 0.02
        bqkv = jnp.zeros((3 * H * D,), dtype=jnp.float32)
        Wproj = jax.random.normal(ks[2], (C, H * D), dtype=jnp.float32) * 0.02
        bproj = jnp.zeros((C,), dtype=jnp.float32)
        temperature = jnp.ones((1, H, 1, 1), dtype=jnp.float32)
        return {'x': x, 'Wqkv': Wqkv, 'bqkv': bqkv, 'Wproj': Wproj, 'bproj': bproj, 'temperature': temperature}
    _L0_mix_all = _L0_mix_setup()
    _L0_mix_in = {k: v for k, v in _L0_mix_all.items() if k in ('Wqkv', 'bqkv', 'Wproj', 'bproj', 'temperature')}
    del _L0_mix_all

    def _L0_ffn_setup():
        import jax, jax.numpy as jnp
        import numpy as np
        NUM_EXPERTS = 8
        TOP_K = 2
        B, S, D = (8, 256, 256)

        def _moe(tokens, router_w, w1, b1, w2, b2):
            N = tokens.shape[0]
            E = router_w.shape[0]
            logits = tokens.astype(jnp.float32) @ router_w.astype(jnp.float32).T
            probs = jax.nn.softmax(logits, axis=-1)
            rw, re = jax.lax.top_k(probs, TOP_K)
            if TOP_K > 1:
                rw = rw / jnp.maximum(rw.sum(-1, keepdims=True), 1e-12)
            rw = rw.astype(tokens.dtype)
            combine = jnp.zeros((N, E), tokens.dtype).at[jnp.arange(N)[:, None], re].set(rw)
            out = tokens
            for e in range(E):
                h = jax.nn.gelu(tokens @ w1[e] + b1[e], approximate=False)
                y = h @ w2[e] + b2[e]
                out = out + combine[:, e:e + 1] * y
            return out
        key = jax.random.key(seed)
        ks = jax.random.split(key, 4)
        scale = 1.0 / np.sqrt(D).astype(np.float32)
        return {'input_embeddings': jax.random.normal(ks[0], (B, S, D), jnp.float32), 'router_w': jax.random.normal(ks[1], (NUM_EXPERTS, D), jnp.float32) * scale, 'w1': jax.random.normal(ks[2], (NUM_EXPERTS, D, D), jnp.float32) * scale, 'b1': jnp.zeros((NUM_EXPERTS, D), jnp.float32), 'w2': jax.random.normal(ks[3], (NUM_EXPERTS, D, D), jnp.float32) * scale, 'b2': jnp.zeros((NUM_EXPERTS, D), jnp.float32)}
    _L0_ffn_all = _L0_ffn_setup()
    _L0_ffn_in = {k: v for k, v in _L0_ffn_all.items() if k in ('router_w', 'w1', 'b1', 'w2', 'b2')}
    del _L0_ffn_all
    return {'x': x, 'src': src, 'dst': dst, 'edge_attr_64': edge_attr_64, 'L0_gnn_u': _L0_gnn_in['u'], 'L0_gnn_W1': _L0_gnn_in['W1'], 'L0_gnn_b1': _L0_gnn_in['b1'], 'L0_gnn_W2': _L0_gnn_in['W2'], 'L0_gnn_b2': _L0_gnn_in['b2'], 'L0_mix_Wqkv': _L0_mix_in['Wqkv'], 'L0_mix_bqkv': _L0_mix_in['bqkv'], 'L0_mix_Wproj': _L0_mix_in['Wproj'], 'L0_mix_bproj': _L0_mix_in['bproj'], 'L0_mix_temperature': _L0_mix_in['temperature'], 'L0_ffn_router_w': _L0_ffn_in['router_w'], 'L0_ffn_w1': _L0_ffn_in['w1'], 'L0_ffn_b1': _L0_ffn_in['b1'], 'L0_ffn_w2': _L0_ffn_in['w2'], 'L0_ffn_b2': _L0_ffn_in['b2']}

def reference(x, src, dst, edge_attr_64, L0_gnn_u, L0_gnn_W1, L0_gnn_b1, L0_gnn_W2, L0_gnn_b2, L0_mix_Wqkv, L0_mix_bqkv, L0_mix_Wproj, L0_mix_bproj, L0_mix_temperature, L0_ffn_router_w, L0_ffn_w1, L0_ffn_b1, L0_ffn_w2, L0_ffn_b2):
    import jax
    import jax.numpy as jnp

    def _L0_gnn_ref(x, edge_index, edge_attr, u, batch, W1, b1, W2, b2):
        import jax, jax.numpy as jnp
        import numpy as np
        N_NODES = 50000
        N_EDGES = 25000
        NODE_IN = 256
        EDGE_OUT = 64
        GLOBAL_IN = 128
        NODE_OUT = 256
        HIDDEN = 512
        N_GRAPHS = 64
        n = x.shape[0]
        src = edge_index[0]
        sums = jax.ops.segment_sum(edge_attr, src, num_segments=n)
        counts = jax.ops.segment_sum(jnp.ones((edge_attr.shape[0],), edge_attr.dtype), src, num_segments=n)
        edge_attr_agg = sums / jnp.maximum(counts, 1.0)[:, None]
        u_expanded = u[batch]
        combined = jnp.concatenate([x, edge_attr_agg, u_expanded], axis=1)
        h = jax.nn.relu(combined @ W1 + b1)
        return h @ W2 + b2

    def _L0_mix_ref(x, Wqkv, bqkv, Wproj, bproj, temperature):
        import jax, jax.numpy as jnp
        import numpy as np
        A, Bc, Cc = (0.5, 1.0, 1.0)
        H = 8
        EPS = 1e-12

        def _normalize(t):
            n = jnp.linalg.norm(t, axis=-1, keepdims=True)
            return t / jnp.maximum(n, EPS)
        B, N, C = x.shape
        D = C // H
        scale = float(D) ** 0.25
        qkv = (x @ Wqkv.T + bqkv).reshape(B, N, 3, H, D)
        qkv = jnp.transpose(qkv, (2, 0, 3, 1, 4))
        q, k, v = (qkv[0], qkv[1], qkv[2])
        q = q * scale
        v1 = jnp.concatenate([jnp.ones((B, H, N, 1), dtype=v.dtype), v], axis=-1)
        qn = _normalize(q) * (scale * temperature)
        kn = _normalize(k) * scale
        vN = v1 / N
        kv_mod = jnp.einsum('bhni,bhnj,bhne->bhije', kn, kn, vN)
        kv = jnp.einsum('bhnd,bhne->bhde', kn, vN)
        vsum = jnp.sum(vN, axis=-2)[:, :, None, :]
        y = A * jnp.einsum('bhni,bhnj,bhije->bhne', qn, qn, kv_mod) + scale ** 2 * Bc * jnp.einsum('bhnd,bhde->bhne', qn, kv) + scale ** 4 * Cc * vsum
        y_norm, y = (y[..., :1], y[..., 1:])
        y = y / y_norm
        out = jnp.transpose(y, (0, 2, 1, 3)).reshape(B, N, H * D)
        return out @ Wproj.T + bproj

    def _L0_ffn_ref(input_embeddings, router_w, w1, b1, w2, b2):
        import jax, jax.numpy as jnp
        import numpy as np
        NUM_EXPERTS = 8
        TOP_K = 2
        B, S, D = (8, 256, 256)

        def _moe(tokens, router_w, w1, b1, w2, b2):
            N = tokens.shape[0]
            E = router_w.shape[0]
            logits = tokens.astype(jnp.float32) @ router_w.astype(jnp.float32).T
            probs = jax.nn.softmax(logits, axis=-1)
            rw, re = jax.lax.top_k(probs, TOP_K)
            if TOP_K > 1:
                rw = rw / jnp.maximum(rw.sum(-1, keepdims=True), 1e-12)
            rw = rw.astype(tokens.dtype)
            combine = jnp.zeros((N, E), tokens.dtype).at[jnp.arange(N)[:, None], re].set(rw)
            out = tokens
            for e in range(E):
                h = jax.nn.gelu(tokens @ w1[e] + b1[e], approximate=False)
                y = h @ w2[e] + b2[e]
                out = out + combine[:, e:e + 1] * y
            return out
        b, s, d = input_embeddings.shape
        tokens = input_embeddings.reshape(b * s, d)
        return _moe(tokens, router_w, w1, b1, w2, b2).reshape(b, s, d)
    edge_index = jnp.stack([src, dst])
    batch0 = jnp.zeros((3125,), jnp.int32)
    xn = _layernorm(x, axis=-1)
    x = x + _L0_gnn_ref(xn, edge_index, edge_attr_64, L0_gnn_u, batch0, L0_gnn_W1, L0_gnn_b1, L0_gnn_W2, L0_gnn_b2) + _L0_mix_ref(xn[None], L0_mix_Wqkv, L0_mix_bqkv, L0_mix_Wproj, L0_mix_bproj, L0_mix_temperature)[0]
    x = x + _L0_ffn_ref(_layernorm(x, axis=-1)[None], L0_ffn_router_w, L0_ffn_w1, L0_ffn_b1, L0_ffn_w2, L0_ffn_b2)[0]
    return x

_drawn_inputs = setup_inputs


def setup_inputs(seed=0):
    import zlib

    import numpy as np

    out = dict(_drawn_inputs(seed))
    spreads = {'L0_gnn_b1': (0.0, 0.1),
     'L0_gnn_b2': (0.0, 0.1),
     'L0_mix_bqkv': (0.0, 0.1),
     'L0_mix_bproj': (0.0, 0.1),
     'L0_mix_temperature': (1.0, 0.6),
     'L0_ffn_b1': (0.0, 0.328),
     'L0_ffn_b2': (0.0, 0.1)}
    factors = {'L0_mix_Wqkv': 8.0}
    for name, (base, spread) in spreads.items():
        noise = np.random.default_rng([zlib.crc32(name.encode()), seed]).standard_normal(out[name].shape)
        drawn = base * np.exp(spread * noise) if base else spread * noise
        out[name] = jnp.asarray(drawn.astype(out[name].dtype))
    for name, factor in factors.items():
        out[name] = (out[name] * factor).astype(out[name].dtype)
    return out
```

```python
import concourse.bass as bass
from concourse import mybir
from contextlib import ExitStack

fp32 = mybir.dt.float32
bf16 = mybir.dt.bfloat16
i32 = mybir.dt.int32
u32 = mybir.dt.uint32
ALU = mybir.AluOpType
ACT = mybir.ActivationFunctionType
AX = mybir.AxisListType


def gps_layer(nc, x, src, edge_attr, u_in, W1, b1, W2, b2, WqkvT, bqkv, WprojT, bproj, temperature,
              routerT, ew1, eb1, ew2, eb2, out):
    N, C = x.shape
    P = 125
    T = N // P
    EA = edge_attr.shape[1]
    ET = src.shape[0] // P
    HID = W1.shape[1]
    MC = HID // 128
    KC = C // 128
    H = temperature.shape[0]
    D = C // H
    E = ew1.shape[0]
    OFF = 16
    QC = OFF * D // 128
    LF = 16 + D + 1
    VE = D + 1
    S = 128
    GT = 4
    NG = (N * 0 + src.shape[0] + T * (GT * S - 1)) // (GT * S) + 1
    NG += -NG % 3
    ST = NG * GT
    RT = 12
    RG = RT // GT
    NR = ST // RT
    F = EA + 2
    BPB = 7
    CH = 17
    NCH = ET // CH
    BANK = 512
    LN_EPS = 1e-5
    EPS2 = 1e-24
    SC = float(D) ** 0.25
    SC2, SC4 = SC * SC, SC ** 4
    GAP = BANK - BPB * F
    assert NR % 2 == 1 and NCH % 2 == 1 and T == 25

    ctx = ExitStack()
    with ctx:
        def sb(name, shape, dt=fp32):
            return ctx.enter_context(nc.sbuf_tensor(name, shape, dt))

        def sem(name):
            return ctx.enter_context(nc.semaphore(name))

        sorted_rows = nc.dram_tensor("sorted_rows", (S * ST, F), fp32, kind="Internal").ap()
        hpre_dram = nc.dram_tensor("hpre_rows", (T * 128, MC * P), fp32, kind="Internal").ap()
        sorted_v = sorted_rows.rearrange("(p t) f -> p t f", p=S)

        x_res = sb("x_res", [P, T, C])
        stage = sb("stage", [P, 2, CH, F])
        idx = sb("idx", [P, 2, CH], u32)
        src_f = sb("src_f", [P, ET])
        addr = sb("addr", [P, ET], u32)
        zeros = sb("zeros", [128, RT * F])
        ones = sb("ones", [128, 128])
        ones_b = sb("ones_b", [P, 1], bf16)
        ident = sb("ident", [128, 128])
        upper = sb("upper", [P, P])
        iota_c = sb("iota_c", [128, P])
        wqkv = sb("wqkv", [128, KC, 3 * C])
        w1x = sb("w1x", [128, KC, HID])
        w1u = sb("w1u", [128, HID])
        w1a = sb("w1a", [EA + 1, HID])
        w2s = sb("w2s", [128, MC, C])
        wproj = sb("wproj", [128, KC, C])
        wr = sb("wr", [128, KC, E])
        bqkv_r = sb("bqkv_r", [1, 3 * C])
        brows = sb("brows", [1, 3, HID])
        u0 = sb("u0", [128, 1])
        temp = sb("temp", [P, H])
        eb1_s = sb("eb1_s", [128, E, KC])
        eb2_s = sb("eb2_s", [E, C])
        stats = sb("stats", [P, T, 6])
        mv = sb("mv", [P, T, 2])
        rstd = sb("rstd", [P, T])
        mask = sb("mask", [2 * LF, 2 * VE])
        sq_half = sb("sq_half", [128, 1])
        bt = sb("bt", [128, NG])
        off_i = sb("off_i", [1, NG], i32)

        r1 = sb("r1", [128, 17700])
        r1_off = [0]

        def carve(shape, dt=fp32, parts=None, at=None):
            n = 1
            for s in shape[1:]:
                n *= s
            words = (n + 1) // 2 if dt == bf16 else n
            o = r1_off[0] if at is None else at
            if at is None:
                r1_off[0] += words
            assert o + words <= 17700, o + words
            v = r1[0:shape[0], o:o + words]
            if dt != fp32:
                v = v.bitcast(dt)
                if dt == bf16:
                    v = v[:, 0:n]
            if len(shape) == 3:
                v = v.rearrange("p (a b) -> p a b", a=shape[1])
            elif len(shape) == 4:
                v = v.rearrange("p (a b c) -> p a b c", a=shape[1], b=shape[2])
            elif len(shape) == 5:
                v = v.rearrange("p (a b c d) -> p a b c d", a=shape[1], b=shape[2], c=shape[3])
            return v

        cum = carve([P, T, ET])
        ge = carve([P, T + 1, ET], bf16, at=0)
        oneh = carve([P, T, ET], bf16)
        pos = carve([P, ET])
        pos_i = carve([P, ET], i32)
        slot_t = carve([P, ET], i32)
        slot_p = carve([P, ET], i32)
        src_i = sb("src_i", [P, ET], i32)
        thr = sb("thr", [P, T + 1])
        iota_g = sb("iota_g", [T, NG])
        clast = sb("clast", [P, T + 1])
        per_part = sb("per_part", [P, T])
        tot_i = sb("tot_i", [128, T], i32)
        padded = sb("padded", [128, T])
        start = sb("start", [128, T + 1])
        base = sb("base", [P, T])
        startT = sb("startT", [T, 1])
        geg = sb("geg", [T, NG])
        off_f = sb("off_f", [1, NG])
        off_g = sb("off_g", [1, NG])
        r1_off[0] = 0
        q_all = carve([P, T, C])
        hpre = carve([128, 2, MC * P])
        after_q = r1_off[0]
        xn = carve([P, 2, C])
        xT = carve([128, 2, KC, P])
        kdup = carve([P, 2, H, 2 * D])
        vn = carve([P, 2, H, VE])
        vr = carve([P, 2, H, VE])
        last = carve([P, 2, H, LF])
        mq = carve([128, H, QC, VE])
        ml = carve([2 * LF, H // 2, 2 * VE])
        phT = carve([128, 3, QC * P])
        y1 = carve([P, 2, H * VE])
        attn = carve([P, 2, C])
        attnT = carve([128, 2, KC, P])
        ssq = carve([P, 2, H])
        nm = carve([P, 2, H])
        r2 = carve([P, 2, H])
        rr = carve([P, 2, H])
        rq = carve([P, 2, H])
        rq2 = carve([P, 2, H])
        ry = carve([P, 2, H])
        tokT = carve([128, KC, T * P], at=0)
        r1_off[0] = after_q
        agg = carve([P, T, EA + 1])
        cnt = carve([P, T])
        agr = carve([P, 2, EA + 1])
        agT = carve([EA + 1, 2, P])
        hs = carve([128, 2, MC * P])
        x2 = carve([P, 2, C])
        xl = carve([P, 2, C])
        tokr = carve([128, 2, KC * P])
        st2 = carve([P, 2, 6])
        mv2 = carve([P, 2, 2])
        sd2 = carve([P, 2, 1])
        rs2 = carve([P, 2, 1])
        lg = carve([P, T, E])
        pr = carve([P, T, E])
        pw = carve([P, T, E])
        eq = carve([P, T, E])
        pick = carve([P, T, E])
        comb = carve([P, T, E])
        red = carve([P, T])
        top1 = carve([P, T])
        top2 = carve([P, T])
        cr = carve([P, 2, E])
        cT = carve([E, 2, P])
        hg = carve([128, 2, KC * P])
        o_s = carve([P, 2, C])
        rank8 = sb("rank8", [P, E])

        NW = E * KC * C
        r2t = sb("r2t", [128, 2 * NW])
        phi = r2t[0:P, 0:2 * H * OFF * D].rearrange("p (u h o d) -> p u h o d", u=2, h=H, o=OFF)
        srt = r2t[:, 0:2 * RT * F].rearrange("p (u t f) -> p u t f", u=2, t=RT)
        o1 = 2 * RT * F
        oh = r2t[:, o1:o1 + 2 * RT * P].rearrange("p (u t c) -> p u t c", u=2, t=RT)
        key = sb("key", [128, 2, RT])
        ew1_s = r2t[:, 0:NW].rearrange("p (e k n) -> p e k n", e=E, k=KC)
        ew2_s = r2t[:, NW:2 * NW].rearrange("p (e k n) -> p e k n", e=E, k=KC)

        ps = ctx.enter_context(nc.psum_tensor("ps", [128, 8 * BANK], fp32))

        def bank(b, parts=128, a=0, z=BANK):
            return ps[0:parts, b * BANK + a:b * BANK + z]

        gate = sem("gate")
        src_loaded = sem("src_loaded")
        x_loaded = sem("x_loaded")
        w_loaded = sem("w_loaded")
        consts = sem("consts")
        zero_filled = sem("zero_filled")
        dve_step = sem("dve_step")
        pool_step = sem("pool_step")
        bias_ready = sem("bias_ready")
        brow_ps = sem("brow_ps")
        counted = sem("counted")
        totals_ps = sem("totals_ps")
        starts = sem("starts")
        starts_ps = sem("starts_ps")
        geg_ready = sem("geg_ready")
        groups_ps = sem("groups_ps")
        addr_ready = sem("addr_ready")
        offs_ready = sem("offs_ready")
        var_ready = sem("var_ready")
        std_ready = sem("std_ready")
        chunk_loaded = [sem(f"chunk_loaded{h}") for h in range(2)]
        chunk_keyed = sem("chunk_keyed")
        scattered = [sem(f"scattered{h}") for h in range(2)]
        m_zeroed = sem("m_zeroed")
        xn_ready = sem("xn_ready")
        xT_ps = sem("xT_ps")
        xT_ready = sem("xT_ready")
        k_ps = sem("k_ps")
        vq_ps = sem("vq_ps")
        h_ps = sem("h_ps")
        kdup_ready = sem("kdup_ready")
        vn_ready = sem("vn_ready")
        vq_free = sem("vq_free")
        hpre_ready = sem("hpre_ready")
        hpre_stored = [sem(f"hpre_stored{h}") for h in range(2)]
        phi_ready = sem("phi_ready")
        ssq_ready = sem("ssq_ready")
        nm_ready = sem("nm_ready")
        inv_ready = sem("inv_ready")
        rk2_ready = sem("rk2_ready")
        rk_ready = sem("rk_ready")
        vr_ready = sem("vr_ready")
        kn_ready = sem("kn_ready")
        last_ready = sem("last_ready")
        m_added = sem("m_added")
        m_ready = sem("m_ready")
        q_ps = sem("q_ps")
        qdup_ready = sem("qdup_ready")
        qphi_ready = [sem(f"qphi_ready{h}") for h in range(2)]
        qssq_ready = sem("qssq_ready")
        qnm_ready = sem("qnm_ready")
        qinv_ready = sem("qinv_ready")
        qsq_ready = sem("qsq_ready")
        rq_ready = sem("rq_ready")
        rq2_ready = sem("rq2_ready")
        qn_ready = sem("qn_ready")
        qlast_ready = sem("qlast_ready")
        NJ = H + 1
        phT_ps = [sem(f"phT_ps{j}") for j in range(3)]
        phT_ready = [sem(f"phT_ready{j}") for j in range(3)]
        y_ps = [sem(f"y_ps{j}") for j in range(3)]
        y_scaled = sem("y_scaled")
        y_taken = sem("y_taken")
        ry_ready = sem("ry_ready")
        attn_ready = sem("attn_ready")
        attnT_ps = sem("attnT_ps")
        attnT_ready = sem("attnT_ready")
        proj_ps = sem("proj_ps")
        x1_ready = sem("x1_ready")
        acc_zeroed = sem("acc_zeroed")
        rows_loaded = [sem(f"rows_loaded{h}") for h in range(2)]
        key_ready = sem("key_ready")
        onehot_ready = sem("onehot_ready")
        rows_used = sem("rows_used")
        agg_ready = sem("agg_ready")
        ew_loaded = sem("ew_loaded")
        hpre_back = [sem(f"hpre_back{h}") for h in range(2)]
        agr_ready = sem("agr_ready")
        agT_ps = sem("agT_ps")
        agT_ready = sem("agT_ready")
        ha_ps = sem("ha_ps")
        hsum_ready = sem("hsum_ready")
        hs_ready = sem("hs_ready")
        gnn_ps = sem("gnn_ps")
        x2_ready = sem("x2_ready")
        st2_ready = sem("st2_ready")
        mv2_ready = sem("mv2_ready")
        ve2_ready = sem("ve2_ready")
        sd2_ready = sem("sd2_ready")
        rs2_ready = sem("rs2_ready")
        xl_ready = sem("xl_ready")
        res_ready = sem("res_ready")
        tok_ps = sem("tok_ps")
        tokr_ready = sem("tokr_ready")
        tokT_ready = sem("tokT_ready")
        lg_ps = sem("lg_ps")
        lg_ready = sem("lg_ready")
        sh_ready = sem("sh_ready")
        ex_ready = sem("ex_ready")
        comb_ready = sem("comb_ready")
        cr_ready = sem("cr_ready")
        cT_ps = sem("cT_ps")
        cT_ready = sem("cT_ready")
        cb_ps = sem("cb_ps")
        o_ready = sem("o_ready")
        eh_ps = [sem(f"eh_ps{e}") for e in range(2)]
        hg_ready = [sem(f"hg_ready{e}") for e in range(2)]
        ey_ps = [sem(f"ey_ps{e}") for e in range(2)]
        stored = [sem(f"stored{h}") for h in range(2)]

        block = ctx.enter_context(nc.Block())

        def wait(eng, s, n):
            if not (isinstance(n, int) and n <= 0):
                eng.wait_ge(s, n)

        def hold(eng, s, n):
            if not (isinstance(n, int) and n <= 0):
                eng.wait_ge(s, n)
                eng.sem_inc(gate)

        def tiles(eng, body, lo, ahead, behind):
            hi = T - ahead
            n = (hi - lo) // 2
            for t in range(lo):
                body(t, t % 2, t // 2)
            with eng.Fori(0, n) as i:
                for k in range(2):
                    body(i * 2 + (lo + k), (lo + k) % 2, i + (lo + k) // 2)
            for t in range(lo + 2 * n, T + behind):
                body(t, t % 2, t // 2)

        def inside(t):
            return not isinstance(t, int) or 0 <= t < T

        def overlapped(v, u):
            w = v[:, u, :, :]
            return bass.AP(w.tensor, w.offset, [w.ap[0], [2 * D, H], [1, OFF], [1, D]])

        def seat(j):
            return (4 + j // 15, j % 15 * VE) if j < H * QC else (6, 2 * VE + (j - H * QC) * 2 * VE)

        ONES_ROW = ones[0:1, 0:P]

        @block.sync
        def _(sp):
            sp.dma_start(src_i[:, :], src.rearrange("(p j) -> p j", p=P)).then_inc(src_loaded, 16)
            sp.dma_start(x_res[:, :, :], x.rearrange("(t p) c -> p t c", p=P)).then_inc(x_loaded, 16)
            sp.wait_ge(consts, 1)
            with sp.Fori(0, NR) as c:
                sp.dma_start(sorted_v[:, bass.ds(c * RT, RT), :],
                             zeros[:, :].rearrange("p (t f) -> p t f", f=F)).then_inc(zero_filled, 16)
            ea = edge_attr.rearrange("(p j) f -> p j f", p=P)

            def load_chunk(c, h):
                sp.dma_start(stage[:, h, :, 0:EA], ea[:, bass.ds(c * CH, CH), :]).then_inc(chunk_loaded[h], 16)

            load_chunk(0, 0)
            load_chunk(1, 1)
            with sp.Fori(0, NCH // 2 - 1) as i:
                for h in range(2):
                    sp.wait_ge(scattered[h], i * (16 * CH) + 16 * CH)
                    load_chunk(i * 2 + (2 + h), h)
            sp.wait_ge(scattered[0], (NCH // 2) * 16 * CH)
            load_chunk(NCH - 1, 0)

            sp.wait_ge(scattered[0], (NCH // 2 + 1) * 16 * CH)
            sp.wait_ge(scattered[1], (NCH // 2) * 16 * CH)
            sp.wait_ge(x1_ready, T)

            def load_rows(c, h):
                sp.dma_start(srt[:, h, :, :], sorted_v[:, bass.ds(c * RT, RT), :]).then_inc(rows_loaded[h], 16)

            load_rows(0, 0)
            load_rows(1, 1)
            with sp.Fori(0, NR // 2 - 1) as i:
                for h in range(2):
                    sp.wait_ge(rows_used, i * 2 + (h + 1))
                    load_rows(i * 2 + (2 + h), h)
            sp.wait_ge(rows_used, NR - 2)
            load_rows(NR - 1, 0)
            hv = hpre_dram.rearrange("(t p) c -> t p c", p=128)

            def load_hpre(t, u, k):
                if not inside(t):
                    return
                wait(sp, hsum_ready, t - 1)
                sp.dma_start(hpre[:, u, :], hv[bass.ds(t, 1), :, :].rearrange("a p c -> (a p) c")).then_inc(hpre_back[u], 16)
            sp.wait_ge(hpre_stored[0], 16 * (T // 2 + 1))
            sp.wait_ge(hpre_stored[1], 16 * (T // 2))
            load_hpre(0, 0, 0)
            load_hpre(1, 1, 0)
            sp.wait_ge(rows_used, NR)
            sp.dma_start(ew1_s, ew1.rearrange("e (k p) n -> p e k n", p=128)).then_inc(ew_loaded, 16)
            sp.dma_start(ew2_s, ew2.rearrange("e (k p) n -> p e k n", p=128)).then_inc(ew_loaded, 16)
            for t in (2, 3):
                load_hpre(t, t % 2, 0)
            with sp.Fori(0, (T - 5) // 2) as i:
                for k in range(2):
                    load_hpre(i * 2 + (4 + k), k, 0)
            load_hpre(T - 1, 0, 0)

            def store(t, u, k):
                sp.wait_ge(o_ready, t * (E + 1) + (E + 1))
                sp.dma_start(out.rearrange("(t p) c -> t p c", p=P)[bass.ds(t, 1), :, :].rearrange("a p c -> (a p) c"),
                             o_s[:, u, :]).then_inc(stored[u], 16)
            tiles(sp, store, 1, 0, 0)
            sp.wait_ge(stored[0], 16 * (T // 2 + 1))
            sp.wait_ge(stored[1], 16 * (T // 2))

        @block.gpsimd
        def _(pool):
            n = [0]

            def iota(v, pattern, cm=0):
                pool.iota(v, pattern, base=0, channel_multiplier=cm,
                          allow_small_or_imprecise_dtypes=True).then_inc(consts, 1)

            pool.memset(zeros[:, :], 0.0).then_inc(consts, 1)
            iota(thr[:, :], [[P, T + 1]])
            iota(iota_g[:, :], [[S * GT, NG]])
            iota(iota_c[:, :], [[1, P]])
            pool.memset(ones[:, :], 1.0).then_inc(consts, 1)
            pool.memset(ident[:, :], 0.0).then_inc(consts, 1)
            pool.memset(upper[:, :], 0.0).then_inc(consts, 1)
            pool.memset(stage[:, :, :, EA + 1:EA + 2], 1.0).then_inc(consts, 1)
            iota(rank8[:, :], [[-1, E]])
            pool.memset(mask[:, :], SC4).then_inc(consts, 1)
            pool.memset(sq_half[:, :], 1.0).then_inc(consts, 1)
            pool.wait_ge(consts, 11)
            pool.affine_select(out=ident[:, :], in_=ident[:, :], compare_op=ALU.not_equal, fill=1.0, base=0,
                               pattern=[[-1, 128]], channel_multiplier=1).then_inc(consts, 1)
            pool.affine_select(out=upper[:, :], in_=upper[:, :], compare_op=ALU.is_ge, fill=1.0, base=0,
                               pattern=[[-1, P]], channel_multiplier=1).then_inc(consts, 1)
            pool.affine_select(out=sq_half[:, :], in_=sq_half[:, :], compare_op=ALU.is_ge, fill=0.5, base=-D,
                               pattern=[[0, 1]], channel_multiplier=1).then_inc(consts, 1)
            for lo, w in ((2 * LF - 1, SC2), (LF + 16, 1.0), (LF, SC4), (LF - 1, SC2), (16, 1.0)):
                pool.affine_select(out=mask[:, :], in_=mask[:, :], compare_op=ALU.is_ge, fill=w, base=-lo,
                                   pattern=[[0, 2 * VE]], channel_multiplier=1).then_inc(pool_step, 1)
                n[0] += 1
                pool.wait_ge(pool_step, n[0])
            pool.affine_select(out=mask[:, 0:VE], in_=mask[:, 0:VE], compare_op=ALU.is_ge, fill=0.0, base=LF - 1,
                               pattern=[[0, VE]], channel_multiplier=-1).then_inc(consts, 1)
            pool.affine_select(out=mask[:, VE:2 * VE], in_=mask[:, VE:2 * VE], compare_op=ALU.is_ge, fill=0.0, base=-LF,
                               pattern=[[0, VE]], channel_multiplier=1).then_inc(consts, 1)

            pool.wait_ge(addr_ready, 1)
            pool.wait_ge(zero_filled, 16 * NR)

            def scatter(c, h, nth):
                hold(pool, chunk_loaded[h], nth * 16)
                if not (isinstance(nth, int) and nth == 1):
                    hold(pool, scattered[h], nth * (16 * CH) - 16 * CH)
                pool.tensor_copy(idx[:, h, :], addr[:, bass.ds(c * CH, CH)]).then_inc(chunk_keyed, 1)
                pool.tensor_copy(stage[:, h, :, EA:EA + 1],
                                 src_f[:, bass.ds(c * CH, CH)].unsqueeze(2)).then_inc(chunk_keyed, 1)
                hold(pool, chunk_keyed, c * 2 + 2)
                for j in range(CH):
                    pool.indirect_dma_start(out=sorted_rows,
                                            out_offset=bass.IndirectOffsetOnAxis(ap=idx[:, h, j:j + 1], axis=0),
                                            in_=stage[:, h, j, :], in_offset=None).then_inc(scattered[h], 16)
            scatter(0, 0, 1)
            scatter(1, 1, 1)
            with pool.Fori(0, NCH // 2 - 1) as i:
                for h in range(2):
                    scatter(i * 2 + (2 + h), h, i + 2)
            scatter(NCH - 1, 0, NCH // 2 + 1)

            def res(t, u):
                if not inside(t):
                    return
                hold(pool, xl_ready, t + 1)
                pool.tensor_tensor(x_res[:, bass.ds(t, 1), :].rearrange("p a c -> p (a c)"), x2[:, u, :], xl[:, u, :],
                                   ALU.add).then_inc(res_ready, 1)

            def tok(t, u):
                if not inside(t):
                    return
                hold(pool, tokr_ready, t + 1)
                pool.tensor_copy(tokT[:, :, bass.ds(t * P, P)],
                                 tokr[:, u, :].rearrange("p (k c) -> p k c", k=KC)).then_inc(tokT_ready, 1)

            def body(t, u, k):
                res(t - 2, u)
                tok(t - 3, 1 - u)
            tiles(pool, body, 6, 3, 4)

        @block.scalar
        def _(act):
            def load(dst, s, slow=False):
                act.dma_start(dst, s, allow_slow_non_contiguous=slow).then_inc(w_loaded, 16)

            load(wqkv[:, :, :], WqkvT.rearrange("(k p) n -> p k n", p=128))
            load(w1x[:, :, :], W1[0:C, :].rearrange("(k p) n -> p k n", p=128))
            load(w1a[1:EA + 1, :], W1[C:C + EA, :])
            load(w1u[:, :], W1[C + EA:C + EA + 128, :])
            load(bqkv_r[:, :], bqkv.rearrange("(a n) -> a n", a=1))
            load(brows[:, 0, :], b1.rearrange("(a n) -> a n", a=1))
            load(brows[:, 1, 0:C], bproj.rearrange("(a n) -> a n", a=1))
            load(brows[:, 2, 0:C], b2.rearrange("(a n) -> a n", a=1))
            load(u0[:, :], u_in[0:1, :].rearrange("a p -> p a"), slow=True)
            load(temp[:, :], temperature.rearrange("(a n) -> a n", a=1).to_broadcast([P, H]))
            load(wproj[:, :, :], WprojT.rearrange("(k p) n -> p k n", p=128))
            load(w2s[:, :, :], W2.rearrange("(k p) n -> p k n", p=128))
            load(wr[:, :, :], routerT.rearrange("(k p) n -> p k n", p=128))
            load(eb1_s[:, :, :], eb1.rearrange("e (k p) -> p e k", p=128), slow=True)
            load(eb2_s[:, :], eb2)

            act.wait_ge(var_ready, 1)
            act.activation(rstd[:, :], rstd[:, :], ACT.Sqrt).then_inc(std_ready, 1)

            def xT_copy(t, u):
                if not inside(t):
                    return
                wait(act, xT_ps, t + 1)
                wait(act, h_ps, t - 1)
                act.activation(xT[:, u, :, :], bank(0, 128, 0, KC * P).rearrange("p (k c) -> p k c", k=KC),
                               ACT.Copy).then_inc(xT_ready, 1)

            def vq_copy(t, u):
                if not inside(t):
                    return
                wait(act, vq_ps, t + 1)
                wait(act, m_added, t - 1)
                act.activation(vn[:, u, :, 0:D], bank(2, P, C, 2 * C).rearrange("p (h d) -> p h d", h=H),
                               ACT.Copy, scale=1.0 / N).then_inc(vn_ready, 1)
                act.activation(q_all[:, bass.ds(t, 1), :].rearrange("p a c -> p (a c)"), bank(2, P, 0, C),
                               ACT.Copy).then_inc(vq_free, 1)

            def pass1(t, u, k):
                if inside(t):
                    wait(act, k_ps, t + 1)
                    wait(act, phi_ready, t - 1)
                    act.activation(kdup[:, u, :, :].rearrange("p h (a d) -> p h a d", a=2),
                                   bank((1, 7)[u], P, 0, C).rearrange("p (h d) -> p h d", h=H).unsqueeze(2)
                                   .to_broadcast([P, H, 2, D]), ACT.Copy).then_inc(kdup_ready, 1)
                    vq_copy(t, u)
                if inside(t - 1):
                    v = 1 - u
                    wait(act, rk2_ready, t)
                    act.activation(rr[:, v, :], r2[:, v, :], ACT.Sqrt).then_inc(rk_ready, 1)
                if inside(t):
                    wait(act, h_ps, t + 1)
                    wait(act, hpre_stored[u], k * 16)
                    act.activation(hpre[:, u, :], bank(3, 128, 0, MC * P), ACT.Copy).then_inc(hpre_ready, 1)
                    hold(act, hpre_ready, t + 1)
                    act.dma_start(hpre_dram[bass.ds(t * 128, 128), :], hpre[:, u, :]).then_inc(hpre_stored[u], 16)
                    xT_copy(t + 1, 1 - u)
            xT_copy(0, 0)
            tiles(act, pass1, 3, 1, 1)

            act.wait_ge(m_ready, 1)

            def q_copy(t, u):
                if not inside(t):
                    return
                wait(act, qn_ready, t - 1)
                qv = q_all[:, bass.ds(t, 1), :]
                act.activation(bank((0, 6)[u], P, 0, C), qv.rearrange("p a c -> p (a c)"), ACT.Copy).then_inc(q_ps, 1)
                act.activation(kdup[:, u, :, :].rearrange("p h (a d) -> p h a d", a=2),
                               qv.rearrange("p a (h d) -> p (a h) d", h=H).unsqueeze(2).to_broadcast([P, H, 2, D]),
                               ACT.Copy).then_inc(qdup_ready, 1)

            def q_root(t, u):
                if not inside(t):
                    return
                wait(act, qinv_ready, t + 1)
                act.activation(rr[:, u, :], r2[:, u, :], ACT.Sqrt).then_inc(qsq_ready, 1)

            def attn_copy(t, u):
                if not inside(t):
                    return
                wait(act, attnT_ps, t + 1)
                act.activation(attnT[:, u, :, :], bank(7, 128, 0, KC * P).rearrange("p (k c) -> p k c", k=KC),
                               ACT.Copy).then_inc(attnT_ready, 1)

            def pass2(t, u, k):
                if inside(t):
                    for j in range(NJ):
                        rows = 128 if j < H else 2 * LF
                        wait(act, phT_ps[j % 3], t * 3 + (j // 3 + 1))
                        wait(act, y_ps[j % 3], t * 3 + j // 3)
                        act.activation(phT[0:rows, j % 3, :], bank(1 + j % 3, rows, 0, QC * P), ACT.Copy).then_inc(phT_ready[j % 3], 1)
                        if j == 2:
                            q_copy(t + 2, u)
                        if j == 5:
                            attn_copy(t - 1, 1 - u)
                        if j == 6:
                            q_root(t + 1, 1 - u)
                else:
                    attn_copy(t - 1, 1 - u)
            q_copy(0, 0)
            q_copy(1, 1)
            q_root(0, 0)
            tiles(act, pass2, 3, 2, 1)

            act.wait_ge(agg_ready, 1)

            def agT_copy(t, u):
                if not inside(t):
                    return
                wait(act, agT_ps, t + 1)
                wait(act, ha_ps, t - 1)
                act.activation(agT[:, u, :], bank(0, EA + 1, 0, P), ACT.Copy).then_inc(agT_ready, 1)

            def relu(t, u):
                if not inside(t):
                    return
                wait(act, hsum_ready, t + 1)
                act.activation(hs[:, u, :], hs[:, u, :], ACT.Relu).then_inc(hs_ready, 1)

            def sd(t, u):
                if not inside(t):
                    return
                wait(act, ve2_ready, t + 1)
                act.activation(sd2[:, u, :], sd2[:, u, :], ACT.Sqrt).then_inc(sd2_ready, 1)

            def tok_copy(t, u):
                if not inside(t):
                    return
                wait(act, tok_ps, t + 1)
                wait(act, lg_ps, t - 1)
                wait(act, tokT_ready, t - 1)
                act.activation(tokr[:, u, :], bank(5, 128, 0, KC * P), ACT.Copy).then_inc(tokr_ready, 1)

            def gnn(t, u, k):
                agT_copy(t + 1, 1 - u)
                relu(t, u)
                sd(t - 1, 1 - u)
                tok_copy(t - 3, 1 - u)
            agT_copy(0, 0)
            tiles(act, gnn, 6, 3, 4)

            act.wait_ge(sh_ready, 1)
            act.activation(pr[:, :, :], pr[:, :, :], ACT.Exp).then_inc(ex_ready, 1)

            def cT_copy(t, u):
                if not inside(t):
                    return
                wait(act, cT_ps, t + 1)
                act.activation(cT[:, u, :], bank(0, E, 0, P), ACT.Copy).then_inc(cT_ready, 1)

            def experts(t, u, k):
                for e in range(E):
                    wait(act, eh_ps[e % 2], t * (E // 2) + (e // 2 + 1))
                    wait(act, ey_ps[e % 2], t * (E // 2) + e // 2)
                    for m in range(KC):
                        g = act.activation(hg[:, e % 2, m * P:(m + 1) * P], bank(2 + e % 2, 128, m * P, (m + 1) * P),
                                           ACT.Gelu, bias=eb1_s[:, e, m:m + 1])
                    g.then_inc(hg_ready[e % 2], 1)
                    if e == 4:
                        cT_copy(t + 1, 1 - u)
            cT_copy(0, 0)
            tiles(act, experts, 3, 1, 0)

        @block.tensor
        def _(pe):
            mm = pe.matmul
            pe.wait_ge(consts, 16)
            pe.wait_ge(counted, 1)
            mm(bank(0, P, 0, T), lhsT=upper[:, :], rhs=per_part[:, :], start=True, stop=True)
            mm(bank(1, 128, 0, T), lhsT=ones[0:P, :], rhs=per_part[:, :], start=True, stop=True).then_inc(totals_ps, 1)
            pe.wait_ge(starts, 1)
            pe.transpose(bank(2, T + 1, 0, 128), start[:, :], ident[:, :]).then_inc(starts_ps, 1)
            pe.wait_ge(w_loaded, 16 * 15)
            mm(bank(3, 1, 0, HID), lhsT=u0[:, :], rhs=w1u[:, :], start=True, stop=True).then_inc(brow_ps, 1)
            pe.wait_ge(geg_ready, 1)
            mm(bank(2, 128, 0, NG), lhsT=ones[0:T, :], rhs=geg[:, :], start=True, stop=True).then_inc(groups_ps, 1)
            for b in (4, 5, 6):
                m = mm(bank(b), lhsT=zeros[:, 0:128], rhs=zeros[:, 0:BANK], start=True, stop=False, skip_group_check=True)
            pe.wait_ge(offs_ready, 1)
            pe.wait_ge(bias_ready, 1)

            def xT_of(t, u):
                if not inside(t):
                    return
                wait(pe, xn_ready, t + 1)
                wait(pe, xT_ready, t)
                for k in range(KC):
                    m = pe.transpose(bank(0, 128, k * P, (k + 1) * P), xn[:, u, k * 128:(k + 1) * 128], ident[0:P, 0:P])
                m.then_inc(xT_ps, 1)

            def project(dst, u, c0):
                for k in range(KC):
                    mm(dst, lhsT=xT[:, u, k, :], rhs=wqkv[:, k, c0:c0 + C], start=(k == 0), stop=False)
                return mm(dst, lhsT=ONES_ROW, rhs=bqkv_r[:, c0:c0 + C], start=False, stop=True)

            def sums(t, u):
                if not inside(t):
                    return
                wait(pe, vr_ready, t + 1)
                wait(pe, phi_ready, t + 1)
                for j in range(H * QC):
                    h, c = j // QC, j % QC
                    b, o = seat(j)
                    mm(bank(b, 128, o, o + VE), lhsT=phi[:, u, h, c * 4:(c + 1) * 4, :].rearrange("p o d -> p (o d)"),
                       rhs=vr[:, u, h, :], start=False, stop=False, skip_group_check=True)
                wait(pe, last_ready, t + 1)
                for g in range(H // 2):
                    b, o = seat(H * QC + g)
                    m = mm(bank(b, 2 * LF, o, o + 2 * VE), lhsT=last[:, u, 2 * g:2 * g + 2, :].rearrange("p h f -> p (h f)"),
                           rhs=vn[:, u, 2 * g:2 * g + 2, :].rearrange("p h v -> p (h v)"), start=False, stop=False,
                           skip_group_check=True)
                m.then_inc(m_added, 1)

            def pass1(t, u, k):
                if inside(t):
                    wait(pe, xT_ready, t + 1)
                    wait(pe, kn_ready, t - 1)
                    project(bank((1, 7)[u], P, 0, C), u, C).then_inc(k_ps, 1)
                    wait(pe, vq_free, t)
                    project(bank(2, P, C, 2 * C), u, 2 * C)
                    project(bank(2, P, 0, C), u, 0).then_inc(vq_ps, 1)
                    wait(pe, hpre_ready, t)
                    for m in range(MC):
                        for kk in range(KC):
                            z = mm(bank(3, 128, m * P, (m + 1) * P), lhsT=w1x[:, kk, m * 128:(m + 1) * 128],
                                   rhs=xT[:, u, kk, :], start=(kk == 0), stop=(kk == KC - 1))
                    z.then_inc(h_ps, 1)
                    xT_of(t + 1, 1 - u)
                sums(t - 1, 1 - u)
            xT_of(0, 0)
            tiles(pe, pass1, 3, 1, 1)

            pe.wait_ge(m_ready, 1)

            def features(t, u, j):
                if j == 0:
                    wait(pe, qphi_ready[0], t + 1)
                if j == H // 2:
                    wait(pe, qphi_ready[1], t + 1)
                if j == H:
                    wait(pe, qlast_ready, t + 1)
                wait(pe, phT_ready[j % 3], t * 3 + j // 3)
                for c in range(QC):
                    if j < H:
                        m = pe.transpose(bank(1 + j % 3, 128, c * P, (c + 1) * P),
                                         phi[:, u, j, c * 4:(c + 1) * 4, :].rearrange("p o d -> p (o d)"), ident[0:P, 0:P])
                    else:
                        m = pe.transpose(bank(1 + j % 3, 2 * LF, c * P, (c + 1) * P),
                                         last[:, u, 2 * c:2 * c + 2, :].rearrange("p h f -> p (h f)"), ident[0:P, 0:P])
                m.then_inc(phT_ps[j % 3], 1)

            def outputs(t, u, j):
                wait(pe, phT_ready[j % 3], t * 3 + (j // 3 + 1))
                if j == 0:
                    wait(pe, y_taken, t)
                for c in range(QC):
                    if j < H:
                        m = mm(bank(4, P, j * VE, (j + 1) * VE), lhsT=phT[:, j % 3, c * P:(c + 1) * P], rhs=mq[:, j, c, :],
                               start=(c == 0), stop=(c == QC - 1))
                    else:
                        m = mm(bank(5, P, c * 2 * VE, (c + 1) * 2 * VE), lhsT=phT[0:2 * LF, j % 3, c * P:(c + 1) * P],
                               rhs=ml[:, c, :], start=True, stop=True)
                m.then_inc(y_ps[j % 3], 1)

            def attn_T(t, u):
                if not inside(t):
                    return
                wait(pe, attn_ready, t + 1)
                wait(pe, x1_ready, t)
                for k in range(KC):
                    m = pe.transpose(bank(7, 128, k * P, (k + 1) * P), attn[:, u, k * 128:(k + 1) * 128], ident[0:P, 0:P])
                m.then_inc(attnT_ps, 1)

            def proj(t, u):
                if not inside(t):
                    return
                wait(pe, attnT_ready, t + 1)
                dst = bank(7, P, 256, 256 + C)
                for k in range(KC):
                    mm(dst, lhsT=attnT[:, u, k, :], rhs=wproj[:, k, :], start=(k == 0), stop=False)
                mm(dst, lhsT=ONES_ROW, rhs=brows[:, 1, 0:C], start=False, stop=True).then_inc(proj_ps, 1)

            def pass2(t, u, k):
                if inside(t):
                    for j in range(NJ):
                        features(t, u, j)
                        if j >= 2:
                            outputs(t, u, j - 2)
                        if j == 5:
                            attn_T(t - 1, 1 - u)
                    proj(t - 1, 1 - u)
                    for j in (NJ - 2, NJ - 1):
                        outputs(t, u, j)
                else:
                    attn_T(t - 1, 1 - u)
                    proj(t - 1, 1 - u)
            tiles(pe, pass2, 3, 2, 1)

            pe.wait_ge(x1_ready, T)
            for b in range(4):
                m = mm(bank(b, P), lhsT=zeros[:, 0:P], rhs=zeros[:, 0:BANK], start=True, stop=False, skip_group_check=True)

            def add_rows(c, h, nth):
                offs = [pe.value_load(off_i[0:1, bass.ds(c * RG + g, 1)]) for g in range(RG)]
                wait(pe, rows_loaded[h], nth * 16)
                hold(pe, onehot_ready, c + 1)
                for g in range(RG):
                    for k in range(GT):
                        m = mm(ps[0:P, bass.ds(offs[g], F)], lhsT=oh[:, h, g * GT + k, :], rhs=srt[:, h, g * GT + k, :],
                               start=False, stop=False, skip_group_check=True)
                m.then_inc(rows_used, 1)
            add_rows(0, 0, 1)
            with pe.Fori(0, NR // 2) as i:
                add_rows(i * 2 + 1, 1, i + 1)
                add_rows(i * 2 + 2, 0, i + 2)

            pe.wait_ge(agg_ready, 1)

            def ag_T(t, u):
                if not inside(t):
                    return
                wait(pe, agr_ready, t + 1)
                wait(pe, agT_ready, t)
                pe.transpose(bank(0, EA + 1, 0, P), agr[:, u, :], ident[0:P, 0:P]).then_inc(agT_ps, 1)

            def ha(t, u):
                if not inside(t):
                    return
                wait(pe, agT_ready, t + 1)
                wait(pe, hsum_ready, t - 1)
                for m in range(MC):
                    z = mm(bank(1 + u, 128, m * P, (m + 1) * P), lhsT=w1a[:, m * 128:(m + 1) * 128], rhs=agT[:, u, :],
                           start=True, stop=True)
                z.then_inc(ha_ps, 1)

            def layer2(t, u):
                if not inside(t):
                    return
                wait(pe, hs_ready, t + 1)
                wait(pe, x2_ready, t - 1)
                for m in range(MC):
                    z = mm(bank(3 + u, P, 0, C), lhsT=hs[:, u, m * P:(m + 1) * P], rhs=w2s[:, m, :], start=(m == 0),
                           stop=(m == MC - 1))
                z.then_inc(gnn_ps, 1)

            def tok_T(t, u):
                if not inside(t):
                    return
                wait(pe, xl_ready, t + 1)
                wait(pe, tokr_ready, t)
                for k in range(KC):
                    m = pe.transpose(bank(5, 128, k * P, (k + 1) * P), xl[:, u, k * 128:(k + 1) * 128], ident[0:P, 0:P])
                m.then_inc(tok_ps, 1)

            def router(t, u):
                if not inside(t):
                    return
                wait(pe, tokr_ready, t + 1)
                wait(pe, lg_ready, t)
                for k in range(KC):
                    m = mm(bank(6, P, 0, E), lhsT=tokr[:, u, k * P:(k + 1) * P], rhs=wr[:, k, :], start=(k == 0), stop=(k == KC - 1))
                m.then_inc(lg_ps, 1)

            def gnn(t, u, k):
                ag_T(t + 1, 1 - u)
                ha(t, u)
                layer2(t - 1, 1 - u)
                tok_T(t - 3, 1 - u)
                router(t - 4, u)
            ag_T(0, 0)
            tiles(pe, gnn, 6, 3, 4)

            pe.wait_ge(comb_ready, 1)
            pe.wait_ge(ew_loaded, 32)
            pe.wait_ge(tokT_ready, T)

            def c_T(t, u):
                if not inside(t):
                    return
                wait(pe, cr_ready, t + 1)
                wait(pe, cT_ready, t)
                pe.transpose(bank(0, E, 0, P), cr[:, u, :], ident[0:P, 0:P]).then_inc(cT_ps, 1)

            def expert_y(t, e):
                wait(pe, hg_ready[e % 2], t * (E // 2) + (e // 2 + 1))
                wait(pe, o_ready, t * (E + 1) + e if e >= 2 else (t - 1) * (E + 1) + (E + e))
                for k in range(KC):
                    m = mm(bank(4 + e % 2, P, 0, C), lhsT=hg[:, e % 2, k * P:(k + 1) * P], rhs=ew2_s[:, e, k, :],
                           start=(k == 0), stop=(k == KC - 1))
                m.then_inc(ey_ps[e % 2], 1)

            def experts(t, u, k):
                for e in range(E):
                    wait(pe, hg_ready[e % 2], t * (E // 2) + e // 2)
                    for m in range(KC):
                        for kk in range(KC):
                            z = mm(bank(2 + e % 2, 128, m * P, (m + 1) * P), lhsT=ew1_s[:, e, kk, m * 128:(m + 1) * 128],
                                   rhs=tokT[:, kk, bass.ds(t * P, P)], start=(kk == 0), stop=(kk == KC - 1))
                    z.then_inc(eh_ps[e % 2], 1)
                    if e == 0:
                        wait(pe, cT_ready, t + 1)
                        wait(pe, o_ready, (t - 1) * (E + 1) + 1)
                        mm(bank(1, P, 0, C), lhsT=cT[:, u, :], rhs=eb2_s[:, :], start=True, stop=True).then_inc(cb_ps, 1)
                    else:
                        expert_y(t, e - 1)
                    if e == 3:
                        c_T(t + 1, 1 - u)
                expert_y(t, E - 1)
            c_T(0, 0)
            tiles(pe, experts, 3, 1, 0)

        @block.vector
        def _(v):
            n = [0]

            def link(ins):
                n[0] += 1
                ins.then_inc(dve_step, 1)
                v.wait_ge(dve_step, n[0])

            v.wait_ge(src_loaded, 16)
            v.wait_ge(consts, 8)
            link(v.tensor_copy(src_f[:, :], src_i[:, :]))
            link(v.memset(clast[:, 0:1], 0.0))
            link(v.memset(start[:, 0:1], 0.0))
            link(v.memset(ones_b[:, :], 1.0))
            link(v.tensor_tensor(ge, src_f[:, :].unsqueeze(1).to_broadcast([P, T + 1, ET]),
                                 thr[:, :].unsqueeze(2).to_broadcast([P, T + 1, ET]), ALU.is_ge))
            link(v.tensor_tensor(oneh, ge[:, 0:T, :], ge[:, 1:T + 1, :], ALU.subtract))
            link(v.tensor_tensor_scan(cum.rearrange("p b j -> p (b j)"), ones_b[:, 0:1].to_broadcast([P, T * ET]),
                                      oneh.rearrange("p b j -> p (b j)"), 0.0, ALU.mult, ALU.add))
            link(v.tensor_copy(clast[:, 1:T + 1], cum[:, :, ET - 1]))
            v.tensor_tensor(per_part[:, :], clast[:, 1:T + 1], clast[:, 0:T], ALU.subtract).then_inc(counted, 1)
            v.wait_ge(totals_ps, 1)
            link(v.tensor_scalar(tot_i[:, :], bank(1, 128, 0, T), float(S * GT - 1), None, ALU.add))
            link(v.tensor_scalar(tot_i[:, :], tot_i[:, :], -S * GT, None, ALU.bitwise_and))
            link(v.tensor_copy(padded[:, :], tot_i[:, :]))
            v.tensor_tensor_scan(start[:, 1:T + 1], ones[:, 0:T], padded[:, :], 0.0, ALU.mult, ALU.add).then_inc(starts, 1)
            v.wait_ge(starts, 1)
            link(v.tensor_tensor(base[:, :], bank(0, P, 0, T), clast[:, 0:T], ALU.subtract))
            link(v.scalar_tensor_tensor(base[:, :], base[:, :], -1.0, start[0:P, 0:T], ALU.add, ALU.add))
            for b in range(T):
                v.scalar_tensor_tensor(cum[:, b, :], cum[:, b, :], base[:, b:b + 1], oneh[:, b, :], ALU.add,
                                       ALU.mult).then_inc(dve_step, 1)
                n[0] += 1
            v.wait_ge(dve_step, n[0])
            link(v.tensor_reduce(pos, cum.rearrange("p b j -> p j b"), AX.X, ALU.add))
            link(v.tensor_copy(pos_i, pos))
            link(v.tensor_scalar(slot_t, pos_i, 7, None, ALU.arith_shift_right))
            link(v.tensor_scalar(slot_p, pos_i, S - 1, None, ALU.bitwise_and))
            v.scalar_tensor_tensor(addr[:, :], slot_p, float(ST), slot_t, ALU.mult, ALU.add).then_inc(addr_ready, 1)
            v.wait_ge(starts_ps, 1)
            link(v.tensor_copy(startT[:, :], bank(2, T, 0, 1)))
            v.tensor_scalar(geg[:, :], iota_g[:, :], startT[:, 0:1], None, ALU.is_ge).then_inc(geg_ready, 1)
            v.wait_ge(brow_ps, 1)
            link(v.tensor_tensor(w1a[0:1, :], bank(3, 1, 0, HID), brows[:, 0, :], ALU.add))
            link(v.tensor_scalar(temp[:, :], temp[:, :], SC2, None, ALU.mult))
            v.tensor_tensor(brows[:, 1, 0:C], brows[:, 1, 0:C], brows[:, 2, 0:C], ALU.add).then_inc(bias_ready, 1)
            v.wait_ge(groups_ps, 1)
            link(v.tensor_scalar(bt[:, :], bank(2, 128, 0, NG), -1.0, None, ALU.add))
            link(v.tensor_scalar(off_f[:, :], bt[0:1, :], float(F), None, ALU.mult))
            for m in range(1, (T - 1) // BPB + 1):
                link(v.tensor_scalar(off_g[:, :], bt[0:1, :], float(BPB * m), float(GAP), ALU.is_ge, ALU.mult))
                link(v.tensor_tensor(off_f[:, :], off_f[:, :], off_g[:, :], ALU.add))
            link(v.tensor_copy(off_i[:, :], off_f[:, :]))
            v.tensor_scalar(bt[:, :], bt[:, :], float(P), None, ALU.mult).then_inc(offs_ready, 1)
            v.wait_ge(offs_ready, 1)

            v.wait_ge(x_loaded, 16)
            for t in range(T):
                v.bn_stats(stats[:, t, :], x_res[:, t, :]).then_inc(dve_step, 1)
                n[0] += 1
            v.wait_ge(dve_step, n[0])
            for t in range(T):
                v.bn_aggr(mv[:, t, :], stats[:, t, :]).then_inc(dve_step, 1)
                n[0] += 1
            v.wait_ge(dve_step, n[0])
            v.tensor_scalar(rstd[:, :], mv[:, :, 1], LN_EPS, None, ALU.add).then_inc(var_ready, 1)
            link(v.memset(vn[:, :, :, D:VE], 1.0 / N))
            link(v.memset(last[:, :, :, LF - 1:LF], 1.0))
            v.wait_ge(std_ready, 1)
            link(v.reciprocal(rstd[:, :], rstd[:, :]))

            def xn_of(t, u):
                if not inside(t):
                    return
                wait(v, xT_ps, t - 1)
                v.tensor_scalar(xn[:, u, :], x_res[:, bass.ds(t, 1), :].rearrange("p a c -> p (a c)"),
                                mv[:, bass.ds(t, 1), 0:1].rearrange("p a b -> p (a b)"), rstd[:, bass.ds(t, 1)],
                                ALU.subtract, ALU.mult).then_inc(xn_ready, 1)

            def heads(ap, w):
                return ap.rearrange("p (h d) -> p h d", h=H) if w is None else ap.unsqueeze(2).to_broadcast([P, H, w])

            def keys(t, u):
                if not inside(t):
                    return
                kb = heads(bank((1, 7)[u], P, 0, C), None)
                wait(v, kdup_ready, t + 1)
                wait(v, m_added, t - 1)
                v.tensor_tensor(phi[:, u], kb.unsqueeze(2).to_broadcast([P, H, OFF, D]), overlapped(kdup, u),
                                ALU.mult).then_inc(phi_ready, 1)
                wait(v, phi_ready, t + 1)
                v.tensor_reduce(ssq[:, u, :], phi[:, u, :, 0, :], AX.X, ALU.add).then_inc(ssq_ready, 1)
                wait(v, ssq_ready, t + 1)
                v.tensor_scalar(nm[:, u, :], ssq[:, u, :], EPS2, 1.0 / SC2, ALU.max, ALU.mult).then_inc(nm_ready, 1)
                wait(v, nm_ready, t + 1)
                v.reciprocal(r2[:, u, :], nm[:, u, :]).then_inc(rk2_ready, 1)
                wait(v, rk2_ready, t + 1)
                wait(v, vn_ready, t + 1)
                v.tensor_tensor(vr[:, u], vn[:, u], heads(r2[:, u, :], VE), ALU.mult).then_inc(vr_ready, 1)
                wait(v, rk_ready, t + 1)
                v.tensor_tensor(last[:, u, :, 16:16 + D], kb, heads(rr[:, u, :], D), ALU.mult).then_inc(kn_ready, 1)
                wait(v, kn_ready, t + 1)
                v.tensor_tensor(last[:, u, :, 0:16], last[:, u, :, 16:32], last[:, u, :, 32:48], ALU.mult).then_inc(last_ready, 1)

            def pass1(t, u, k):
                xn_of(t + 1, 1 - u)
                keys(t - 1, 1 - u)
            xn_of(0, 0)
            tiles(v, pass1, 3, 1, 1)

            v.wait_ge(m_added, T)
            mqf = mq.rearrange("p h c e -> p (h c e)")
            link(v.tensor_copy(mqf[:, 0:15 * VE], bank(4, 128, 0, 15 * VE)))
            link(v.tensor_copy(mqf[:, 15 * VE:30 * VE], bank(5, 128, 0, 15 * VE)))
            link(v.tensor_copy(mqf[:, 30 * VE:32 * VE], bank(6, 128, 0, 2 * VE)))
            link(v.tensor_scalar(mq[:, :, 0, :], mq[:, :, 0, :], sq_half[:, 0:1], None, ALU.mult))
            v.tensor_tensor(ml, bank(6, 2 * LF, 2 * VE, (2 + H) * VE).rearrange("p (g e) -> p g e", g=H // 2),
                            mask[:, :].unsqueeze(1).to_broadcast([2 * LF, H // 2, 2 * VE]), ALU.mult).then_inc(m_ready, 1)

            def queries(t, u):
                if not inside(t):
                    return
                qb = heads(bank((0, 6)[u], P, 0, C), None)
                wait(v, q_ps, t + 1)
                wait(v, qdup_ready, t + 1)
                wait(v, phT_ps[H % 3], (t - 1) * 3)
                o = overlapped(kdup, u)
                for g in range(2):
                    hh = slice(g * H // 2, (g + 1) * H // 2)
                    og = bass.AP(o.tensor, o.offset + g * (H // 2) * 2 * D, [o.ap[0], [2 * D, H // 2], [1, OFF], [1, D]])
                    v.tensor_tensor(phi[:, u, hh], qb[:, hh].unsqueeze(2).to_broadcast([P, H // 2, OFF, D]), og,
                                    ALU.mult).then_inc(qphi_ready[g], 1)
                wait(v, qphi_ready[0], t + 1)
                wait(v, qphi_ready[1], t + 1)
                v.tensor_reduce(ssq[:, u, :], phi[:, u, :, 0, :], AX.X, ALU.add).then_inc(qssq_ready, 1)
                wait(v, qssq_ready, t + 1)
                v.tensor_scalar(nm[:, u, :], ssq[:, u, :], SC2, EPS2, ALU.mult, ALU.max).then_inc(qnm_ready, 1)
                wait(v, qnm_ready, t + 1)
                v.reciprocal(r2[:, u, :], nm[:, u, :]).then_inc(qinv_ready, 1)
                wait(v, qsq_ready, t + 1)
                v.tensor_tensor(rq[:, u, :], rr[:, u, :], temp[:, :], ALU.mult).then_inc(rq_ready, 1)
                wait(v, rq_ready, t + 1)
                v.tensor_tensor(rq2[:, u, :], rq[:, u, :], rq[:, u, :], ALU.mult).then_inc(rq2_ready, 1)
                v.tensor_tensor(last[:, u, :, 16:16 + D], qb, heads(rq[:, u, :], D), ALU.mult).then_inc(qn_ready, 1)
                wait(v, qn_ready, t + 1)
                v.tensor_tensor(last[:, u, :, 0:16], last[:, u, :, 16:32], last[:, u, :, 32:48], ALU.mult).then_inc(qlast_ready, 1)

            def x1(t, u):
                if not inside(t):
                    return
                wait(v, proj_ps, t + 1)
                xr = x_res[:, bass.ds(t, 1), :].rearrange("p a c -> p (a c)")
                v.tensor_tensor(xr, bank(7, P, 256, 256 + C), xr, ALU.add).then_inc(x1_ready, 1)

            def normalise(t, u):
                if not inside(t):
                    return
                wait(v, y_ps[H % 3], t * 3 + 3)
                wait(v, rq2_ready, t + 1)
                yv = y1[:, u, :].rearrange("p (h e) -> p h e", h=H)
                v.tensor_tensor(yv, bank(4, P, 0, H * VE).rearrange("p (h e) -> p h e", h=H), heads(rq2[:, u, :], VE),
                                ALU.mult).then_inc(y_scaled, 1)
                wait(v, y_scaled, t + 1)
                v.tensor_tensor(y1[:, u, :], bank(5, P, 0, H * VE), y1[:, u, :], ALU.add).then_inc(y_taken, 1)
                wait(v, y_taken, t + 1)
                v.reciprocal(ry[:, u, :], yv[:, :, D:VE].rearrange("p h e -> p (h e)")).then_inc(ry_ready, 1)
                wait(v, ry_ready, t + 1)
                wait(v, attnT_ps, t - 1)
                v.tensor_tensor(heads(attn[:, u, :], None), yv[:, :, 0:D], heads(ry[:, u, :], D), ALU.mult).then_inc(attn_ready, 1)

            def pass2(t, u, k):
                queries(t + 1, 1 - u)
                x1(t - 1, 1 - u)
                normalise(t, u)
            queries(0, 0)
            tiles(v, pass2, 3, 2, 1)

            def onehots(c, h, nth):
                wait(v, rows_loaded[h], nth * 16)
                wait(v, rows_used, c - 1)
                v.tensor_tensor(key[:, h, :].rearrange("p (g k) -> p g k", g=RG),
                                srt[:, h, :, EA].rearrange("p (g k) -> p g k", g=RG),
                                bt[:, bass.ds(c * RG, RG)].unsqueeze(2).to_broadcast([128, RG, GT]),
                                ALU.subtract).then_inc(key_ready, 1)
                hold(v, key_ready, c + 1)
                for k in range(RT):
                    z = v.tensor_scalar(oh[:, h, k, :], iota_c[:, :], key[:, h, k:k + 1], None, ALU.is_equal)
                z.then_inc(onehot_ready, 1)
            onehots(0, 0, 1)
            onehots(1, 1, 1)
            onehots(2, 0, 2)
            with v.Fori(0, NR // 2 - 1) as i:
                onehots(i * 2 + 3, 1, i + 2)
                onehots(i * 2 + 4, 0, i + 3)
            v.wait_ge(rows_used, NR)
            link(v.memset(agg[:, :, 0:1], 1.0))
            for b in range(4):
                nb = min(BPB, T - b * BPB)
                v.tensor_copy(cnt[:, b * BPB:b * BPB + nb],
                              bank(b, P, 0, nb * F).rearrange("p (b f) -> p b f", f=F)[:, :, EA + 1]).then_inc(dve_step, 1)
                n[0] += 1
            v.wait_ge(dve_step, n[0])
            link(v.tensor_scalar(cnt, cnt, 1.0, None, ALU.max))
            link(v.reciprocal(cnt, cnt))
            for b in range(4):
                nb = min(BPB, T - b * BPB)
                z = v.tensor_tensor(agg[:, b * BPB:b * BPB + nb, 1:EA + 1],
                                    bank(b, P, 0, nb * F).rearrange("p (b f) -> p b f", f=F)[:, :, 0:EA],
                                    cnt[:, b * BPB:b * BPB + nb].unsqueeze(2).to_broadcast([P, nb, EA]), ALU.mult)
                link(z)
            v.sem_inc(agg_ready)

            def agr_of(t, u):
                if not inside(t):
                    return
                hold(v, agT_ps, t - 1)
                v.tensor_copy(agr[:, u, :], agg[:, bass.ds(t, 1), :].rearrange("p a c -> p (a c)")).then_inc(agr_ready, 1)

            def hsum(t, u, k):
                if not inside(t):
                    return
                wait(v, ha_ps, t + 1)
                wait(v, hpre_back[u], k * 16 + 16)
                wait(v, gnn_ps, t - 1)
                v.tensor_tensor(hs[:, u, :], bank(1 + u, 128, 0, MC * P), hpre[:, u, :], ALU.add).then_inc(hsum_ready, 1)

            def x2_of(t, u):
                if not inside(t):
                    return
                wait(v, gnn_ps, t + 1)
                wait(v, res_ready, t - 1)
                v.tensor_tensor(x2[:, u, :], bank(3 + u, P, 0, C), x_res[:, bass.ds(t, 1), :].rearrange("p a c -> p (a c)"),
                                ALU.add).then_inc(x2_ready, 1)
                wait(v, x2_ready, t + 1)
                v.bn_stats(st2[:, u, :], x2[:, u, :]).then_inc(st2_ready, 1)
                hold(v, st2_ready, t + 1)
                v.bn_aggr(mv2[:, u, :], st2[:, u, :]).then_inc(mv2_ready, 1)
                wait(v, mv2_ready, t + 1)
                v.tensor_scalar(sd2[:, u, :], mv2[:, u, 1:2], LN_EPS, None, ALU.add).then_inc(ve2_ready, 1)

            def xl_of(t, u):
                if not inside(t):
                    return
                wait(v, sd2_ready, t + 1)
                v.reciprocal(rs2[:, u, :], sd2[:, u, :]).then_inc(rs2_ready, 1)
                wait(v, rs2_ready, t + 1)
                wait(v, tok_ps, t - 1)
                v.tensor_scalar(xl[:, u, :], x2[:, u, :], mv2[:, u, 0:1], rs2[:, u, :], ALU.subtract, ALU.mult).then_inc(xl_ready, 1)

            def lg_of(t, u):
                if not inside(t):
                    return
                hold(v, lg_ps, t + 1)
                v.tensor_copy(lg[:, bass.ds(t, 1), :].rearrange("p a c -> p (a c)"), bank(6, P, 0, E)).then_inc(lg_ready, 1)

            def gnn(t, u, k):
                agr_of(t + 2, u)
                hsum(t, u, k)
                x2_of(t - 1, 1 - u)
                xl_of(t - 2, u)
                lg_of(t - 4, u)
            agr_of(0, 0)
            agr_of(1, 1)
            tiles(v, gnn, 6, 3, 4)

            def wide(a):
                return a.unsqueeze(2).to_broadcast([P, T, E])

            v.wait_ge(lg_ready, T)
            link(v.tensor_reduce(red, lg, AX.X, ALU.max))
            v.tensor_tensor(pr, lg, wide(red), ALU.subtract).then_inc(sh_ready, 1)
            v.wait_ge(ex_ready, 1)
            link(v.tensor_reduce(red, pr, AX.X, ALU.add))
            link(v.reciprocal(red, red))
            link(v.tensor_tensor(pr, pr, wide(red), ALU.mult))
            link(v.tensor_copy(pw, pr))
            link(v.memset(comb, 0.0))
            for m in range(2):
                best = (top1, top2)[m]
                link(v.tensor_reduce(best, pw, AX.X, ALU.max))
                link(v.tensor_tensor(eq, pw, wide(best), ALU.is_equal))
                link(v.scalar_tensor_tensor(pick, rank8[:, :].unsqueeze(1).to_broadcast([P, T, E]), float(E), eq, ALU.add, ALU.mult))
                link(v.tensor_reduce(red, pick, AX.X, ALU.max))
                link(v.tensor_tensor(eq, pick, wide(red), ALU.is_equal))
                link(v.tensor_tensor(comb, comb, eq, ALU.add))
                if m == 0:
                    link(v.scalar_tensor_tensor(pw, eq, -2.0, pw, ALU.mult, ALU.add))
            link(v.tensor_tensor(red, top1, top2, ALU.add))
            link(v.tensor_scalar(red, red, 1e-12, None, ALU.max))
            link(v.reciprocal(red, red))
            link(v.tensor_tensor(pr, pr, wide(red), ALU.mult))
            v.tensor_tensor(comb, comb, pr, ALU.mult).then_inc(comb_ready, 1)
            v.wait_ge(comb_ready, 1)

            def cr_of(t, u):
                if not inside(t):
                    return
                hold(v, cT_ps, t - 1)
                hold(v, o_ready, (t - 1) * (E + 1))
                v.tensor_copy(cr[:, u, :], comb[:, bass.ds(t, 1), :].rearrange("p a c -> p (a c)")).then_inc(cr_ready, 1)

            v.wait_ge(res_ready, T)

            def experts(t, u, k):
                wait(v, cb_ps, t + 1)
                wait(v, stored[u], k * 16)
                v.tensor_tensor(o_s[:, u, :], bank(1, P, 0, C), x_res[:, bass.ds(t, 1), :].rearrange("p a c -> p (a c)"),
                                ALU.add).then_inc(o_ready, 1)
                for e in range(E):
                    wait(v, ey_ps[e % 2], t * (E // 2) + (e // 2 + 1))
                    wait(v, o_ready, t * (E + 1) + (e + 1))
                    v.scalar_tensor_tensor(o_s[:, u, :], bank(4 + e % 2, P, 0, C), cr[:, u, e:e + 1], o_s[:, u, :], ALU.mult,
                                           ALU.add).then_inc(o_ready, 1)
                    if e == 0:
                        cr_of(t + 1, 1 - u)
            cr_of(0, 0)
            tiles(v, experts, 3, 1, 0)


def kernel(**inputs):
    import numpy as _np
    import concourse.bacc as _bacc
    from concourse import mybir as _mybir
    from concourse.bass_utils import run_bass_kernel_spmd as _run

    f = {k: _np.asarray(a) for k, a in inputs.items()}
    laid = [
        ("x", f["x"]), ("src", f["src"]), ("edge_attr", f["edge_attr_64"]), ("u", f["L0_gnn_u"]),
        ("W1", f["L0_gnn_W1"]), ("b1", f["L0_gnn_b1"]), ("W2", f["L0_gnn_W2"]), ("b2", f["L0_gnn_b2"]),
        ("WqkvT", f["L0_mix_Wqkv"].T), ("bqkv", f["L0_mix_bqkv"]), ("WprojT", f["L0_mix_Wproj"].T),
        ("bproj", f["L0_mix_bproj"]), ("temperature", f["L0_mix_temperature"].reshape(-1)),
        ("routerT", f["L0_ffn_router_w"].T), ("ew1", f["L0_ffn_w1"]), ("eb1", f["L0_ffn_b1"]),
        ("ew2", f["L0_ffn_w2"]), ("eb2", f["L0_ffn_b2"]),
    ]
    nc = _bacc.Bacc("TRN2", target_bir_lowering=False, num_devices=1)
    arrays, args = {}, []
    for name, a in laid:
        a = _np.ascontiguousarray(a)
        arrays[f"in_{name}"] = a
        args.append(nc.dram_tensor(f"in_{name}", a.shape, _mybir.dt.from_np(a.dtype), kind="ExternalInput").ap())
    args.append(nc.dram_tensor("out_x", f["x"].shape, _mybir.dt.float32, kind="ExternalOutput").ap())
    gps_layer(nc, *args)
    r = _run(nc, [arrays], core_ids=[0])
    return r.results[0]["out_x"]
```

```python
import concourse.bass as bass
from concourse import mybir
from contextlib import ExitStack

fp32 = mybir.dt.float32
bf16 = mybir.dt.bfloat16
i32 = mybir.dt.int32
u32 = mybir.dt.uint32
ALU = mybir.AluOpType
ACT = mybir.ActivationFunctionType
AX = mybir.AxisListType


def gps_layer(nc, x, src, edge_attr, u_in, W1, b1, W2, b2, WqkvT, bqkv, WprojT, bproj, temperature,
              routerT, ew1, eb1, ew2, eb2, out):
    N, C = x.shape
    P = 125
    T = N // P
    EA = edge_attr.shape[1]
    ET = src.shape[0] // P
    HID = W1.shape[1]
    MC = HID // 128
    KC = C // 128
    H = temperature.shape[0]
    D = C // H
    E = ew1.shape[0]
    OFF = 16
    QC = OFF * D // 128
    LF = 16 + D + 1
    VE = D + 1
    VW = 64
    S = 128
    GT = 4
    NG = (N * 0 + src.shape[0] + T * (GT * S - 1)) // (GT * S) + 1
    NG += -NG % 3
    ST = NG * GT
    RT = 12
    RG = RT // GT
    NR = ST // RT
    RB = 4
    SB = 6
    REG = N + 128
    NS = 2 * N // 128 + E
    XF = C + 2
    F = EA + 2
    BPB = 4
    NBK = (T - 1) // BPB + 1
    CH = 17
    NCH = ET // CH
    BANK = 512
    LN_EPS = 1e-5
    EPS2 = 1e-24
    SC = float(D) ** 0.25
    SC2, SC4 = SC * SC, SC ** 4
    GAP = BANK - BPB * P
    assert NR % RB == 3 and NCH % 2 == 1 and T == 25

    ctx = ExitStack()
    with ctx:
        def sb(name, shape, dt=fp32):
            return ctx.enter_context(nc.sbuf_tensor(name, shape, dt))

        def sem(name):
            return ctx.enter_context(nc.semaphore(name))

        sorted_rows = nc.dram_tensor("sorted_rows", (S * ST, F), fp32, kind="Internal").ap()
        hpre_dram = nc.dram_tensor("hpre_rows", (T * 128, MC * P), fp32, kind="Internal").ap()
        routed = nc.dram_tensor("routed_rows", (E * REG + 128, XF), fp32, kind="Internal").ap()
        youts = nc.dram_tensor("expert_outputs", (2 * N, C), fp32, kind="Internal").ap()
        sorted_v = sorted_rows.rearrange("(p t) f -> p t f", p=S)

        x_res = sb("x_res", [P, T, C])
        stage = sb("stage", [P, 2, CH, F])
        idx = sb("idx", [P, 2, CH], u32)
        src_f = sb("src_f", [P, ET])
        addr = sb("addr", [P, ET], u32)
        zeros = sb("zeros", [128, RT * F])
        ones = sb("ones", [128, 128])
        ones_b = sb("ones_b", [P, 1], bf16)
        ident = sb("ident", [128, 128])
        upper = sb("upper", [P, P])
        iota_c = sb("iota_c", [128, P])
        wqkv = sb("wqkv", [128, KC, 3 * C])
        w1x = sb("w1x", [128, KC, HID])
        w1u = sb("w1u", [128, HID])
        w1a = sb("w1a", [EA + 1, HID])
        w2s = sb("w2s", [128, MC, C])
        wproj = sb("wproj", [128, KC, C])
        wr = sb("wr", [128, KC, E])
        NBR = 4 + 2 * E
        bias_rows = sb("bias_rows", [NBR, C])
        bias_more = sb("bias_more", [NBR, C])
        u0 = sb("u0", [128, 1])
        temp = sb("temp", [P, H])
        stats = sb("stats", [P, T, 6])
        mv = sb("mv", [P, T, 2])
        rstd = sb("rstd", [P, T])
        mask = sb("mask", [2 * LF, 2 * VE])
        sq_half = sb("sq_half", [128, 1])
        bt = sb("bt", [128, NG])
        bias3 = sb("bias3", [3, NBR, C], bf16)
        ones3 = sb("ones3", [3, P], bf16)
        bparts = sb("bparts", [NBR, 3, C], bf16)
        brest = sb("brest", [NBR, C])
        ones3w = sb("ones3w", [3, 128], bf16)
        dst_row = sb("dst_row", [P, T])
        reg_start = sb("reg_start", [P, E])
        reg_fill = sb("reg_fill", [128, E])
        step_row = sb("step_row", [1, NS])
        pad_rows = sb("pad_rows", [128, XF])
        pad_idx = sb("pad_idx", [128, E], u32)
        row_idx = sb("row_idx", [P, 2, T], u32)
        exp_i = sb("exp_i", [1, NS], i32)
        row_i = sb("row_i", [1, NS], i32)
        off_i = sb("off_i", [1, NG], i32)

        r1 = sb("r1", [128, 17700])
        r1_off = [0]

        def carve(shape, dt=fp32, parts=None, at=None):
            n = 1
            for s in shape[1:]:
                n *= s
            words = (n + 1) // 2 if dt == bf16 else n
            o = r1_off[0] if at is None else at
            if at is None:
                r1_off[0] += words
            assert o + words <= 17700, o + words
            v = r1[0:shape[0], o:o + words]
            if dt != fp32:
                v = v.bitcast(dt)
                if dt == bf16:
                    v = v[:, 0:n]
            if len(shape) == 3:
                v = v.rearrange("p (a b) -> p a b", a=shape[1])
            elif len(shape) == 4:
                v = v.rearrange("p (a b c) -> p a b c", a=shape[1], b=shape[2])
            elif len(shape) == 5:
                v = v.rearrange("p (a b c d) -> p a b c d", a=shape[1], b=shape[2], c=shape[3])
            return v

        cum = carve([P, T, ET])
        ge = carve([P, T + 1, ET], bf16, at=0)
        oneh = carve([P, T, ET], bf16)
        pos = carve([P, ET])
        pos_i = carve([P, ET], i32)
        slot_t = carve([P, ET], i32)
        slot_p = carve([P, ET], i32)
        src_i = sb("src_i", [P, ET], i32)
        thr = sb("thr", [P, T + 1])
        iota_g = sb("iota_g", [T, NG])
        clast = sb("clast", [P, T + 1])
        per_part = sb("per_part", [P, T])
        tot_i = sb("tot_i", [128, T], i32)
        padded = sb("padded", [128, T])
        start = sb("start", [128, T + 1])
        base = sb("base", [P, T])
        startT = sb("startT", [T, 1])
        geg = sb("geg", [T, NG])
        off_f = sb("off_f", [1, NG])
        off_g = sb("off_g", [1, NG])
        r1_off[0] = 0
        xT_all = carve([128, KC, T * P])
        hpre = carve([128, 2, MC * P])
        after_q = r1_off[0]
        xn = carve([P, 2, C])
        vn = carve([P, 2, H, VW])
        vr = carve([P, 2, H, VW])
        first_only = r1_off[0]
        r1_off[0] = after_q
        phT = carve([128, 2, QC * P])
        yT = carve([128, (H // 2) * P])
        sqs = carve([P, 2, C])
        attn = carve([P, 2, C])
        r1_off[0] = max(first_only, r1_off[0])
        xT = carve([128, 2, KC, P])
        kdup = carve([P, 2, H, 2 * D])
        last = carve([P, 2, H, LF])
        mq = carve([128, H // 2, QC, 2 * VW])
        ml = carve([2 * LF, H // 2, 2 * VW])
        attnT = carve([128, 2, KC, P])
        ssq = carve([P, 2, H])
        nm = carve([P, 2, H])
        r2 = carve([P, 2, H])
        rr = carve([P, 2, H])
        rq = carve([P, 2, H])
        ry = carve([P, 2, H])
        r1_off[0] = 0
        xl_all = carve([P, T, XF])
        hpre2 = carve([128, 2, MC * P])
        after_xl = r1_off[0]
        aggT = carve([EA + 1, T * P])
        cnt = carve([EA + 1, T * P], at=0)
        cinv = carve([P, T])
        cmax = carve([P, T])
        hs = carve([128, 2, MC * P])
        x2 = carve([P, 2, C])
        xl = carve([P, 2, C])
        tokr = carve([128, 2, KC * P])
        st2 = carve([P, 2, 6])
        mv2 = carve([P, 2, 2])
        sd2 = carve([P, 2, 1])
        rs2 = carve([P, 2, 1])
        lg = carve([P, T, E])
        pr = carve([P, T, E])
        pw = carve([P, T, E])
        eq = carve([P, T, E])
        pick = carve([P, T, E])
        slot = carve([P, T, E])
        tot = carve([128, E, T])
        cumt = carve([128, E, T])
        first = carve([P, T, E])
        second = carve([P, T, E])
        both = carve([P, T, E])
        top = carve([P, 2, T])
        red = carve([P, T])
        keep = carve([128, E, T])
        e_n = carve([128, E])
        e_i = carve([128, E], i32)
        e_pad = carve([1, E])
        e_end = carve([1, E])
        past = carve([1, NS, E])
        pasts = carve([1, NS, E])
        exp_f = carve([1, NS])
        row_f = carve([1, NS])
        r1_off[0] = after_xl
        xs = carve([128, SB, XF])
        xsT = carve([128, 2, C])
        hg = carve([128, 2, C])
        hT = carve([128, 2, C])
        ys = carve([128, SB, C])
        y_idx = carve([128, SB], u32)
        FT = 5
        yb = carve([P, 2, 2, FT, C])
        rank8 = sb("rank8", [P, E])

        NW = E * KC * C
        r2t = sb("r2t", [128, 2 * NW])
        phi_m = r2t[:, 0:(H // 2) * QC * 128].rearrange("p (g n) -> p g n", g=H // 2)
        phi = r2t[0:P, 0:2 * H * OFF * D].rearrange("p (u h o d) -> p u h o d", u=2, h=H, o=OFF)
        srt = r2t[:, 0:RB * RT * F].rearrange("p (u t f) -> p u t f", u=RB, t=RT)
        o1 = RB * RT * F
        oh = r2t[:, o1:o1 + 2 * RT * P].rearrange("p (u t c) -> p u t c", u=2, t=RT)
        key = sb("key", [128, 2, RT])
        ew1_s = r2t[:, 0:NW].rearrange("p (k n) -> p k n", k=KC)
        ew2_s = r2t[:, NW:2 * NW].rearrange("p (k n) -> p k n", k=KC)

        ps = ctx.enter_context(nc.psum_tensor("ps", [128, 8 * BANK], fp32))

        def bank(b, parts=128, a=0, z=BANK):
            return ps[0:parts, b * BANK + a:b * BANK + z]

        gate = sem("gate")
        src_loaded = sem("src_loaded")
        x_loaded = sem("x_loaded")
        w_loaded = sem("w_loaded")
        consts = sem("consts")
        zero_filled = sem("zero_filled")
        dve_step = sem("dve_step")
        pool_step = sem("pool_step")
        bias_zeroed = sem("bias_zeroed")
        bias_ready = sem("bias_ready")
        bias_spread = sem("bias_spread")
        brow_ps = sem("brow_ps")
        counted = sem("counted")
        totals_ps = sem("totals_ps")
        starts = sem("starts")
        starts_ps = sem("starts_ps")
        geg_ready = sem("geg_ready")
        groups_ps = sem("groups_ps")
        addr_ready = sem("addr_ready")
        offs_ready = sem("offs_ready")
        var_ready = sem("var_ready")
        std_ready = sem("std_ready")
        chunk_loaded = [sem(f"chunk_loaded{h}") for h in range(2)]
        chunk_keyed = sem("chunk_keyed")
        scattered = [sem(f"scattered{h}") for h in range(2)]
        m_zeroed = sem("m_zeroed")
        xn_ready = sem("xn_ready")
        xT_ps = sem("xT_ps")
        xT_ready = sem("xT_ready")
        xT_kept = sem("xT_kept")
        kv_ps = sem("kv_ps")
        kdup_ready = sem("kdup_ready")
        vn_ready = sem("vn_ready")
        phi_ready = sem("phi_ready")
        ssq_ready = sem("ssq_ready")
        nm_ready = sem("nm_ready")
        rk2_ready = sem("rk2_ready")
        rk_ready = sem("rk_ready")
        vr_ready = sem("vr_ready")
        kn_ready = sem("kn_ready")
        last_ready = sem("last_ready")
        m_added = sem("m_added")
        m_copied = sem("m_copied")
        mT_ps = sem("mT_ps")
        mT_taken = sem("mT_taken")
        m_ready = sem("m_ready")
        hpre_stored = [sem(f"hpre_stored{h}") for h in range(2)]
        xr_ready = sem("xr_ready")
        q_ps = sem("q_ps")
        qsq_ready = sem("qsq_ready")
        qssq_ready = sem("qssq_ready")
        qnm_ready = sem("qnm_ready")
        qinv_ready = sem("qinv_ready")
        qroot_ready = sem("qroot_ready")
        rq_ready = sem("rq_ready")
        qn_ready = sem("qn_ready")
        qdup_ready = sem("qdup_ready")
        qlin_ready = sem("qlin_ready")
        qphi_ready = [sem(f"qphi_ready{h}") for h in range(2)]
        qlast_ready = sem("qlast_ready")
        NJ = H + 2
        grp_ps = [sem(f"grp_ps{j}") for j in range(2)]
        grp_ready = [sem(f"grp_ready{j}") for j in range(2)]
        y_added = [sem(f"y_added{j}") for j in range(2)]
        yT_ready = sem("yT_ready")
        y_ps = sem("y_ps")
        ry_ready = sem("ry_ready")
        attn_ready = sem("attn_ready")
        attnT_ps = sem("attnT_ps")
        attnT_ready = sem("attnT_ready")
        proj_ps = sem("proj_ps")
        x1_ready = sem("x1_ready")
        acc_zeroed = sem("acc_zeroed")
        rows_loaded = [sem(f"rows_loaded{h}") for h in range(RB)]
        key_ready = sem("key_ready")
        onehot_ready = sem("onehot_ready")
        rows_used = sem("rows_used")
        cnt_copied = sem("cnt_copied")
        cnt_ps = sem("cnt_ps")
        sums_copied = sem("sums_copied")
        inv_ready = sem("inv_ready")
        inv_ps = sem("inv_ps")
        mean_ready = sem("mean_ready")
        agg_one = sem("agg_one")
        ew_loaded = sem("ew_loaded")
        hpre_back = [sem(f"hpre_back{h}") for h in range(2)]
        ha_ps = sem("ha_ps")
        hsum_ready = sem("hsum_ready")
        hs_ready = sem("hs_ready")
        gnn_ps = sem("gnn_ps")
        x2_ready = sem("x2_ready")
        st2_ready = sem("st2_ready")
        mv2_ready = sem("mv2_ready")
        ve2_ready = sem("ve2_ready")
        sd2_ready = sem("sd2_ready")
        rs2_ready = sem("rs2_ready")
        xl_ready = sem("xl_ready")
        xl_kept = sem("xl_kept")
        res_ready = sem("res_ready")
        tok_ps = sem("tok_ps")
        tokr_ready = sem("tokr_ready")
        lg_ps = sem("lg_ps")
        lg_ready = sem("lg_ready")
        sh_ready = sem("sh_ready")
        ex_ready = sem("ex_ready")
        mask_ready = sem("mask_ready")
        ranks_ps = sem("ranks_ps")
        totals_taken = sem("totals_taken")
        meta_ready = sem("meta_ready")
        meta2_ready = sem("meta2_ready")
        pads_ready = sem("pads_ready")
        table_ready = sem("table_ready")
        routed_rows = [sem(f"routed_rows{c}") for c in range(3)]
        spare_filled = sem("spare_filled")
        xs_loaded = [sem(f"xs_loaded{h}") for h in range(SB)]
        xs_ps = sem("xs_ps")
        xsT_ready = sem("xsT_ready")
        eh_ps = sem("eh_ps")
        hg_ready = sem("hg_ready")
        hg_ps = sem("hg_ps")
        hT_ready = sem("hT_ready")
        ey_ps = sem("ey_ps")
        ys_ready = sem("ys_ready")
        idx_ready = sem("idx_ready")
        ys_stored = [sem(f"ys_stored{h}") for h in range(SB)]
        yb_loaded = [sem(f"yb_loaded{h}") for h in range(2)]
        yb_added = sem("yb_added")
        stored = sem("stored")

        block = ctx.enter_context(nc.Block())

        def wait(eng, s, n):
            if not (isinstance(n, int) and n <= 0):
                eng.wait_ge(s, n)

        def hold(eng, s, n):
            if not (isinstance(n, int) and n <= 0):
                eng.wait_ge(s, n)
                eng.sem_inc(gate)

        def tiles(eng, body, lo, ahead, behind):
            hi = T - ahead
            n = (hi - lo) // 2
            for t in range(lo):
                body(t, t % 2, t // 2)
            with eng.Fori(0, n) as i:
                for k in range(2):
                    body(i * 2 + (lo + k), (lo + k) % 2, i + (lo + k) // 2)
            for t in range(lo + 2 * n, T + behind):
                body(t, t % 2, t // 2)

        def step_at(st, d):
            s, h, nth = st
            return s + d, (h + d) % SB, nth + (h + d) // SB

        def steps(eng, body, lo, ahead):
            n = (NS - ahead - lo) // SB
            body([(s, s % SB, s // SB) for s in range(lo)])
            with eng.Fori(0, n) as i:
                body([(i * SB + (lo + k), (lo + k) % SB, i + (lo + k) // SB) for k in range(SB)])
            body([(s, s % SB, s // SB) for s in range(lo + n * SB, NS + 2)])

        def some(st):
            return not isinstance(st[0], int) or 0 <= st[0] < NS

        def inside(t):
            return not isinstance(t, int) or 0 <= t < T

        def overlapped(v, u, h0, nh):
            w = v[:, u, h0:h0 + nh, :]
            return bass.AP(w.tensor, w.offset, [w.ap[0], [2 * D, nh], [1, OFF], [1, D]])

        def split(t, j):
            return t * (NJ // 2) + (j // 2 + 1)


        @block.sync
        def _(sp):
            sp.dma_start(src_i[:, :], src.rearrange("(p j) -> p j", p=P)).then_inc(src_loaded, 16)
            sp.dma_start(x_res[:, :, :], x.rearrange("(t p) c -> p t c", p=P)).then_inc(x_loaded, 16)
            sp.wait_ge(consts, 1)
            with sp.Fori(0, NR) as c:
                sp.dma_start(sorted_v[:, bass.ds(c * RT, RT), :],
                             zeros[:, :].rearrange("p (t f) -> p t f", f=F)).then_inc(zero_filled, 16)
            ea = edge_attr.rearrange("(p j) f -> p j f", p=P)

            def load_chunk(c, h):
                sp.dma_start(stage[:, h, :, 0:EA], ea[:, bass.ds(c * CH, CH), :]).then_inc(chunk_loaded[h], 16)

            load_chunk(0, 0)
            load_chunk(1, 1)
            with sp.Fori(0, NCH // 2 - 1) as i:
                for h in range(2):
                    sp.wait_ge(scattered[h], i * (16 * CH) + 16 * CH)
                    load_chunk(i * 2 + (2 + h), h)
            sp.wait_ge(scattered[0], (NCH // 2) * 16 * CH)
            load_chunk(NCH - 1, 0)

            sp.wait_ge(scattered[0], (NCH // 2 + 1) * 16 * CH)
            sp.wait_ge(scattered[1], (NCH // 2) * 16 * CH)
            sp.wait_ge(x1_ready, T)

            def load_rows(c, h):
                sp.dma_start(srt[:, h, :, :], sorted_v[:, bass.ds(c * RT, RT), :]).then_inc(rows_loaded[h], 16)

            for c in range(RB):
                load_rows(c, c)

            def reload_rows(c, h):
                sp.wait_ge(rows_used, c - (RB - 1))
                load_rows(c, h)
            for c in range(RB, RB + 3):
                reload_rows(c, c % RB)
            with sp.Fori(0, (NR - RB - 3) // RB) as i:
                for h in range(RB):
                    reload_rows(i * RB + (RB + 3 + h), (3 + h) % RB)
            hv = hpre_dram.rearrange("(t p) c -> t p c", p=128)

            def load_hpre(t, u, k):
                if not inside(t):
                    return
                wait(sp, hsum_ready, t - 1)
                sp.dma_start(hpre2[:, u, :], hv[bass.ds(t, 1), :, :].rearrange("a p c -> (a p) c")).then_inc(hpre_back[u], 16)
            sp.wait_ge(hpre_stored[0], 16 * (T // 2 + 1))
            sp.wait_ge(hpre_stored[1], 16 * (T // 2))
            load_hpre(0, 0, 0)
            load_hpre(1, 1, 0)
            sp.wait_ge(rows_used, NR)
            for k in range(KC):
                for dst, w in ((ew1_s, ew1), (ew2_s, ew2)):
                    sp.dma_start(dst[:, k, :].rearrange("p (e n) -> p e n", e=E),
                                 w.rearrange("e (k p) n -> k p e n", p=128)[k]).then_inc(ew_loaded, 16)
            sp.wait_ge(consts, 22)
            sp.dma_start(routed[E * REG:E * REG + 128, :], pad_rows[:, :]).then_inc(spare_filled, 16)
            for t in (2, 3):
                load_hpre(t, t % 2, 0)
            with sp.Fori(0, (T - 5) // 2) as i:
                for k in range(2):
                    load_hpre(i * 2 + (4 + k), k, 0)
            load_hpre(T - 1, 0, 0)

            sp.wait_ge(table_ready, 1)
            for c, count in ((0, T), (1, T), (2, E)):
                sp.wait_ge(routed_rows[c], 16 * count)
            sp.wait_ge(spare_filled, 16)

            def load_steps(sts):
                for s, h, nth in filter(some, sts):
                    row = sp.value_load(row_i[0:1, bass.ds(s, 1)], min_val=0, max_val=E * REG)
                    wait(sp, ys_ready, s - (SB - 1))
                    wait(sp, idx_ready, s - (SB - 1))
                    sp.dma_start(xs[:, h, :], routed[bass.ds(row, 128), :]).then_inc(xs_loaded[h], 16)
            steps(sp, load_steps, SB, 0)

            for h in range(SB):
                sp.wait_ge(ys_stored[h], 16 * ((NS - h + SB - 1) // SB))

            def load_outputs(g):
                if g >= 2:
                    sp.wait_ge(yb_added, g - 1)
                for c in range(2):
                    sp.dma_start(yb[:, g % 2, c, :, :], youts[c * N + g * FT * P:c * N + (g + 1) * FT * P, :]
                                 .rearrange("(t p) c -> p t c", p=P)).then_inc(yb_loaded[g % 2], 16)
            load_outputs(0)
            load_outputs(1)
            for g in range(T // FT):
                sp.wait_ge(yb_added, g + 1)
                sp.dma_start(out.rearrange("(t p) c -> p t c", p=P)[:, g * FT:(g + 1) * FT, :],
                             x_res[:, g * FT:(g + 1) * FT, :]).then_inc(stored, 16)
                if g + 2 < T // FT:
                    load_outputs(g + 2)
            sp.wait_ge(stored, 16 * (T // FT))

        @block.gpsimd
        def _(pool):
            n = [0]

            def iota(v, pattern, cm=0):
                pool.iota(v, pattern, base=0, channel_multiplier=cm,
                          allow_small_or_imprecise_dtypes=True).then_inc(consts, 1)

            pool.memset(zeros[:, :], 0.0).then_inc(consts, 1)
            iota(thr[:, :], [[P, T + 1]])
            iota(iota_g[:, :], [[S * GT, NG]])
            iota(iota_c[:, :], [[1, P]])
            pool.memset(ones[:, :], 1.0).then_inc(consts, 1)
            pool.memset(ident[:, :], 0.0).then_inc(consts, 1)
            pool.memset(upper[:, :], 0.0).then_inc(consts, 1)
            pool.memset(stage[:, :, :, EA:EA + 1], 1.0).then_inc(consts, 1)
            iota(rank8[:, :], [[-1, E]])
            iota(dst_row[:, :], [[P, T]], 1)
            iota(reg_start[:, :], [[REG, E]])
            iota(reg_fill[:, :], [[REG, E]], 1)
            iota(step_row[:, :], [[128, NS]])
            pool.memset(pad_rows[:, 0:C + 1], 0.0).then_inc(consts, 1)
            pool.memset(bias_more[:, :], 0.0).then_inc(bias_zeroed, 1)
            pool.iota(pad_rows[:, C + 1:XF], [[0, 1]], base=2 * N, channel_multiplier=1,
                      allow_small_or_imprecise_dtypes=True).then_inc(consts, 1)
            pool.memset(mask[:, :], SC4).then_inc(consts, 1)
            pool.memset(sq_half[:, :], 1.0).then_inc(consts, 1)
            pool.wait_ge(consts, 17)
            pool.affine_select(out=ident[:, :], in_=ident[:, :], compare_op=ALU.not_equal, fill=1.0, base=0,
                               pattern=[[-1, 128]], channel_multiplier=1).then_inc(consts, 1)
            pool.affine_select(out=upper[:, :], in_=upper[:, :], compare_op=ALU.is_ge, fill=1.0, base=0,
                               pattern=[[-1, P]], channel_multiplier=1).then_inc(consts, 1)
            pool.affine_select(out=sq_half[:, :], in_=sq_half[:, :], compare_op=ALU.is_ge, fill=0.5, base=-D,
                               pattern=[[0, 1]], channel_multiplier=1).then_inc(consts, 1)
            for lo, w in ((2 * LF - 1, SC2), (LF + 16, 1.0), (LF, SC4), (LF - 1, SC2), (16, 1.0)):
                pool.affine_select(out=mask[:, :], in_=mask[:, :], compare_op=ALU.is_ge, fill=w, base=-lo,
                                   pattern=[[0, 2 * VE]], channel_multiplier=1).then_inc(pool_step, 1)
                n[0] += 1
                pool.wait_ge(pool_step, n[0])
            pool.affine_select(out=mask[:, 0:VE], in_=mask[:, 0:VE], compare_op=ALU.is_ge, fill=0.0, base=LF - 1,
                               pattern=[[0, VE]], channel_multiplier=-1).then_inc(consts, 1)
            pool.affine_select(out=mask[:, VE:2 * VE], in_=mask[:, VE:2 * VE], compare_op=ALU.is_ge, fill=0.0, base=-LF,
                               pattern=[[0, VE]], channel_multiplier=1).then_inc(consts, 1)

            pool.wait_ge(addr_ready, 1)
            pool.wait_ge(zero_filled, 16 * NR)

            def scatter(c, h, nth):
                hold(pool, chunk_loaded[h], nth * 16)
                if not (isinstance(nth, int) and nth == 1):
                    hold(pool, scattered[h], nth * (16 * CH) - 16 * CH)
                pool.tensor_copy(idx[:, h, :], addr[:, bass.ds(c * CH, CH)]).then_inc(chunk_keyed, 1)
                pool.tensor_copy(stage[:, h, :, EA + 1:EA + 2],
                                 src_f[:, bass.ds(c * CH, CH)].unsqueeze(2)).then_inc(chunk_keyed, 1)
                hold(pool, chunk_keyed, c * 2 + 2)
                for j in range(CH):
                    pool.indirect_dma_start(out=sorted_rows,
                                            out_offset=bass.IndirectOffsetOnAxis(ap=idx[:, h, j:j + 1], axis=0),
                                            in_=stage[:, h, j, :], in_offset=None).then_inc(scattered[h], 16)
            scatter(0, 0, 1)
            scatter(1, 1, 1)
            with pool.Fori(0, NCH // 2 - 1) as i:
                for h in range(2):
                    scatter(i * 2 + (2 + h), h, i + 2)
            scatter(NCH - 1, 0, NCH // 2 + 1)
            pool.wait_ge(x1_ready, T)
            pool.memset(aggT[EA:EA + 1, :], 1.0).then_inc(agg_one, 1)

            def res(t, u):
                if not inside(t):
                    return
                hold(pool, xl_ready, t + 1)
                pool.tensor_tensor(x_res[:, bass.ds(t, 1), :].rearrange("p a c -> p (a c)"), x2[:, u, :], xl[:, u, :],
                                   ALU.add).then_inc(res_ready, 1)
                pool.tensor_copy(xl_all[:, bass.ds(t, 1), 0:C].rearrange("p a c -> p (a c)"), xl[:, u, :]).then_inc(xl_kept, 1)

            def body(t, u, k):
                res(t - 2, u)
            tiles(pool, body, 6, 3, 4)

            pool.wait_ge(xl_kept, T)
            pool.wait_ge(pads_ready, 1)
            for e in range(E):
                pool.indirect_dma_start(out=routed, out_offset=bass.IndirectOffsetOnAxis(ap=pad_idx[:, e:e + 1], axis=0),
                                        in_=pad_rows[:, :], in_offset=None).then_inc(routed_rows[2], 16)
            for c in range(2):
                pool.wait_ge((meta_ready, meta2_ready)[c], 1)
                for t in range(T):
                    pool.indirect_dma_start(out=routed,
                                            out_offset=bass.IndirectOffsetOnAxis(ap=row_idx[:, c, t:t + 1], axis=0),
                                            in_=xl_all[:, t, :], in_offset=None).then_inc(routed_rows[c], 16)

            def scatter_outputs(sts):
                for s, h, nth in filter(some, sts):
                    hold(pool, ys_ready, s + 1)
                    hold(pool, idx_ready, s + 1)
                    pool.indirect_dma_start(out=youts, out_offset=bass.IndirectOffsetOnAxis(ap=y_idx[:, h:h + 1], axis=0),
                                            in_=ys[:, h, :], in_offset=None, bounds_check=2 * N - 1, oob_is_err=False).then_inc(ys_stored[h], 16)
            steps(pool, scatter_outputs, SB, 0)

        @block.scalar
        def _(act):
            def load(dst, s, slow=False):
                act.dma_start(dst, s, allow_slow_non_contiguous=slow).then_inc(w_loaded, 16)

            load(wqkv[:, :, :], WqkvT.rearrange("(k p) n -> p k n", p=128))
            load(w1x[:, :, :], W1[0:C, :].rearrange("(k p) n -> p k n", p=128))
            load(w1a[0:EA, :], W1[C:C + EA, :])
            load(w1u[:, :], W1[C + EA:C + EA + 128, :])
            load(bias_rows[0:3, :], bqkv.rearrange("(a n) -> a n", a=3))
            act.wait_ge(bias_zeroed, 1)
            load(bias_more[3:4, :], b2.rearrange("(a n) -> a n", a=1))
            load(w1a[EA:EA + 1, :], b1.rearrange("(a n) -> a n", a=1))
            load(bias_rows[3:4, :], bproj.rearrange("(a n) -> a n", a=1))
            load(u0[:, :], u_in[0:1, :].rearrange("a p -> p a"), slow=True)
            load(temp[:, :], temperature.rearrange("(a n) -> a n", a=1).to_broadcast([P, H]))
            load(wproj[:, :, :], WprojT.rearrange("(k p) n -> p k n", p=128))
            load(w2s[:, :, :], W2.rearrange("(k p) n -> p k n", p=128))
            load(wr[:, :, :], routerT.rearrange("(k p) n -> p k n", p=128))
            load(bias_rows[4:4 + E, :], eb1)
            load(bias_rows[4 + E:4 + 2 * E, :], eb2)

            act.wait_ge(bias_ready, 1)
            for m in range(3):
                act.dma_start(bias3[m:m + 1, :, :], bparts[:, m, :]).then_inc(bias_spread, 16)
            act.wait_ge(var_ready, 1)
            act.activation(rstd[:, :], rstd[:, :], ACT.Sqrt).then_inc(std_ready, 1)

            def xT_copy(t, u):
                if not inside(t):
                    return
                wait(act, xT_ps, t + 1)
                wait(act, kv_ps, t - 1)
                act.activation(xT[:, u, :, :], bank(0, 128, 0, KC * P).rearrange("p (k c) -> p k c", k=KC),
                               ACT.Copy).then_inc(xT_ready, 1)

            def pass1(t, u, k):
                if inside(t):
                    wait(act, kv_ps, t + 1)
                    wait(act, phi_ready, t - 1)
                    act.activation(kdup[:, u, :, :].rearrange("p h (a d) -> p h a d", a=2),
                                   bank(1 + u, P, 0, C).rearrange("p (h d) -> p h d", h=H).unsqueeze(2)
                                   .to_broadcast([P, H, 2, D]), ACT.Copy).then_inc(kdup_ready, 1)
                    wait(act, m_added, t - 1)
                    act.activation(vn[:, u, :, 0:D], bank(1 + u, P, C, 2 * C).rearrange("p (h d) -> p h d", h=H),
                                   ACT.Copy, scale=1.0 / N).then_inc(vn_ready, 1)
                    hold(act, xT_ready, t + 1)
                    act.activation(xT_all[:, :, bass.ds(t * P, P)], xT[:, u, :, :], ACT.Copy).then_inc(xT_kept, 1)
                    xT_copy(t + 1, 1 - u)
                if inside(t - 1):
                    v = 1 - u
                    wait(act, rk2_ready, t)
                    act.activation(rr[:, v, :], r2[:, v, :], ACT.Sqrt).then_inc(rk_ready, 1)
            xT_copy(0, 0)
            tiles(act, pass1, 3, 1, 1)

            act.wait_ge(m_ready, 1)

            def q_square(t, u):
                if not inside(t):
                    return
                wait(act, q_ps, t + 1)
                wait(act, qssq_ready, t - 1)
                act.activation(sqs[:, u, :], bank((0, 6)[u], P, 0, C), ACT.Square).then_inc(qsq_ready, 1)

            def q_root(t, u):
                if not inside(t):
                    return
                wait(act, qinv_ready, t + 1)
                act.activation(rr[:, u, :], r2[:, u, :], ACT.Sqrt).then_inc(qroot_ready, 1)

            def q_rows(t, u):
                if not inside(t):
                    return
                wait(act, qn_ready, t + 1)
                wait(act, qphi_ready[1], t - 1)
                act.activation(kdup[:, u, :, :].rearrange("p h (a d) -> p h a d", a=2),
                               bank((0, 6)[u], P, 0, C).rearrange("p (h d) -> p h d", h=H).unsqueeze(2)
                               .to_broadcast([P, H, 2, D]), ACT.Copy).then_inc(qdup_ready, 1)
                wait(act, qdup_ready, t + 1)
                wait(act, grp_ps[0], (t - 2) * (NJ // 2) + (H // 2 + 1))
                act.activation(last[:, u, :, 16:16 + D], kdup[:, u, :, 0:D], ACT.Copy).then_inc(qlin_ready, 1)

            def attn_copy(t, u):
                if not inside(t):
                    return
                wait(act, attnT_ps, t + 1)
                act.activation(attnT[:, u, :, :], bank(7, 128, 0, KC * P).rearrange("p (k c) -> p k c", k=KC),
                               ACT.Copy).then_inc(attnT_ready, 1)

            def yT_copy(t, u):
                if not inside(t):
                    return
                wait(act, y_added[0], (t + 1) * (H // 2 + 1))
                wait(act, y_ps, t)
                act.activation(yT[:, :], bank(3 + u, 128, 0, (H // 2) * P), ACT.Copy).then_inc(yT_ready, 1)

            def pass2(t, u, k):
                if inside(t):
                    for j in range(NJ):
                        rows = 2 * LF if j == H else 128
                        if j < NJ - 1:
                            wait(act, grp_ps[j % 2], split(t, j))
                            wait(act, y_added[j % 2], t * (H // 2 + 1 - j % 2) + j // 2)
                            act.activation(phT[0:rows, j % 2, :], bank(1 + j % 2, rows, 0, QC * P),
                                           ACT.Copy).then_inc(grp_ready[j % 2], 1)
                        else:
                            wait(act, grp_ps[j % 2], split(t, j))
                            wait(act, hpre_stored[u], k * 16)
                            act.activation(hpre[:, u, :], bank(1 + j % 2, 128, 0, MC * P), ACT.Copy).then_inc(grp_ready[j % 2], 1)
                            hold(act, grp_ready[j % 2], split(t, j))
                            act.dma_start(hpre_dram[bass.ds(t * 128, 128), :], hpre[:, u, :]).then_inc(hpre_stored[u], 16)
                        if j == 0:
                            q_square(t + 2, u)
                        if j == 2:
                            yT_copy(t - 1, 1 - u)
                        if j == 4:
                            q_root(t + 2, u)
                        if j == 5:
                            attn_copy(t - 1, 1 - u)
                        if j == 6:
                            q_rows(t + 2, u)
                else:
                    yT_copy(t - 1, 1 - u)
                    attn_copy(t - 1, 1 - u)
            for t in range(2):
                q_square(t, t)
                q_root(t, t)
                q_rows(t, t)
            tiles(act, pass2, 4, 3, 2)

            act.wait_ge(rows_used, NR)
            for b in range(NBK):
                nb = min(BPB, T - b * BPB) * P
                act.activation(cnt[EA:EA + 1, b * BPB * P:b * BPB * P + nb], ps[EA:EA + 1, b * BANK:b * BANK + nb],
                               ACT.Copy).then_inc(cnt_copied, 1)

            def relu(t, u):
                if not inside(t):
                    return
                wait(act, hsum_ready, t + 1)
                act.activation(hs[:, u, :], hs[:, u, :], ACT.Relu).then_inc(hs_ready, 1)

            def sd(t, u):
                if not inside(t):
                    return
                wait(act, ve2_ready, t + 1)
                act.activation(sd2[:, u, :], sd2[:, u, :], ACT.Sqrt).then_inc(sd2_ready, 1)

            def tok_copy(t, u):
                if not inside(t):
                    return
                wait(act, tok_ps, t + 1)
                wait(act, lg_ps, t - 1)
                act.activation(tokr[:, u, :], bank(5, 128, 0, KC * P), ACT.Copy).then_inc(tokr_ready, 1)

            def gnn(t, u, k):
                relu(t, u)
                sd(t - 1, 1 - u)
                tok_copy(t - 3, 1 - u)
            tiles(act, gnn, 6, 3, 4)

            act.wait_ge(sh_ready, 1)
            act.activation(pr[:, :, :], pr[:, :, :], ACT.Exp).then_inc(ex_ready, 1)

            def xsT_copy(st):
                if not some(st):
                    return
                s, h, nth = st
                wait(act, xs_ps, s + 1)
                wait(act, eh_ps, s - 1)
                act.activation(xsT[:, h % 2, :], bank(h % 2, 128, 0, C), ACT.Copy).then_inc(xsT_ready, 1)

            def gelu(st):
                if not some(st):
                    return
                s, h, nth = st
                wait(act, eh_ps, s + 1)
                wait(act, hg_ps, s - 1)
                act.activation(hg[:, h % 2, :], bank(2 + h % 2, 128, 0, C), ACT.Gelu).then_inc(hg_ready, 1)

            def expert_steps(sts):
                for st in sts:
                    xsT_copy(step_at(st, 2))
                    gelu(step_at(st, 1))
            xsT_copy((0, 0, 0))
            xsT_copy((1, 1, 0))
            gelu((0, 0, 0))
            steps(act, expert_steps, SB, 2)

        @block.tensor
        def _(pe):
            mm = pe.matmul
            pe.wait_ge(consts, 22)
            pe.wait_ge(counted, 1)
            mm(bank(0, P, 0, T), lhsT=upper[:, :], rhs=per_part[:, :], start=True, stop=True)
            mm(bank(1, 128, 0, T), lhsT=ones[0:P, :], rhs=per_part[:, :], start=True, stop=True).then_inc(totals_ps, 1)
            pe.wait_ge(starts, 1)
            pe.transpose(bank(2, T + 1, 0, 128), start[:, :], ident[:, :]).then_inc(starts_ps, 1)
            pe.wait_ge(w_loaded, 16 * 15)
            mm(ps[EA:EA + 1, 3 * BANK:3 * BANK + HID], lhsT=u0[:, :], rhs=w1u[:, :], start=True, stop=True).then_inc(brow_ps, 1)
            pe.wait_ge(geg_ready, 1)
            mm(bank(2, 128, 0, NG), lhsT=ones[0:T, :], rhs=geg[:, :], start=True, stop=True).then_inc(groups_ps, 1)
            pe.wait_ge(offs_ready, 1)
            pe.wait_ge(bias_spread, 48)
            pe.wait_ge(var_ready, 1)
            for b in (3, 4, 5, 6, 7):
                mm(bank(b), lhsT=zeros[:, 0:128], rhs=zeros[:, 0:BANK], start=True, stop=False, skip_group_check=True)

            def xT_of(t, u):
                if not inside(t):
                    return
                wait(pe, xn_ready, t + 1)
                wait(pe, xT_ready, t)
                for k in range(KC):
                    m = pe.transpose(bank(0, 128, k * P, (k + 1) * P), xn[:, u, k * 128:(k + 1) * 128], ident[0:P, 0:P])
                m.then_inc(xT_ps, 1)

            def project(dst, xt, c0, width):
                for k in range(KC):
                    mm(dst, lhsT=xt[:, k, :], rhs=wqkv[:, k, c0:c0 + width], start=(k == 0), stop=False)
                return mm(dst, lhsT=ones3[:, :], rhs=bias3[:, c0 // C:(c0 + width) // C, :].rearrange("p a c -> p (a c)"), start=False, stop=True)

            def sums(t, u):
                if not inside(t):
                    return
                wait(pe, vr_ready, t + 1)
                wait(pe, phi_ready, t + 1)
                for h in range(H):
                    a = VW * (h % 2)
                    mm(ps[a:a + VW, (4 + h // 2) * BANK:(5 + h // 2) * BANK], lhsT=vr[:, u, h, :],
                       rhs=phi[:, u, h, :, :].rearrange("p o d -> p (o d)"), start=False, stop=False, skip_group_check=True)
                wait(pe, last_ready, t + 1)
                for g in range(H // 2):
                    m = mm(bank(3, 2 * LF, g * 2 * VE, (g + 1) * 2 * VE),
                           lhsT=last[:, u, 2 * g:2 * g + 2, :].rearrange("p h f -> p (h f)"),
                           rhs=vn[:, u, 2 * g:2 * g + 2, 0:VE], start=False, stop=False, skip_group_check=True)
                m.then_inc(m_added, 1)

            def pass1(t, u, k):
                if inside(t):
                    wait(pe, xT_ready, t + 1)
                    wait(pe, kn_ready, t - 1)
                    wait(pe, vn_ready, t - 1)
                    project(bank(1 + u, P), xT[:, u], C, 2 * C).then_inc(kv_ps, 1)
                    xT_of(t + 1, 1 - u)
                sums(t - 1, 1 - u)
            xT_of(0, 0)
            tiles(pe, pass1, 3, 1, 1)

            for g in range(H // 2):
                pe.wait_ge(m_copied, g + 1)
                if g >= 2:
                    pe.wait_ge(mT_taken, g - 1)
                for c in range(QC):
                    m = pe.transpose(bank(g % 2, 128, c * 128, (c + 1) * 128), phi_m[:, g, c * 128:(c + 1) * 128], ident[:, :])
                m.then_inc(mT_ps, 1)

            pe.wait_ge(m_ready, 1)

            def queries(t, u):
                if not inside(t):
                    return
                wait(pe, xr_ready, t + 1)
                wait(pe, qphi_ready[1], t - 1)
                project(bank((0, 6)[u], P, 0, C), xT[:, u], 0, C).then_inc(q_ps, 1)

            def group(t, u, j):
                if j == 0:
                    wait(pe, qphi_ready[0], t + 1)
                if j == H // 2:
                    wait(pe, qphi_ready[1], t + 1)
                if j == H:
                    wait(pe, qlast_ready, t + 1)
                wait(pe, grp_ready[j % 2], split(t, j) - 1)
                if j < H:
                    for c in range(QC):
                        m = pe.transpose(bank(1 + j % 2, 128, c * P, (c + 1) * P),
                                         phi[:, u, j, c * 4:(c + 1) * 4, :].rearrange("p o d -> p (o d)"), ident[0:P, 0:P])
                elif j == H:
                    for g in range(H // 2):
                        m = pe.transpose(bank(1 + j % 2, 2 * LF, g * P, (g + 1) * P),
                                         last[:, u, 2 * g:2 * g + 2, :].rearrange("p h f -> p (h f)"), ident[0:P, 0:P])
                else:
                    for c in range(MC):
                        for kk in range(KC):
                            m = mm(bank(1 + j % 2, 128, c * P, (c + 1) * P), lhsT=w1x[:, kk, c * 128:(c + 1) * 128],
                                   rhs=xT_all[:, kk, bass.ds(t * P, P)], start=(kk == 0), stop=(kk == KC - 1))
                m.then_inc(grp_ps[j % 2], 1)

            def outputs(t, u, j):
                wait(pe, grp_ready[j % 2], split(t, j))
                if j == 0:
                    wait(pe, yT_ready, t - 1)

                def y(h):
                    a = VW * (h % 2)
                    return ps[a:a + VW, (3 + u) * BANK + (h // 2) * P:(3 + u) * BANK + (h // 2 + 1) * P]
                if j < H:
                    for c in range(QC):
                        m = mm(y(j), lhsT=mq[:, j // 2, c, (j % 2) * VW:(j % 2 + 1) * VW], rhs=phT[:, j % 2, c * P:(c + 1) * P],
                               start=(j < 2 and c == 0), stop=False, skip_group_check=True)
                else:
                    for h in range(H):
                        m = mm(y(h), lhsT=ml[:, h // 2, (h % 2) * VW:(h % 2 + 1) * VW],
                               rhs=phT[0:2 * LF, j % 2, (h // 2) * P:(h // 2 + 1) * P], start=False, stop=(h >= H - 2),
                               skip_group_check=True)
                m.then_inc(y_added[j % 2], 1)

            def y_T(t, u):
                if not inside(t):
                    return
                wait(pe, yT_ready, t + 1)
                wait(pe, attn_ready, t)
                for g in range(H // 2):
                    m = pe.transpose(bank(5, P, g * 2 * VW, (g + 1) * 2 * VW), yT[:, g * P:(g + 1) * P], ident[:, :])
                m.then_inc(y_ps, 1)

            def attn_T(t, u):
                if not inside(t):
                    return
                wait(pe, attn_ready, t + 1)
                wait(pe, x1_ready, t)
                for k in range(KC):
                    m = pe.transpose(bank(7, 128, k * P, (k + 1) * P), attn[:, u, k * 128:(k + 1) * 128], ident[0:P, 0:P])
                m.then_inc(attnT_ps, 1)

            def proj(t, u):
                if not inside(t):
                    return
                wait(pe, attnT_ready, t + 1)
                dst = bank(7, P, 256, 256 + C)
                for k in range(KC):
                    mm(dst, lhsT=attnT[:, u, k, :], rhs=wproj[:, k, :], start=(k == 0), stop=False)
                mm(dst, lhsT=ones3[:, :], rhs=bias3[:, 3, :], start=False, stop=True).then_inc(proj_ps, 1)

            def pass2(t, u, k):
                if inside(t):
                    for j in range(NJ):
                        group(t, u, j)
                        if j >= 1:
                            outputs(t, u, j - 1)
                        if j == 1:
                            queries(t + 2, u)
                        if j == 3:
                            y_T(t - 1, 1 - u)
                        if j == 6:
                            attn_T(t - 1, 1 - u)
                    proj(t - 1, 1 - u)
                else:
                    y_T(t - 1, 1 - u)
                    attn_T(t - 1, 1 - u)
                    proj(t - 1, 1 - u)
            queries(0, 0)
            queries(1, 1)
            tiles(pe, pass2, 4, 3, 2)

            pe.wait_ge(x1_ready, T)
            for b in range(NBK):
                mm(bank(b, EA + 1), lhsT=zeros[:, 0:EA + 1], rhs=zeros[:, 0:BANK], start=True, stop=False, skip_group_check=True)

            def offset(c, g):
                return pe.value_load(off_i[0:1, bass.ds(c * RG + g, 1)], min_val=0,
                                     max_val=(T - 1) // BPB * BANK + (T - 1) % BPB * P)

            def add_rows(chunks):
                off = offset(chunks[0][0], 0)
                for n_, (c, h, o, nth) in enumerate(chunks):
                    wait(pe, rows_loaded[h], nth * 16)
                    hold(pe, onehot_ready, c + 1)
                    for g in range(RG):
                        here = off
                        if g + 1 < RG:
                            off = offset(c, g + 1)
                        elif n_ + 1 < len(chunks):
                            off = offset(chunks[n_ + 1][0], 0)
                        for k in range(GT):
                            m = mm(ps[0:EA + 1, bass.ds(here, P)], lhsT=srt[:, h, g * GT + k, 0:EA + 1],
                                   rhs=oh[:, o, g * GT + k, :], start=False, stop=False, skip_group_check=True)
                    m.then_inc(rows_used, 1)
            add_rows([(c, c, c % 2, 1) for c in range(3)])
            with pe.Fori(0, (NR - 3) // RB) as i:
                add_rows([(i * RB + (3 + k), (3 + k) % RB, (3 + k) % 2, i + (3 + k) // RB + 1) for k in range(RB)])
            for t in range(T):
                if t % BPB == 0:
                    pe.wait_ge(cnt_copied, t // BPB + 1)
                m = mm(bank(7, P, t, t + 1), lhsT=cnt[EA:EA + 1, t * P:(t + 1) * P], rhs=ones[EA:EA + 1, 0:1],
                       start=True, stop=True)
            m.then_inc(cnt_ps, 1)
            pe.wait_ge(inv_ready, 1)
            for b in range(NBK):
                pe.wait_ge(sums_copied, NBK)
                for t in range(b * BPB, min((b + 1) * BPB, T)):
                    m = mm(bank((b - 1) % 8, EA, t % BPB * P, (t % BPB + 1) * P), lhsT=cinv[:, t:t + 1].to_broadcast([P, EA]),
                           rhs=ident[0:P, 0:P], start=True, stop=True)
                m.then_inc(inv_ps, 1)

            pe.wait_ge(mean_ready, NBK)
            pe.wait_ge(agg_one, 1)

            def ha(t, u):
                if not inside(t):
                    return
                wait(pe, hsum_ready, t - 1)
                for m in range(MC):
                    z = mm(bank(1 + u, 128, m * P, (m + 1) * P), lhsT=w1a[:, m * 128:(m + 1) * 128], rhs=aggT[:, bass.ds(t * P, P)],
                           start=True, stop=True)
                z.then_inc(ha_ps, 1)

            def layer2(t, u):
                if not inside(t):
                    return
                wait(pe, hs_ready, t + 1)
                wait(pe, x2_ready, t - 1)
                for m in range(MC):
                    z = mm(bank(3 + u, P, 0, C), lhsT=hs[:, u, m * P:(m + 1) * P], rhs=w2s[:, m, :], start=(m == 0),
                           stop=(m == MC - 1))
                z.then_inc(gnn_ps, 1)

            def tok_T(t, u):
                if not inside(t):
                    return
                wait(pe, xl_ready, t + 1)
                wait(pe, tokr_ready, t)
                for k in range(KC):
                    m = pe.transpose(bank(5, 128, k * P, (k + 1) * P), xl[:, u, k * 128:(k + 1) * 128], ident[0:P, 0:P])
                m.then_inc(tok_ps, 1)

            def router(t, u):
                if not inside(t):
                    return
                wait(pe, tokr_ready, t + 1)
                wait(pe, lg_ready, t)
                for k in range(KC):
                    m = mm(bank(6, P, 0, E), lhsT=tokr[:, u, k * P:(k + 1) * P], rhs=wr[:, k, :], start=(k == 0), stop=(k == KC - 1))
                m.then_inc(lg_ps, 1)

            def gnn(t, u, k):
                ha(t, u)
                layer2(t - 1, 1 - u)
                tok_T(t - 3, 1 - u)
                router(t - 4, u)
            tiles(pe, gnn, 6, 3, 4)

            pe.wait_ge(mask_ready, 1)
            mm(bank(0, P, 0, T * E), lhsT=upper[:, :], rhs=both.rearrange("p t e -> p (t e)"), start=True, stop=True)
            mm(bank(1, 128, 0, T * E), lhsT=ones[0:P, :], rhs=both.rearrange("p t e -> p (t e)"), start=True,
               stop=True).then_inc(ranks_ps, 1)

            pe.wait_ge(totals_taken, 1)
            pe.wait_ge(table_ready, 1)
            pe.wait_ge(ew_loaded, 16 * 2 * KC)

            def xs_T(st):
                if not some(st):
                    return
                s, h, nth = st
                wait(pe, xs_loaded[h], nth * 16 + 16)
                wait(pe, xsT_ready, s - 1)
                for k in range(KC):
                    m = pe.transpose(bank(h % 2, 128, k * 128, (k + 1) * 128), xs[:, h, k * 128:(k + 1) * 128], ident[:, :])
                m.then_inc(xs_ps, 1)

            def layer(dst, xt, w, bias_row, col):
                for k in range(KC):
                    mm(dst, lhsT=xt[:, k * 128:(k + 1) * 128], rhs=w[:, k, bass.ds(col, C)], start=(k == 0), stop=False)
                return mm(dst, lhsT=ones3w[:, :], rhs=bias3[:, bias_row:bias_row + E, :].rearrange("p e c -> p (e c)")[:, bass.ds(col, C)],
                          start=False, stop=True)

            def expert_of(st):
                return pe.value_load(exp_i[0:1, bass.ds(st[0], 1)], min_val=0, max_val=(E - 1) * C) if some(st) else None

            def hidden(st, col):
                if not some(st):
                    return
                s, h, nth = st
                wait(pe, xsT_ready, s + 1)
                hold(pe, hg_ready, s - 1)
                layer(bank(2 + h % 2, 128, 0, C), xsT[:, h % 2, :], ew1_s, 4, col).then_inc(eh_ps, 1)

            def hidden_T(st):
                if not some(st):
                    return
                s, h, nth = st
                wait(pe, hg_ready, s + 1)
                wait(pe, hT_ready, s - 1)
                for k in range(KC):
                    m = pe.transpose(bank(4 + h % 2, 128, k * 128, (k + 1) * 128), hg[:, h % 2, k * 128:(k + 1) * 128], ident[:, :])
                m.then_inc(hg_ps, 1)

            def output(st, col):
                if not some(st):
                    return
                s, h, nth = st
                wait(pe, hT_ready, s + 1)
                hold(pe, ys_ready, s - 1)
                layer(bank(6 + h % 2, 128, 0, C), hT[:, h % 2, :], ew2_s, 4 + E, col).then_inc(ey_ps, 1)

            def expert_steps(sts):
                cols = [expert_of(step_at(sts[0], -1)), expert_of(sts[0])]
                for st in sts:
                    xs_T(step_at(st, 2))
                    cols.append(expert_of(step_at(st, 1)))
                    hidden(step_at(st, 1), cols[-1])
                    hidden_T(st)
                    output(step_at(st, -1), cols[-3])
            xs_T((0, 0, 0))
            xs_T((1, 1, 0))
            hidden((0, 0, 0), expert_of((0, 0, 0)))
            steps(pe, expert_steps, SB, 2)

        @block.vector
        def _(v):
            n = [0]

            def link(ins):
                n[0] += 1
                ins.then_inc(dve_step, 1)
                v.wait_ge(dve_step, n[0])

            v.wait_ge(src_loaded, 16)
            v.wait_ge(consts, 17)
            link(v.tensor_copy(src_f[:, :], src_i[:, :]))
            link(v.memset(clast[:, 0:1], 0.0))
            link(v.memset(start[:, 0:1], 0.0))
            link(v.memset(ones_b[:, :], 1.0))
            link(v.tensor_tensor(ge, src_f[:, :].unsqueeze(1).to_broadcast([P, T + 1, ET]),
                                 thr[:, :].unsqueeze(2).to_broadcast([P, T + 1, ET]), ALU.is_ge))
            link(v.tensor_tensor(oneh, ge[:, 0:T, :], ge[:, 1:T + 1, :], ALU.subtract))
            link(v.tensor_tensor_scan(cum.rearrange("p b j -> p (b j)"), ones_b[:, 0:1].to_broadcast([P, T * ET]),
                                      oneh.rearrange("p b j -> p (b j)"), 0.0, ALU.mult, ALU.add))
            link(v.tensor_copy(clast[:, 1:T + 1], cum[:, :, ET - 1]))
            v.tensor_tensor(per_part[:, :], clast[:, 1:T + 1], clast[:, 0:T], ALU.subtract).then_inc(counted, 1)
            v.wait_ge(totals_ps, 1)
            link(v.tensor_scalar(tot_i[:, :], bank(1, 128, 0, T), float(S * GT - 1), None, ALU.add))
            link(v.tensor_scalar(tot_i[:, :], tot_i[:, :], -S * GT, None, ALU.bitwise_and))
            link(v.tensor_copy(padded[:, :], tot_i[:, :]))
            v.tensor_tensor_scan(start[:, 1:T + 1], ones[:, 0:T], padded[:, :], 0.0, ALU.mult, ALU.add).then_inc(starts, 1)
            v.wait_ge(starts, 1)
            link(v.tensor_tensor(base[:, :], bank(0, P, 0, T), clast[:, 0:T], ALU.subtract))
            link(v.scalar_tensor_tensor(base[:, :], base[:, :], -1.0, start[0:P, 0:T], ALU.add, ALU.add))
            for b in range(T):
                v.scalar_tensor_tensor(cum[:, b, :], cum[:, b, :], base[:, b:b + 1], oneh[:, b, :], ALU.add,
                                       ALU.mult).then_inc(dve_step, 1)
                n[0] += 1
            v.wait_ge(dve_step, n[0])
            link(v.tensor_reduce(pos, cum.rearrange("p b j -> p j b"), AX.X, ALU.add))
            link(v.tensor_copy(pos_i, pos))
            link(v.tensor_scalar(slot_t, pos_i, 7, None, ALU.arith_shift_right))
            link(v.tensor_scalar(slot_p, pos_i, S - 1, None, ALU.bitwise_and))
            v.scalar_tensor_tensor(addr[:, :], slot_p, float(ST), slot_t, ALU.mult, ALU.add).then_inc(addr_ready, 1)
            v.wait_ge(starts_ps, 1)
            link(v.tensor_copy(startT[:, :], bank(2, T, 0, 1)))
            v.tensor_scalar(geg[:, :], iota_g[:, :], startT[:, 0:1], None, ALU.is_ge).then_inc(geg_ready, 1)
            v.wait_ge(brow_ps, 1)
            link(v.tensor_tensor(w1a[EA:EA + 1, :], ps[EA:EA + 1, 3 * BANK:3 * BANK + HID], w1a[EA:EA + 1, :], ALU.add))
            link(v.tensor_scalar(temp[:, :], temp[:, :], SC2, None, ALU.mult))
            v.wait_ge(w_loaded, 16 * 15)
            link(v.tensor_tensor(bias_rows[:, :], bias_rows[:, :], bias_more[:, :], ALU.add))
            link(v.tensor_copy(bparts[:, 0, :], bias_rows[:, :]))
            link(v.tensor_tensor(brest[:, :], bias_rows[:, :], bparts[:, 0, :], ALU.subtract))
            link(v.tensor_copy(bparts[:, 1, :], brest[:, :]))
            link(v.tensor_tensor(brest[:, :], brest[:, :], bparts[:, 1, :], ALU.subtract))
            v.tensor_copy(bparts[:, 2, :], brest[:, :]).then_inc(bias_ready, 1)
            link(v.memset(ones3[:, :], 1.0))
            link(v.memset(ones3w[:, :], 1.0))
            v.wait_ge(groups_ps, 1)
            link(v.tensor_scalar(bt[:, :], bank(2, 128, 0, NG), -1.0, None, ALU.add))
            link(v.tensor_scalar(off_f[:, :], bt[0:1, :], float(P), None, ALU.mult))
            for m in range(1, (T - 1) // BPB + 1):
                link(v.tensor_scalar(off_g[:, :], bt[0:1, :], float(BPB * m), float(GAP), ALU.is_ge, ALU.mult))
                link(v.tensor_tensor(off_f[:, :], off_f[:, :], off_g[:, :], ALU.add))
            link(v.tensor_copy(off_i[:, :], off_f[:, :]))
            v.tensor_scalar(bt[:, :], bt[:, :], float(P), None, ALU.mult).then_inc(offs_ready, 1)
            v.wait_ge(offs_ready, 1)

            v.wait_ge(x_loaded, 16)
            for t in range(T):
                v.bn_stats(stats[:, t, :], x_res[:, t, :]).then_inc(dve_step, 1)
                n[0] += 1
            v.wait_ge(dve_step, n[0])
            for t in range(T):
                v.bn_aggr(mv[:, t, :], stats[:, t, :]).then_inc(dve_step, 1)
                n[0] += 1
            v.wait_ge(dve_step, n[0])
            v.tensor_scalar(rstd[:, :], mv[:, :, 1], LN_EPS, None, ALU.add).then_inc(var_ready, 1)
            link(v.memset(vn[:, :, :, :], 0.0))
            link(v.memset(vr[:, :, :, :], 0.0))
            link(v.memset(vn[:, :, :, D:VE], 1.0 / N))
            link(v.memset(last[:, :, :, LF - 1:LF], 1.0))
            v.wait_ge(std_ready, 1)
            link(v.reciprocal(rstd[:, :], rstd[:, :]))

            def xn_of(t, u):
                if not inside(t):
                    return
                wait(v, xT_ps, t - 1)
                v.tensor_scalar(xn[:, u, :], x_res[:, bass.ds(t, 1), :].rearrange("p a c -> p (a c)"),
                                mv[:, bass.ds(t, 1), 0:1].rearrange("p a b -> p (a b)"), rstd[:, bass.ds(t, 1)],
                                ALU.subtract, ALU.mult).then_inc(xn_ready, 1)

            def heads(ap, w):
                return ap.rearrange("p (h d) -> p h d", h=H) if w is None else ap.unsqueeze(2).to_broadcast([P, H, w])

            def keys(t, u):
                if not inside(t):
                    return
                kb = heads(bank(1 + u, P, 0, C), None)
                wait(v, kdup_ready, t + 1)
                wait(v, vn_ready, t + 1)
                wait(v, m_added, t - 1)
                v.tensor_tensor(phi[:, u], kb.unsqueeze(2).to_broadcast([P, H, OFF, D]), overlapped(kdup, u, 0, H),
                                ALU.mult).then_inc(phi_ready, 1)
                wait(v, phi_ready, t + 1)
                v.tensor_reduce(ssq[:, u, :], phi[:, u, :, 0, :], AX.X, ALU.add).then_inc(ssq_ready, 1)
                wait(v, ssq_ready, t + 1)
                v.tensor_scalar(nm[:, u, :], ssq[:, u, :], EPS2, 1.0 / SC2, ALU.max, ALU.mult).then_inc(nm_ready, 1)
                wait(v, nm_ready, t + 1)
                v.reciprocal(r2[:, u, :], nm[:, u, :]).then_inc(rk2_ready, 1)
                wait(v, rk2_ready, t + 1)
                v.tensor_tensor(vr[:, u, :, 0:VE], vn[:, u, :, 0:VE], heads(r2[:, u, :], VE), ALU.mult).then_inc(vr_ready, 1)
                wait(v, rk_ready, t + 1)
                v.tensor_tensor(last[:, u, :, 16:16 + D], kb, heads(rr[:, u, :], D), ALU.mult).then_inc(kn_ready, 1)
                wait(v, kn_ready, t + 1)
                v.tensor_tensor(last[:, u, :, 0:16], last[:, u, :, 16:32], last[:, u, :, 32:48], ALU.mult).then_inc(last_ready, 1)

            def pass1(t, u, k):
                xn_of(t + 1, 1 - u)
                keys(t - 1, 1 - u)
            xn_of(0, 0)
            tiles(v, pass1, 3, 1, 1)

            v.wait_ge(m_added, T)
            for g in range(H // 2):
                v.tensor_copy(phi_m[:, g, :], bank(4 + g)).then_inc(m_copied, 1)
            for g in range(H // 2):
                v.wait_ge(mT_ps, g + 1)
                v.tensor_scalar(mq[:, g, 0, :], bank(g % 2, 128, 0, 128), sq_half[:, 0:1], None, ALU.mult)
                v.tensor_copy(mq[:, g, 1:QC, :], bank(g % 2, 128, 128, QC * 128).rearrange("p (c e) -> p c e", c=QC - 1)).then_inc(mT_taken, 1)
            link(v.memset(ml, 0.0))
            v.tensor_tensor(ml.rearrange("p g (a e) -> p g a e", a=2)[:, :, :, 0:VE],
                            bank(3, 2 * LF, 0, H * VE).rearrange("p (g a e) -> p g a e", g=H // 2, a=2),
                            mask[:, :].rearrange("p (a e) -> p a e", a=2).unsqueeze(1).to_broadcast([2 * LF, H // 2, 2, VE]),
                            ALU.mult).then_inc(m_ready, 1)
            v.wait_ge(m_ready, 1)

            def xr(t, u):
                if not inside(t):
                    return
                hold(v, q_ps, t - 1)
                v.tensor_copy(xT[:, u, :, :], xT_all[:, :, bass.ds(t * P, P)]).then_inc(xr_ready, 1)

            def norm_a(t, u):
                if not inside(t):
                    return
                wait(v, qsq_ready, t + 1)
                v.tensor_reduce(ssq[:, u, :], heads(sqs[:, u, :], None), AX.X, ALU.add).then_inc(qssq_ready, 1)
                wait(v, qssq_ready, t + 1)
                v.tensor_scalar(nm[:, u, :], ssq[:, u, :], SC2, EPS2, ALU.mult, ALU.max).then_inc(qnm_ready, 1)
                wait(v, qnm_ready, t + 1)
                v.reciprocal(r2[:, u, :], nm[:, u, :]).then_inc(qinv_ready, 1)

            def norm_b(t, u):
                if not inside(t):
                    return
                wait(v, qroot_ready, t + 1)
                v.tensor_tensor(rq[:, u, :], rr[:, u, :], temp[:, :], ALU.mult).then_inc(rq_ready, 1)
                wait(v, rq_ready, t + 1)
                qb = heads(bank((0, 6)[u], P, 0, C), None)
                v.tensor_tensor(qb, qb, heads(rq[:, u, :], D), ALU.mult).then_inc(qn_ready, 1)

            def products(t, u, g):
                if not inside(t):
                    return
                qb = heads(bank((0, 6)[u], P, 0, C), None)
                if g == 0:
                    wait(v, qdup_ready, t + 1)
                    wait(v, grp_ps[0], (t - 2) * (NJ // 2) + (H // 2 + 1))
                hh = slice(g * H // 2, (g + 1) * H // 2)
                v.tensor_tensor(phi[:, u, hh], qb[:, hh].unsqueeze(2).to_broadcast([P, H // 2, OFF, D]),
                                overlapped(kdup, u, g * H // 2, H // 2), ALU.mult).then_inc(qphi_ready[g], 1)

            def pairs(t, u):
                if not inside(t):
                    return
                wait(v, qlin_ready, t + 1)
                v.tensor_tensor(last[:, u, :, 0:16], last[:, u, :, 16:32], last[:, u, :, 32:48], ALU.mult).then_inc(qlast_ready, 1)

            def x1(t, u):
                if not inside(t):
                    return
                wait(v, proj_ps, t + 1)
                xv = x_res[:, bass.ds(t, 1), :].rearrange("p a c -> p (a c)")
                v.tensor_tensor(xv, bank(7, P, 256, 256 + C), xv, ALU.add).then_inc(x1_ready, 1)

            def normalise(t, u):
                if not inside(t):
                    return
                wait(v, y_ps, t + 1)
                yv = bank(5, P).rearrange("p (h e) -> p h e", h=H)
                v.reciprocal(ry[:, u, :], yv[:, :, D:VE].rearrange("p h e -> p (h e)")).then_inc(ry_ready, 1)
                wait(v, ry_ready, t + 1)
                wait(v, attnT_ps, t - 1)
                v.tensor_tensor(heads(attn[:, u, :], None), yv[:, :, 0:D], heads(ry[:, u, :], D), ALU.mult).then_inc(attn_ready, 1)

            def pass2(t, u, k):
                products(t + 1, 1 - u, 0)
                x1(t - 2, u)
                normalise(t - 1, 1 - u)
                norm_a(t + 2, u)
                products(t + 1, 1 - u, 1)
                norm_b(t + 2, u)
                pairs(t + 1, 1 - u)
                xr(t + 3, 1 - u)
            for t in range(3):
                xr(t, t % 2)
            for t in range(2):
                norm_a(t, t)
                norm_b(t, t)
            products(0, 0, 0)
            products(0, 0, 1)
            pairs(0, 0)
            tiles(v, pass2, 4, 3, 2)

            def onehots(c, h, o, nth):
                wait(v, rows_loaded[h], nth * 16)
                wait(v, rows_used, c - 1)
                v.tensor_tensor(key[:, o, :].rearrange("p (g k) -> p g k", g=RG),
                                srt[:, h, :, EA + 1].rearrange("p (g k) -> p g k", g=RG),
                                bt[:, bass.ds(c * RG, RG)].unsqueeze(2).to_broadcast([128, RG, GT]),
                                ALU.subtract).then_inc(key_ready, 1)
                hold(v, key_ready, c + 1)
                v.tensor_tensor(oh[:, o, :, :], iota_c[:, :].unsqueeze(1).to_broadcast([128, RT, P]),
                                key[:, o, :].unsqueeze(2).to_broadcast([128, RT, P]), ALU.is_equal).then_inc(onehot_ready, 1)
            for c in range(3):
                onehots(c, c, c % 2, 1)
            with v.Fori(0, (NR - 3) // RB) as i:
                for k in range(RB):
                    onehots(i * RB + (3 + k), (3 + k) % RB, (3 + k) % 2, i + (3 + k) // RB + 1)
            v.wait_ge(rows_used, NR)

            for b in range(NBK):
                nb = min(BPB, T - b * BPB) * P
                v.tensor_copy(aggT[0:EA, b * BPB * P:b * BPB * P + nb], bank(b, EA, 0, nb)).then_inc(sums_copied, 1)
            v.wait_ge(cnt_ps, 1)
            link(v.tensor_scalar(cmax, bank(7, P, 0, T), 1.0, None, ALU.max))
            link(v.reciprocal(cinv, cmax))
            v.sem_inc(inv_ready)
            for b in range(NBK):
                nb = min(BPB, T - b * BPB) * P
                v.wait_ge(inv_ps, b + 1)
                v.wait_ge(sums_copied, b + 1)
                v.tensor_tensor(aggT[0:EA, b * BPB * P:b * BPB * P + nb], bank((b - 1) % 8, EA, 0, nb),
                                aggT[0:EA, b * BPB * P:b * BPB * P + nb], ALU.mult).then_inc(mean_ready, 1)

            def hsum(t, u, k):
                if not inside(t):
                    return
                wait(v, ha_ps, t + 1)
                wait(v, hpre_back[u], k * 16 + 16)
                wait(v, gnn_ps, t - 1)
                v.tensor_tensor(hs[:, u, :], bank(1 + u, 128, 0, MC * P), hpre2[:, u, :], ALU.add).then_inc(hsum_ready, 1)

            def x2_of(t, u):
                if not inside(t):
                    return
                wait(v, gnn_ps, t + 1)
                wait(v, res_ready, t - 1)
                v.tensor_tensor(x2[:, u, :], bank(3 + u, P, 0, C), x_res[:, bass.ds(t, 1), :].rearrange("p a c -> p (a c)"),
                                ALU.add).then_inc(x2_ready, 1)
                wait(v, x2_ready, t + 1)
                v.bn_stats(st2[:, u, :], x2[:, u, :]).then_inc(st2_ready, 1)
                hold(v, st2_ready, t + 1)
                v.bn_aggr(mv2[:, u, :], st2[:, u, :]).then_inc(mv2_ready, 1)
                wait(v, mv2_ready, t + 1)
                v.tensor_scalar(sd2[:, u, :], mv2[:, u, 1:2], LN_EPS, None, ALU.add).then_inc(ve2_ready, 1)

            def xl_of(t, u):
                if not inside(t):
                    return
                wait(v, sd2_ready, t + 1)
                v.reciprocal(rs2[:, u, :], sd2[:, u, :]).then_inc(rs2_ready, 1)
                wait(v, rs2_ready, t + 1)
                wait(v, tok_ps, t - 1)
                wait(v, xl_kept, t - 1)
                v.tensor_scalar(xl[:, u, :], x2[:, u, :], mv2[:, u, 0:1], rs2[:, u, :], ALU.subtract, ALU.mult).then_inc(xl_ready, 1)

            def lg_of(t, u):
                if not inside(t):
                    return
                hold(v, lg_ps, t + 1)
                v.tensor_copy(lg[:, bass.ds(t, 1), :].rearrange("p a c -> p (a c)"), bank(6, P, 0, E)).then_inc(lg_ready, 1)

            def gnn(t, u, k):
                hsum(t, u, k)
                x2_of(t - 1, 1 - u)
                xl_of(t - 2, u)
                lg_of(t - 4, u)
            tiles(v, gnn, 6, 3, 4)

            def wide(a):
                return a.unsqueeze(2).to_broadcast([P, T, E])

            v.wait_ge(lg_ready, T)
            link(v.tensor_reduce(red, lg, AX.X, ALU.max))
            v.tensor_tensor(pr, lg, wide(red), ALU.subtract).then_inc(sh_ready, 1)
            v.wait_ge(ex_ready, 1)
            link(v.tensor_reduce(red, pr, AX.X, ALU.add))
            link(v.reciprocal(red, red))
            link(v.tensor_tensor(pr, pr, wide(red), ALU.mult))
            link(v.tensor_copy(pw, pr))
            for m in range(2):
                best = top[:, m, :]
                eq = (first, second)[m]
                link(v.tensor_reduce(best, pw, AX.X, ALU.max))
                link(v.tensor_tensor(eq, pw, wide(best), ALU.is_equal))
                link(v.scalar_tensor_tensor(pick, rank8[:, :].unsqueeze(1).to_broadcast([P, T, E]), float(E), eq, ALU.add, ALU.mult))
                link(v.tensor_reduce(red, pick, AX.X, ALU.max))
                link(v.tensor_tensor(eq, pick, wide(red), ALU.is_equal))
                if m == 0:
                    link(v.scalar_tensor_tensor(pw, eq, -2.0, pw, ALU.mult, ALU.add))
            v.tensor_tensor(both, first, second, ALU.add).then_inc(mask_ready, 1)
            link(v.tensor_tensor(red, top[:, 0, :], top[:, 1, :], ALU.add))
            link(v.tensor_scalar(red, red, 1e-12, None, ALU.max))
            link(v.reciprocal(red, red))
            link(v.tensor_tensor(top, top, red.unsqueeze(1).to_broadcast([P, 2, T]), ALU.mult))
            link(v.memset(keep, 1.0))
            link(v.memset(keep[:, :, 0:1], 0.0))
            v.wait_ge(ranks_ps, 1)
            link(v.tensor_copy(tot, bank(1, 128, 0, T * E).rearrange("p (t e) -> p e t", e=E)))
            link(v.tensor_tensor_scan(cumt.rearrange("p e t -> p (e t)"), keep.rearrange("p e t -> p (e t)"),
                                      tot.rearrange("p e t -> p (e t)"), 0.0, ALU.mult, ALU.add))
            link(v.tensor_tensor(e_n, reg_fill[:, :], cumt[:, :, T - 1], ALU.add))
            v.tensor_copy(pad_idx[:, :], e_n).then_inc(pads_ready, 1)
            link(v.tensor_tensor(slot, bank(0, P, 0, T * E).rearrange("p (t e) -> p t e", e=E),
                                 cumt[0:P].rearrange("p e t -> p t e"), ALU.add))
            link(v.tensor_tensor(slot, slot, tot[0:P].rearrange("p e t -> p t e"), ALU.subtract))
            link(v.tensor_tensor(slot, slot, reg_start[:, :].unsqueeze(1).to_broadcast([P, T, E]), ALU.add))
            v.sem_inc(totals_taken)
            for m in range(2):
                link(v.tensor_tensor(pick, slot, (first, second)[m], ALU.mult))
                link(v.tensor_reduce(red, pick, AX.X, ALU.add))
                link(v.tensor_copy(row_idx[:, m, :], red))
            link(v.tensor_copy(xl_all[:, :, C], top[:, 0, :]))
            v.tensor_copy(xl_all[:, :, C + 1], dst_row[:, :]).then_inc(meta_ready, 1)
            link(v.tensor_scalar(e_i, cumt[:, :, T - 1], 127.0, None, ALU.add))
            link(v.tensor_scalar(e_i, e_i, -128, None, ALU.bitwise_and))
            link(v.tensor_copy(e_pad, e_i[0:1, :]))
            link(v.tensor_tensor_scan(e_end, ones[0:1, 0:E], e_pad, 0.0, ALU.mult, ALU.add))
            link(v.tensor_tensor(past, step_row[:, :].unsqueeze(2).to_broadcast([1, NS, E]),
                                 e_end.unsqueeze(1).to_broadcast([1, NS, E]), ALU.is_ge))
            link(v.tensor_reduce(exp_f, past, AX.X, ALU.add))
            link(v.tensor_tensor(pasts, past, e_pad.unsqueeze(1).to_broadcast([1, NS, E]), ALU.mult))
            link(v.tensor_reduce(row_f, pasts, AX.X, ALU.add))
            link(v.tensor_tensor(row_f, step_row[:, :], row_f, ALU.subtract))
            link(v.scalar_tensor_tensor(row_f, exp_f, float(REG), row_f, ALU.mult, ALU.add))
            link(v.tensor_scalar(row_f, row_f, float(E * REG), None, ALU.min))
            link(v.tensor_copy(row_i[:, :], row_f))
            link(v.tensor_scalar(exp_f, exp_f, float(E - 1), float(C), ALU.min, ALU.mult))
            v.tensor_copy(exp_i[:, :], exp_f).then_inc(table_ready, 1)
            v.wait_ge(routed_rows[0], 16 * T)
            link(v.tensor_copy(xl_all[:, :, C], top[:, 1, :]))
            v.tensor_scalar(xl_all[:, :, C + 1], dst_row[:, :], float(N), None, ALU.add).then_inc(meta2_ready, 1)

            def hT_copy(st):
                if not some(st):
                    return
                s, h, nth = st
                wait(v, hg_ps, s + 1)
                wait(v, ey_ps, s - 1)
                v.tensor_copy(hT[:, h % 2, :], bank(4 + h % 2, 128, 0, C)).then_inc(hT_ready, 1)

            def output_rows(st):
                if not some(st):
                    return
                s, h, nth = st
                wait(v, xs_loaded[h], nth * 16 + 16)
                wait(v, ys_stored[h], nth * 16)
                v.tensor_copy(y_idx[:, h:h + 1], xs[:, h, C + 1:XF]).then_inc(idx_ready, 1)

            def weigh(st):
                if not some(st):
                    return
                s, h, nth = st
                wait(v, ey_ps, s + 1)
                wait(v, ys_stored[h], nth * 16)
                v.tensor_scalar(ys[:, h, :], bank(6 + h % 2, 128, 0, C), xs[:, h, C:C + 1], None, ALU.mult).then_inc(ys_ready, 1)

            def expert_steps(sts):
                for st in sts:
                    hT_copy(st)
                    output_rows(st)
                    weigh(step_at(st, -1))
            steps(v, expert_steps, SB, 2)

            v.wait_ge(res_ready, T)
            for g in range(T // FT):
                xv = x_res[:, g * FT:(g + 1) * FT, :]
                v.wait_ge(yb_loaded[g % 2], 32 * (g // 2 + 1))
                link(v.tensor_tensor(xv, xv, yb[:, g % 2, 0, :, :], ALU.add))
                v.tensor_tensor(xv, xv, yb[:, g % 2, 1, :, :], ALU.add).then_inc(yb_added, 1)


def kernel(**inputs):
    import numpy as _np
    import concourse.bacc as _bacc
    from concourse import mybir as _mybir
    from concourse.bass_utils import run_bass_kernel_spmd as _run

    f = {k: _np.asarray(a) for k, a in inputs.items()}
    laid = [
        ("x", f["x"]), ("src", f["src"]), ("edge_attr", f["edge_attr_64"]), ("u", f["L0_gnn_u"]),
        ("W1", f["L0_gnn_W1"]), ("b1", f["L0_gnn_b1"]), ("W2", f["L0_gnn_W2"]), ("b2", f["L0_gnn_b2"]),
        ("WqkvT", f["L0_mix_Wqkv"].T), ("bqkv", f["L0_mix_bqkv"]), ("WprojT", f["L0_mix_Wproj"].T),
        ("bproj", f["L0_mix_bproj"]), ("temperature", f["L0_mix_temperature"].reshape(-1)),
        ("routerT", f["L0_ffn_router_w"].T), ("ew1", f["L0_ffn_w1"]), ("eb1", f["L0_ffn_b1"]),
        ("ew2", f["L0_ffn_w2"]), ("eb2", f["L0_ffn_b2"]),
    ]
    nc = _bacc.Bacc("TRN2", target_bir_lowering=False, num_devices=1)
    arrays, args = {}, []
    for name, a in laid:
        a = _np.ascontiguousarray(a)
        arrays[f"in_{name}"] = a
        args.append(nc.dram_tensor(f"in_{name}", a.shape, _mybir.dt.from_np(a.dtype), kind="ExternalInput").ap())
    args.append(nc.dram_tensor("out_x", f["x"].shape, _mybir.dt.float32, kind="ExternalOutput").ap())
    gps_layer(nc, *args)
    r = _run(nc, [arrays], core_ids=[0])
    return r.results[0]["out_x"]
```

```python
import concourse.bass as bass
from concourse import mybir
from contextlib import ExitStack

fp32 = mybir.dt.float32
bf16 = mybir.dt.bfloat16
i32 = mybir.dt.int32
u32 = mybir.dt.uint32
ALU = mybir.AluOpType
ACT = mybir.ActivationFunctionType
AX = mybir.AxisListType


def gps_layer(nc, x, src, edge_attr, u_in, W1, b1, W2, b2, WqkvT, bqkv, WprojT, bproj, temperature,
              routerT, ew1, eb1, ew2, eb2, out):
    N, C = x.shape
    P = 125
    T = N // P
    EA = edge_attr.shape[1]
    ET = src.shape[0] // P
    HID = W1.shape[1]
    MC = HID // 128
    KC = C // 128
    H = temperature.shape[0]
    D = C // H
    E = ew1.shape[0]
    OFF = 16
    QC = OFF * D // 128
    LF = 16 + D + 1
    VE = D + 1
    VW = 64
    S = 128
    GT = 4
    NG = (src.shape[0] + T * (GT * S - 1)) // (GT * S) + 1
    NG += -NG % 3
    ST = NG * GT
    RT = 12
    RG = RT // GT
    NR = ST // RT
    RB = 4
    SB = 6
    REG = N + 128
    NS = 2 * N // 128 + E
    BATCHES = ((0, 8), (8, 16), (16, T))
    XF = C + 2
    F = EA + 2
    BPB = 4
    NBK = (T - 1) // BPB + 1
    CH = 17
    NCH = ET // CH
    BANK = 512
    LN_EPS = 1e-5
    EPS2 = 1e-24
    SC = float(D) ** 0.25
    SC2, SC4 = SC * SC, SC ** 4
    GAP = BANK - BPB * P
    assert NR % RB == 3 and NCH % 2 == 1 and T == 25

    ctx = ExitStack()
    with ctx:
        def sb(name, shape, dt=fp32):
            return ctx.enter_context(nc.sbuf_tensor(name, shape, dt))

        def sem(name):
            return ctx.enter_context(nc.semaphore(name))

        sorted_rows = nc.dram_tensor("sorted_rows", (S * ST, F), fp32, kind="Internal").ap()
        hpre_dram = nc.dram_tensor("hpre_rows", (T * 128, MC * P), fp32, kind="Internal").ap()
        routed = nc.dram_tensor("routed_rows", (E * REG + 128, XF), fp32, kind="Internal").ap()
        youts = nc.dram_tensor("expert_outputs", (2 * N, C), fp32, kind="Internal").ap()
        sorted_v = sorted_rows.rearrange("(p t) f -> p t f", p=S)

        x_res = sb("x_res", [P, T, C])
        stage = sb("stage", [P, 2, CH, F])
        idx = sb("idx", [P, 2, CH], u32)
        src_f = sb("src_f", [P, ET])
        addr = sb("addr", [P, ET], u32)
        zeros = sb("zeros", [128, RT * F])
        ones = sb("ones", [128, 128])
        ones_b = sb("ones_b", [P, 1], bf16)
        ident = sb("ident", [128, 128])
        upper = sb("upper", [P, P])
        iota_c = sb("iota_c", [128, P])
        wqkv = sb("wqkv", [128, KC, 3 * C])
        w1x = sb("w1x", [128, KC, HID])
        w1u = sb("w1u", [128, HID])
        w1a = sb("w1a", [EA + 1, HID])
        w2s = sb("w2s", [128, MC, C])
        wproj = sb("wproj", [128, KC, C])
        wr = sb("wr", [128, KC, E])
        NBR = 4 + 2 * E
        bias_rows = sb("bias_rows", [NBR, C])
        bias_more = sb("bias_more", [NBR, C])
        u0 = sb("u0", [128, 1])
        temp = sb("temp", [P, H])
        x_sum = sb("x_sum", [P, T])
        neg_mean = sb("neg_mean", [P, T])
        rstd = sb("rstd", [P, T])
        mask = sb("mask", [2 * LF, 2 * VE])
        sq_half = sb("sq_half", [128, 1])
        bt = sb("bt", [128, NG])
        bias3 = sb("bias3", [3, NBR, C], bf16)
        ones3 = sb("ones3", [3, P], bf16)
        bparts = sb("bparts", [NBR, 3, C], bf16)
        brest = sb("brest", [NBR, C])
        ones3w = sb("ones3w", [3, 128], bf16)
        dst_row = sb("dst_row", [P, T])
        reg_start = sb("reg_start", [128, E])
        reg_part = sb("reg_part", [128, E])
        step_row = sb("step_row", [1, NS])
        pad_rows = sb("pad_rows", [128, XF])
        pad_idx = sb("pad_idx", [128, E], u32)
        row_idx = sb("row_idx", [P, 2, T], u32)
        exp_i = sb("exp_i", [1, NS], i32)
        row_i = sb("row_i", [1, NS], i32)
        off_i = sb("off_i", [1, NG], i32)

        r1 = sb("r1", [128, 17700])
        r1_off = [0]

        def carve(shape, dt=fp32, parts=None, at=None):
            n = 1
            for s in shape[1:]:
                n *= s
            words = (n + 1) // 2 if dt == bf16 else n
            o = r1_off[0] if at is None else at
            if at is None:
                r1_off[0] += words
            assert o + words <= 17700, o + words
            v = r1[0:shape[0], o:o + words]
            if dt != fp32:
                v = v.bitcast(dt)
                if dt == bf16:
                    v = v[:, 0:n]
            if len(shape) == 3:
                v = v.rearrange("p (a b) -> p a b", a=shape[1])
            elif len(shape) == 4:
                v = v.rearrange("p (a b c) -> p a b c", a=shape[1], b=shape[2])
            elif len(shape) == 5:
                v = v.rearrange("p (a b c d) -> p a b c d", a=shape[1], b=shape[2], c=shape[3])
            return v

        cum = carve([P, T, ET])
        ge = carve([P, T + 1, ET], bf16, at=0)
        oneh = carve([P, T, ET], bf16)
        pos = carve([P, ET])
        pos_i = carve([P, ET], i32)
        slot_t = carve([P, ET], i32)
        slot_p = carve([P, ET], i32)
        src_i = sb("src_i", [P, ET], i32)
        thr = sb("thr", [P, T + 1])
        iota_g = sb("iota_g", [T, NG])
        clast = sb("clast", [P, T + 1])
        per_part = sb("per_part", [P, T])
        tot_i = sb("tot_i", [128, T], i32)
        padded = sb("padded", [128, T])
        start = sb("start", [128, T + 1])
        base = sb("base", [P, T])
        startT = sb("startT", [T, 1])
        geg = sb("geg", [T, NG])
        off_f = sb("off_f", [1, NG])
        off_g = sb("off_g", [1, NG])
        r1_off[0] = 0
        xT_all = carve([128, KC, T * P])
        hpre = carve([128, 2, MC * P])
        after_q = r1_off[0]
        xn = carve([P, 2, C])
        vn = carve([P, 2, H, VW])
        vr = carve([P, 2, H, VW])
        first_only = r1_off[0]
        r1_off[0] = after_q
        phT = carve([128, 2, QC * P])
        yT = carve([128, (H // 2) * P])
        sqs = carve([P, 2, C])
        attn = carve([P, 2, C])
        r1_off[0] = max(first_only, r1_off[0])
        xT = carve([128, 2, KC, P])
        kdup = carve([P, 2, H, 2 * D])
        last = carve([P, 2, H, LF])
        mq = carve([128, H // 2, QC, 2 * VW])
        ml = carve([2 * LF, H // 2, 2 * VW])
        attnT = carve([128, 2, KC, P])
        ssq = carve([P, 2, H])
        nm = carve([P, 2, H])
        r2 = carve([P, 2, H])
        rr = carve([P, 2, H])
        rq = carve([P, 2, H])
        ry = carve([P, 2, H])
        r1_off[0] = 0
        xl_all = carve([P, T, XF])
        hpre2 = carve([128, 2, MC * P])
        after_xl = r1_off[0]
        aggT = carve([EA + 1, T * P])
        cnt = carve([EA + 1, T * P], at=0)
        cinv = carve([P, T])
        cmax = carve([P, T])
        hs = carve([128, 2, MC * P])
        x2 = carve([P, 2, C])
        xl = carve([P, 2, C])
        tokr = carve([128, 2, KC * P])
        st2 = carve([P, 2, 6])
        mv2 = carve([P, 2, 2])
        sd2 = carve([P, 2, 1])
        rs2 = carve([P, 2, 1])
        lg = carve([P, T, E])
        pr = carve([P, T, E])
        pw = carve([P, T, E])
        pick = carve([P, T, E])
        slot = carve([P, T, E])
        most = max(t1 - t0 for t0, t1 in BATCHES)
        tot_b = carve([128, E * most])
        cumt_b = carve([128, E * most])
        keeps = {n_: carve([128, E, n_]) for n_ in sorted({t1 - t0 for t0, t1 in BATCHES})}
        carry = carve([128, E])
        meta = carve([P, 2, T, 2])
        first = carve([P, T, E])
        second = carve([P, T, E])
        both = carve([P, T, E])
        top = carve([P, 2, T])
        red = carve([P, T])
        e_n = carve([128, E])
        e_i = carve([128, E], i32)
        e_pad = carve([1, E])
        e_end = carve([1, E])
        past = carve([1, NS, E])
        pasts = carve([1, NS, E])
        exp_f = carve([1, NS])
        row_f = carve([1, NS])
        r1_off[0] = after_xl
        xs = carve([128, SB, XF])
        xsT = carve([128, 2, C])
        hg = carve([128, 2, C])
        hT = carve([128, 2, C])
        ys = carve([128, SB, C])
        y_idx = carve([128, SB], u32)
        FT = 5
        yb = carve([P, 2, 2, FT, C])
        rank8 = sb("rank8", [P, E])

        NW = E * KC * C
        r2t = sb("r2t", [128, 2 * NW])
        x_dev = r2t[0:P, 0:T * C].rearrange("p (t c) -> p t c", t=T)
        phi_m = r2t[:, 0:(H // 2) * QC * 128].rearrange("p (g n) -> p g n", g=H // 2)
        phi = r2t[0:P, 0:2 * H * OFF * D].rearrange("p (u h o d) -> p u h o d", u=2, h=H, o=OFF)
        srt = r2t[:, 0:RB * RT * F].rearrange("p (u t f) -> p u t f", u=RB, t=RT)
        o1 = RB * RT * F
        oh = r2t[:, o1:o1 + 2 * RT * P].rearrange("p (u t c) -> p u t c", u=2, t=RT)
        key = sb("key", [128, 2, RT])
        ew1_s = r2t[:, 0:NW].rearrange("p (k n) -> p k n", k=KC)
        ew2_s = r2t[:, NW:2 * NW].rearrange("p (k n) -> p k n", k=KC)

        ps = ctx.enter_context(nc.psum_tensor("ps", [128, 8 * BANK], fp32))

        def bank(b, parts=128, a=0, z=BANK):
            return ps[0:parts, b * BANK + a:b * BANK + z]

        gate = sem("gate")
        src_loaded = sem("src_loaded")
        x_loaded = sem("x_loaded")
        w_loaded = sem("w_loaded")
        consts = sem("consts")
        zero_filled = sem("zero_filled")
        dve_step = sem("dve_step")
        pool_step = sem("pool_step")
        bias_zeroed = sem("bias_zeroed")
        bias_ready = sem("bias_ready")
        bias_spread = sem("bias_spread")
        brow_ps = sem("brow_ps")
        counted = sem("counted")
        totals_ps = sem("totals_ps")
        starts = sem("starts")
        starts_ps = sem("starts_ps")
        geg_ready = sem("geg_ready")
        groups_ps = sem("groups_ps")
        addr_ready = sem("addr_ready")
        offs_ready = sem("offs_ready")
        x_stats = sem("x_stats")
        mix_init = sem("mix_init")
        groups_read = sem("groups_read")
        var_ready = sem("var_ready")
        std_ready = sem("std_ready")
        chunk_loaded = [sem(f"chunk_loaded{h}") for h in range(2)]
        chunk_keyed = sem("chunk_keyed")
        scattered = [sem(f"scattered{h}") for h in range(2)]
        m_zeroed = sem("m_zeroed")
        xn_ready = sem("xn_ready")
        xT_ps = sem("xT_ps")
        xT_ready = sem("xT_ready")
        xT_kept = sem("xT_kept")
        kv_ps = sem("kv_ps")
        kdup_ready = sem("kdup_ready")
        vn_ready = sem("vn_ready")
        ksq_ready = sem("ksq_ready")
        phi_ready = sem("phi_ready")
        ssq_ready = sem("ssq_ready")
        nm_ready = sem("nm_ready")
        rk2_ready = sem("rk2_ready")
        rk_ready = sem("rk_ready")
        vr_ready = sem("vr_ready")
        kn_ready = sem("kn_ready")
        last_ready = sem("last_ready")
        m_added = sem("m_added")
        m_copied = sem("m_copied")
        mT_ps = sem("mT_ps")
        mT_taken = sem("mT_taken")
        m_ready = sem("m_ready")
        hpre_stored = [sem(f"hpre_stored{h}") for h in range(2)]
        xr_ready = sem("xr_ready")
        q_ps = sem("q_ps")
        qsq_ready = sem("qsq_ready")
        qssq_ready = sem("qssq_ready")
        qnm_ready = sem("qnm_ready")
        qinv_ready = sem("qinv_ready")
        qroot_ready = sem("qroot_ready")
        rq_ready = sem("rq_ready")
        qdup_ready = sem("qdup_ready")
        qlin_ready = sem("qlin_ready")
        qphi_ready = [sem(f"qphi_ready{h}") for h in range(2)]
        qlast_ready = sem("qlast_ready")
        NJ = H + 2
        grp_ps = [sem(f"grp_ps{j}") for j in range(2)]
        grp_ready = [sem(f"grp_ready{j}") for j in range(2)]
        y_added = [sem(f"y_added{j}") for j in range(2)]
        yT_ready = sem("yT_ready")
        y_ps = sem("y_ps")
        ry_ready = sem("ry_ready")
        attn_ready = sem("attn_ready")
        attnT_ps = sem("attnT_ps")
        attnT_ready = sem("attnT_ready")
        proj_ps = sem("proj_ps")
        x1_ready = sem("x1_ready")
        acc_zeroed = sem("acc_zeroed")
        rows_loaded = [sem(f"rows_loaded{h}") for h in range(RB)]
        key_ready = sem("key_ready")
        onehot_ready = sem("onehot_ready")
        rows_used = sem("rows_used")
        cnt_copied = sem("cnt_copied")
        cnt_ps = sem("cnt_ps")
        sums_copied = sem("sums_copied")
        inv_ready = sem("inv_ready")
        inv_ps = sem("inv_ps")
        mean_ready = sem("mean_ready")
        agg_one = sem("agg_one")
        ew_loaded = sem("ew_loaded")
        hpre_back = [sem(f"hpre_back{h}") for h in range(2)]
        ha_ps = sem("ha_ps")
        hsum_ready = sem("hsum_ready")
        hs_ready = sem("hs_ready")
        gnn_ps = sem("gnn_ps")
        x2_ready = sem("x2_ready")
        st2_ready = sem("st2_ready")
        mv2_ready = sem("mv2_ready")
        ve2_ready = sem("ve2_ready")
        sd2_ready = sem("sd2_ready")
        rs2_ready = sem("rs2_ready")
        xl_ready = sem("xl_ready")
        xl_kept = sem("xl_kept")
        res_ready = sem("res_ready")
        tok_ps = sem("tok_ps")
        tokr_ready = sem("tokr_ready")
        lg_ps = sem("lg_ps")
        lg_ready = sem("lg_ready")
        sh_ready = sem("sh_ready")
        ex_ready = sem("ex_ready")
        mask_ready = sem("mask_ready")
        ranks_ps = sem("ranks_ps")
        meta_ready = sem("meta_ready")
        meta_put = sem("meta_put")
        pads_ready = sem("pads_ready")
        table_ready = sem("table_ready")
        routed_rows = [sem(f"routed_rows{c}") for c in range(3)]
        spare_filled = sem("spare_filled")
        xs_loaded = [sem(f"xs_loaded{h}") for h in range(SB)]
        xs_ps = sem("xs_ps")
        xsT_ready = sem("xsT_ready")
        eh_ps = sem("eh_ps")
        hg_ready = sem("hg_ready")
        hg_ps = sem("hg_ps")
        hT_ready = sem("hT_ready")
        ey_ps = sem("ey_ps")
        ys_ready = sem("ys_ready")
        idx_ready = sem("idx_ready")
        ys_stored = [sem(f"ys_stored{h}") for h in range(SB)]
        yb_loaded = [sem(f"yb_loaded{g}") for g in range(T // FT)]
        yb_added = sem("yb_added")
        stored = sem("stored")

        block = ctx.enter_context(nc.Block())

        def wait(eng, s, n):
            if not (isinstance(n, int) and n <= 0):
                eng.wait_ge(s, n)

        def hold(eng, s, n):
            if not (isinstance(n, int) and n <= 0):
                eng.wait_ge(s, n)
                eng.sem_inc(gate)

        def tiles(eng, body, lo, ahead, behind, between=()):
            hi = T - ahead
            end = lo + (hi - lo) // 2 * 2
            between = dict(between)
            cuts = [lo] + [t for t in sorted(between) if lo < t < end] + [end]
            for t in range(lo):
                body(t, t % 2, t // 2)
            for a, z in zip(cuts, cuts[1:]):
                if a in between:
                    between[a]()
                assert (z - a) % 2 == 0
                with eng.Fori(0, (z - a) // 2) as i:
                    for k in range(2):
                        body(i * 2 + (a + k), (a + k) % 2, i + (a + k) // 2)
            for t in range(end, T + behind):
                if t in between:
                    between[t]()
                body(t, t % 2, t // 2)

        def outputs_of(g):
            if g < 2:
                return yb[:, g, :, :, :]
            w = 2 * FT * C
            return r2t[0:P, (g - 2) * w:(g - 1) * w].rearrange("p (a t c) -> p a t c", a=2, t=FT)

        def step_at(st, d):
            s, h, nth = st
            return s + d, (h + d) % SB, nth + (h + d) // SB

        def steps(eng, body, lo, ahead):
            n = (NS - ahead - lo) // SB
            body([(s, s % SB, s // SB) for s in range(lo)])
            with eng.Fori(0, n) as i:
                body([(i * SB + (lo + k), (lo + k) % SB, i + (lo + k) // SB) for k in range(SB)])
            body([(s, s % SB, s // SB) for s in range(lo + n * SB, NS + 2)])

        def some(st):
            return not isinstance(st[0], int) or 0 <= st[0] < NS

        def inside(t):
            return not isinstance(t, int) or 0 <= t < T

        def overlapped(v, u, h0, nh, off):
            w = v[:, u, h0:h0 + nh, off:]
            return bass.AP(w.tensor, w.offset, [w.ap[0], [2 * D, nh], [1, OFF - off], [1, D]])

        def split(t, j):
            return t * (NJ // 2) + (j // 2 + 1)

        @block.sync
        def _(sp):
            sp.dma_start(src_i[:, :], src.rearrange("(p j) -> p j", p=P)).then_inc(src_loaded, 16)
            sp.dma_start(x_res[:, :, :], x.rearrange("(t p) c -> p t c", p=P)).then_inc(x_loaded, 16)
            sp.wait_ge(consts, 1)
            with sp.Fori(0, NR) as c:
                sp.dma_start(sorted_v[:, bass.ds(c * RT, RT), :],
                             zeros[:, :].rearrange("p (t f) -> p t f", f=F)).then_inc(zero_filled, 16)
            ea = edge_attr.rearrange("(p j) f -> p j f", p=P)

            def load_chunk(c, h):
                sp.dma_start(stage[:, h, :, 0:EA], ea[:, bass.ds(c * CH, CH), :]).then_inc(chunk_loaded[h], 16)

            load_chunk(0, 0)
            load_chunk(1, 1)
            with sp.Fori(0, NCH // 2 - 1) as i:
                for h in range(2):
                    sp.wait_ge(scattered[h], i * (16 * CH) + 16 * CH)
                    load_chunk(i * 2 + (2 + h), h)
            sp.wait_ge(scattered[0], (NCH // 2) * 16 * CH)
            load_chunk(NCH - 1, 0)

            sp.wait_ge(scattered[0], (NCH // 2 + 1) * 16 * CH)
            sp.wait_ge(scattered[1], (NCH // 2) * 16 * CH)
            sp.wait_ge(x1_ready, T)

            def load_rows(c, h):
                sp.dma_start(srt[:, h, :, :], sorted_v[:, bass.ds(c * RT, RT), :]).then_inc(rows_loaded[h], 16)

            for c in range(RB):
                load_rows(c, c)

            def reload_rows(c, h):
                sp.wait_ge(rows_used, c - (RB - 1))
                load_rows(c, h)
            for c in range(RB, RB + 3):
                reload_rows(c, c % RB)
            with sp.Fori(0, (NR - RB - 3) // RB) as i:
                for h in range(RB):
                    reload_rows(i * RB + (RB + 3 + h), (3 + h) % RB)
            hv = hpre_dram.rearrange("(t p) c -> t p c", p=128)

            def load_hpre(t, u, k):
                if not inside(t):
                    return
                wait(sp, hsum_ready, t - 1)
                sp.dma_start(hpre2[:, u, :], hv[bass.ds(t, 1), :, :].rearrange("a p c -> (a p) c")).then_inc(hpre_back[u], 16)
            sp.wait_ge(hpre_stored[0], 16 * (T // 2 + 1))
            sp.wait_ge(hpre_stored[1], 16 * (T // 2))
            load_hpre(0, 0, 0)
            load_hpre(1, 1, 0)
            sp.wait_ge(rows_used, NR)
            for k in range(KC):
                for dst, w in ((ew1_s, ew1), (ew2_s, ew2)):
                    sp.dma_start(dst[:, k, :].rearrange("p (e n) -> p e n", e=E),
                                 w.rearrange("e (k p) n -> k p e n", p=128)[k]).then_inc(ew_loaded, 16)
            sp.wait_ge(consts, 22)
            sp.dma_start(routed[E * REG:E * REG + 128, :], pad_rows[:, :]).then_inc(spare_filled, 16)
            for t in (2, 3):
                load_hpre(t, t % 2, 0)
            with sp.Fori(0, (T - 5) // 2) as i:
                for k in range(2):
                    load_hpre(i * 2 + (4 + k), k, 0)
            load_hpre(T - 1, 0, 0)

            sp.wait_ge(table_ready, 1)
            for c, count in ((0, T), (1, T), (2, E)):
                sp.wait_ge(routed_rows[c], 16 * count)
            sp.wait_ge(spare_filled, 16)

            def load_steps(sts):
                for s, h, nth in filter(some, sts):
                    row = sp.value_load(row_i[0:1, bass.ds(s, 1)], min_val=0, max_val=E * REG)
                    wait(sp, ys_ready, s - (SB - 1))
                    wait(sp, idx_ready, s - (SB - 1))
                    sp.dma_start(xs[:, h, :], routed[bass.ds(row, 128), :]).then_inc(xs_loaded[h], 16)
            steps(sp, load_steps, SB, 0)

            for h in range(SB):
                sp.wait_ge(ys_stored[h], 16 * ((NS - h + SB - 1) // SB))

            sp.wait_ge(ey_ps, NS)
            for g in range(T // FT):
                for c in range(2):
                    sp.dma_start(outputs_of(g)[:, c, :, :], youts[c * N + g * FT * P:c * N + (g + 1) * FT * P, :]
                                 .rearrange("(t p) c -> p t c", p=P)).then_inc(yb_loaded[g], 16)
            for g in range(T // FT):
                sp.wait_ge(yb_added, g + 1)
                sp.dma_start(out.rearrange("(t p) c -> p t c", p=P)[:, g * FT:(g + 1) * FT, :],
                             x_res[:, g * FT:(g + 1) * FT, :]).then_inc(stored, 16)
            sp.wait_ge(stored, 16 * (T // FT))

        @block.gpsimd
        def _(pool):
            n = [0]

            def iota(v, pattern, cm=0):
                pool.iota(v, pattern, base=0, channel_multiplier=cm,
                          allow_small_or_imprecise_dtypes=True).then_inc(consts, 1)

            pool.memset(zeros[:, :], 0.0).then_inc(consts, 1)
            iota(thr[:, :], [[P, T + 1]])
            iota(iota_g[:, :], [[S * GT, NG]])
            iota(iota_c[:, :], [[1, P]])
            pool.memset(ones[:, :], 1.0).then_inc(consts, 1)
            pool.memset(ident[:, :], 0.0).then_inc(consts, 1)
            pool.memset(upper[:, :], 0.0).then_inc(consts, 1)
            pool.memset(stage[:, :, :, EA:EA + 1], 1.0).then_inc(consts, 1)
            iota(rank8[:, :], [[-1, E]])
            iota(dst_row[:, :], [[P, T]], 1)
            iota(reg_start[:, :], [[REG, E]])
            iota(reg_part[:, :], [[0, E]], 1)
            iota(step_row[:, :], [[128, NS]])
            pool.memset(pad_rows[:, 0:C + 1], 0.0).then_inc(consts, 1)
            pool.memset(bias_more[:, :], 0.0).then_inc(bias_zeroed, 1)
            pool.iota(pad_rows[:, C + 1:XF], [[0, 1]], base=2 * N, channel_multiplier=1,
                      allow_small_or_imprecise_dtypes=True).then_inc(consts, 1)
            pool.memset(mask[:, :], SC4).then_inc(consts, 1)
            pool.memset(sq_half[:, :], 1.0).then_inc(consts, 1)
            pool.wait_ge(consts, 17)
            pool.affine_select(out=ident[:, :], in_=ident[:, :], compare_op=ALU.not_equal, fill=1.0, base=0,
                               pattern=[[-1, 128]], channel_multiplier=1).then_inc(consts, 1)
            pool.affine_select(out=upper[:, :], in_=upper[:, :], compare_op=ALU.is_ge, fill=1.0, base=0,
                               pattern=[[-1, P]], channel_multiplier=1).then_inc(consts, 1)
            pool.affine_select(out=sq_half[:, :], in_=sq_half[:, :], compare_op=ALU.is_ge, fill=0.5, base=-D,
                               pattern=[[0, 1]], channel_multiplier=1).then_inc(consts, 1)
            for lo, w in ((2 * LF - 1, SC2), (LF + 16, 1.0), (LF, SC4), (LF - 1, SC2), (16, 1.0)):
                pool.affine_select(out=mask[:, :], in_=mask[:, :], compare_op=ALU.is_ge, fill=w, base=-lo,
                                   pattern=[[0, 2 * VE]], channel_multiplier=1).then_inc(pool_step, 1)
                n[0] += 1
                pool.wait_ge(pool_step, n[0])
            pool.affine_select(out=mask[:, 0:VE], in_=mask[:, 0:VE], compare_op=ALU.is_ge, fill=0.0, base=LF - 1,
                               pattern=[[0, VE]], channel_multiplier=-1).then_inc(consts, 1)
            pool.affine_select(out=mask[:, VE:2 * VE], in_=mask[:, VE:2 * VE], compare_op=ALU.is_ge, fill=0.0, base=-LF,
                               pattern=[[0, VE]], channel_multiplier=1).then_inc(consts, 1)

            def pool_link(ins):
                n[0] += 1
                ins.then_inc(pool_step, 1)
                pool.wait_ge(pool_step, n[0])
            pool_link(pool.memset(ones3[:, :], 1.0))
            pool_link(pool.memset(ones3w[:, :], 1.0))
            pool.wait_ge(w_loaded, 16 * 15)
            pool_link(pool.tensor_tensor(bias_rows[:, :], bias_rows[:, :], bias_more[:, :], ALU.add))
            pool_link(pool.tensor_copy(bparts[:, 0, :], bias_rows[:, :]))
            pool_link(pool.tensor_tensor(brest[:, :], bias_rows[:, :], bparts[:, 0, :], ALU.subtract))
            pool_link(pool.tensor_copy(bparts[:, 1, :], brest[:, :]))
            pool_link(pool.tensor_tensor(brest[:, :], brest[:, :], bparts[:, 1, :], ALU.subtract))
            pool.tensor_copy(bparts[:, 2, :], brest[:, :]).then_inc(bias_ready, 1)

            pool.wait_ge(addr_ready, 1)
            pool_link(pool.memset(vn[:, :, :, :], 0.0))
            pool.memset(vr[:, :, :, :], 0.0).then_inc(mix_init, 1)
            pool.memset(vn[:, :, :, D:VE], 1.0 / N).then_inc(mix_init, 1)
            pool.memset(last[:, :, :, LF - 1:LF], 1.0).then_inc(mix_init, 1)
            pool.wait_ge(pool_step, n[0])
            pool.sem_inc(mix_init)

            pool.wait_ge(addr_ready, 1)
            pool.wait_ge(zero_filled, 16 * NR)

            def scatter(c, h, nth):
                hold(pool, chunk_loaded[h], nth * 16)
                if not (isinstance(nth, int) and nth == 1):
                    hold(pool, scattered[h], nth * (16 * CH) - 16 * CH)
                pool.tensor_copy(idx[:, h, :], addr[:, bass.ds(c * CH, CH)]).then_inc(chunk_keyed, 1)
                pool.tensor_copy(stage[:, h, :, EA + 1:EA + 2],
                                 src_f[:, bass.ds(c * CH, CH)].unsqueeze(2)).then_inc(chunk_keyed, 1)
                hold(pool, chunk_keyed, c * 2 + 2)
                for j in range(CH):
                    pool.indirect_dma_start(out=sorted_rows,
                                            out_offset=bass.IndirectOffsetOnAxis(ap=idx[:, h, j:j + 1], axis=0),
                                            in_=stage[:, h, j, :], in_offset=None).then_inc(scattered[h], 16)
            scatter(0, 0, 1)
            scatter(1, 1, 1)
            with pool.Fori(0, NCH // 2 - 1) as i:
                for h in range(2):
                    scatter(i * 2 + (2 + h), h, i + 2)
            scatter(NCH - 1, 0, NCH // 2 + 1)
            pool.wait_ge(x1_ready, T)
            pool.memset(aggT[EA:EA + 1, :], 1.0).then_inc(agg_one, 1)

            for b, (t0, t1) in enumerate(BATCHES):
                pool.wait_ge(meta_ready, b + 1)
                pool.wait_ge(xl_kept, t1)
                for c in range(2):
                    if c == 1 and t1 == T:
                        pool.wait_ge(pads_ready, 1)
                        for e in range(E):
                            pool.indirect_dma_start(out=routed,
                                                    out_offset=bass.IndirectOffsetOnAxis(ap=pad_idx[:, e:e + 1], axis=0),
                                                    in_=pad_rows[:, :], in_offset=None).then_inc(routed_rows[2], 16)
                    if c == 1:
                        pool.wait_ge(routed_rows[0], 16 * t1)
                    pool.tensor_copy(xl_all[:, t0:t1, C:XF], meta[:, c, t0:t1, :]).then_inc(meta_put, 1)
                    pool.wait_ge(meta_put, 2 * b + c + 1)
                    for t in range(t0, t1):
                        pool.indirect_dma_start(out=routed,
                                                out_offset=bass.IndirectOffsetOnAxis(ap=row_idx[:, c, t:t + 1], axis=0),
                                                in_=xl_all[:, t, :], in_offset=None).then_inc(routed_rows[c], 16)

            def scatter_outputs(sts):
                for s, h, nth in filter(some, sts):
                    hold(pool, ys_ready, s + 1)
                    hold(pool, idx_ready, s + 1)
                    pool.indirect_dma_start(out=youts, out_offset=bass.IndirectOffsetOnAxis(ap=y_idx[:, h:h + 1], axis=0),
                                            in_=ys[:, h, :], in_offset=None, bounds_check=2 * N - 1, oob_is_err=False).then_inc(ys_stored[h], 16)
            steps(pool, scatter_outputs, SB, 0)

        @block.scalar
        def _(act):
            def load(dst, s, slow=False):
                act.dma_start(dst, s, allow_slow_non_contiguous=slow).then_inc(w_loaded, 16)

            load(wqkv[:, :, :], WqkvT.rearrange("(k p) n -> p k n", p=128))
            load(w1x[:, :, :], W1[0:C, :].rearrange("(k p) n -> p k n", p=128))
            load(w1a[0:EA, :], W1[C:C + EA, :])
            load(w1u[:, :], W1[C + EA:C + EA + 128, :])
            load(bias_rows[0:3, :], bqkv.rearrange("(a n) -> a n", a=3))
            act.wait_ge(bias_zeroed, 1)
            load(bias_more[3:4, :], b2.rearrange("(a n) -> a n", a=1))
            load(w1a[EA:EA + 1, :], b1.rearrange("(a n) -> a n", a=1))
            load(bias_rows[3:4, :], bproj.rearrange("(a n) -> a n", a=1))
            load(u0[:, :], u_in[0:1, :].rearrange("a p -> p a"), slow=True)
            load(temp[:, :], temperature.rearrange("(a n) -> a n", a=1).to_broadcast([P, H]))
            load(wproj[:, :, :], WprojT.rearrange("(k p) n -> p k n", p=128))
            load(w2s[:, :, :], W2.rearrange("(k p) n -> p k n", p=128))
            load(wr[:, :, :], routerT.rearrange("(k p) n -> p k n", p=128))
            load(bias_rows[4:4 + E, :], eb1)
            load(bias_rows[4 + E:4 + 2 * E, :], eb2)

            act.wait_ge(x_loaded, 16)
            for t in range(T):
                act.activation(x_dev[:, t, :], x_res[:, t, :], ACT.Copy, accum_out=x_sum[:, t:t + 1]).then_inc(x_stats, 1)
            act.wait_ge(x_stats, T)
            act.activation(neg_mean[:, :], x_sum[:, :], ACT.Copy, scale=-1.0 / C).then_inc(x_stats, 1)
            act.wait_ge(x_stats, T + 1)
            for t in range(T):
                act.activation(x_dev[:, t, :], x_res[:, t, :], ACT.Square, bias=neg_mean[:, t:t + 1],
                               accum_out=rstd[:, t:t + 1]).then_inc(x_stats, 1)
            act.wait_ge(x_stats, 2 * T + 1)
            act.activation(rstd[:, :], rstd[:, :], ACT.Copy, scale=1.0 / C, bias=LN_EPS).then_inc(var_ready, 1)
            act.wait_ge(var_ready, 1)
            act.activation(rstd[:, :], rstd[:, :], ACT.Sqrt).then_inc(std_ready, 1)
            act.wait_ge(bias_ready, 1)
            for m in range(3):
                act.dma_start(bias3[m:m + 1, :, :], bparts[:, m, :]).then_inc(bias_spread, 16)
            def xT_copy(t, u):
                if not inside(t):
                    return
                wait(act, xT_ps, t + 1)
                wait(act, kv_ps, t - 1)
                act.activation(xT[:, u, :, :], bank(0, 128, 0, KC * P).rearrange("p (k c) -> p k c", k=KC),
                               ACT.Copy).then_inc(xT_ready, 1)

            def pass1(t, u, k):
                if inside(t):
                    wait(act, kv_ps, t + 1)
                    wait(act, phi_ready, t - 1)
                    act.activation(kdup[:, u, :, :].rearrange("p h (a d) -> p h a d", a=2),
                                   bank(1 + u, P, 0, C).rearrange("p (h d) -> p h d", h=H).unsqueeze(2)
                                   .to_broadcast([P, H, 2, D]), ACT.Copy).then_inc(kdup_ready, 1)
                    wait(act, m_added, t - 1)
                    act.activation(vn[:, u, :, 0:D], bank(1 + u, P, C, 2 * C).rearrange("p (h d) -> p h d", h=H),
                                   ACT.Copy, scale=1.0 / N).then_inc(vn_ready, 1)
                    act.activation(phi[:, u, :, 0, :], bank(1 + u, P, 0, C).rearrange("p (h d) -> p h d", h=H),
                                   ACT.Square).then_inc(ksq_ready, 1)
                    hold(act, xT_ready, t + 1)
                    act.activation(xT_all[:, :, bass.ds(t * P, P)], xT[:, u, :, :], ACT.Copy).then_inc(xT_kept, 1)
                    xT_copy(t + 1, 1 - u)
                    wait(act, rk2_ready, t + 1)
                    act.activation(rr[:, u, :], r2[:, u, :], ACT.Sqrt).then_inc(rk_ready, 1)
            xT_copy(0, 0)
            act.wait_ge(mix_init, 4)
            tiles(act, pass1, 3, 1, 0)

            act.wait_ge(m_added, T)

            def q_square(t, u):
                if not inside(t):
                    return
                wait(act, q_ps, t + 1)
                wait(act, qssq_ready, t - 1)
                act.activation(sqs[:, u, :], bank((0, 6)[u], P, 0, C), ACT.Square).then_inc(qsq_ready, 1)

            def q_root(t, u):
                if not inside(t):
                    return
                wait(act, qinv_ready, t + 1)
                act.activation(rr[:, u, :], r2[:, u, :], ACT.Sqrt).then_inc(qroot_ready, 1)

            def q_rows(t, u):
                if not inside(t):
                    return
                wait(act, qdup_ready, t + 1)
                wait(act, grp_ps[0], (t - 2) * (NJ // 2) + (H // 2 + 1))
                act.activation(last[:, u, :, 16:16 + D], kdup[:, u, :, 0:D], ACT.Copy).then_inc(qlin_ready, 1)

            def attn_copy(t, u):
                if not inside(t):
                    return
                wait(act, attnT_ps, t + 1)
                act.activation(attnT[:, u, :, :], bank(7, 128, 0, KC * P).rearrange("p (k c) -> p k c", k=KC),
                               ACT.Copy).then_inc(attnT_ready, 1)

            def pass2(t, u, k):
                if inside(t):
                    for j in range(NJ):
                        rows = 2 * LF if j == H else 128
                        if j < NJ - 1:
                            wait(act, grp_ps[j % 2], split(t, j))
                            wait(act, y_added[j % 2], t * (H // 2 + 1 - j % 2) + j // 2)
                            act.activation(phT[0:rows, j % 2, :], bank(1 + j % 2, rows, 0, QC * P),
                                           ACT.Copy).then_inc(grp_ready[j % 2], 1)
                        else:
                            wait(act, grp_ps[j % 2], split(t, j))
                            wait(act, hpre_stored[u], k * 16)
                            act.activation(hpre[:, u, :], bank(1 + j % 2, 128, 0, MC * P), ACT.Copy).then_inc(grp_ready[j % 2], 1)
                            hold(act, grp_ready[j % 2], split(t, j))
                            act.dma_start(hpre_dram[bass.ds(t * 128, 128), :], hpre[:, u, :]).then_inc(hpre_stored[u], 16)
                        if j == 2:
                            q_square(t + 2, u)
                        if j == 4:
                            q_root(t + 2, u)
                        if j == 5:
                            attn_copy(t - 1, 1 - u)
                        if j == 7:
                            q_rows(t + 2, u)
                else:
                    attn_copy(t - 1, 1 - u)
            for t in range(2):
                q_square(t, t)
                q_root(t, t)
                q_rows(t, t)
            tiles(act, pass2, 4, 3, 2)

            act.wait_ge(rows_used, NR)
            for b in range(NBK):
                nb = min(BPB, T - b * BPB) * P
                act.activation(cnt[EA:EA + 1, b * BPB * P:b * BPB * P + nb], ps[EA:EA + 1, b * BANK:b * BANK + nb],
                               ACT.Copy).then_inc(cnt_copied, 1)

            def relu(t, u):
                if not inside(t):
                    return
                wait(act, hsum_ready, t + 1)
                act.activation(hs[:, u, :], hs[:, u, :], ACT.Relu).then_inc(hs_ready, 1)

            def sd(t, u):
                if not inside(t):
                    return
                wait(act, ve2_ready, t + 1)
                act.activation(sd2[:, u, :], sd2[:, u, :], ACT.Sqrt).then_inc(sd2_ready, 1)

            def tok_copy(t, u):
                if not inside(t):
                    return
                wait(act, tok_ps, t + 1)
                wait(act, lg_ps, t - 1)
                act.activation(tokr[:, u, :], bank(5, 128, 0, KC * P), ACT.Copy).then_inc(tokr_ready, 1)
                hold(act, xl_ready, t + 1)
                act.activation(xl_all[:, bass.ds(t, 1), 0:C].rearrange("p a c -> p (a c)"), xl[:, u, :],
                               ACT.Copy).then_inc(xl_kept, 1)

            def gnn(t, u, k):
                relu(t, u)
                sd(t - 1, 1 - u)
                tok_copy(t - 3, 1 - u)

            def exps(b):
                t0, t1 = BATCHES[b]
                act.wait_ge(sh_ready, b + 1)
                act.activation(pr[:, t0:t1, :], pr[:, t0:t1, :], ACT.Exp).then_inc(ex_ready, 1)
            tiles(act, gnn, 6, 3, 4, ((12, lambda: exps(0)), (20, lambda: exps(1))))
            exps(2)

            def xsT_copy(st):
                if not some(st):
                    return
                s, h, nth = st
                wait(act, xs_ps, s + 1)
                wait(act, eh_ps, s - 1)
                act.activation(xsT[:, h % 2, :], bank(h % 2, 128, 0, C), ACT.Copy).then_inc(xsT_ready, 1)

            def gelu(st):
                if not some(st):
                    return
                s, h, nth = st
                wait(act, eh_ps, s + 1)
                wait(act, hg_ps, s - 1)
                act.activation(hg[:, h % 2, :], bank(2 + h % 2, 128, 0, C), ACT.Gelu).then_inc(hg_ready, 1)

            def expert_steps(sts):
                for st in sts:
                    xsT_copy(step_at(st, 2))
                    gelu(step_at(st, 1))
            xsT_copy((0, 0, 0))
            xsT_copy((1, 1, 0))
            gelu((0, 0, 0))
            steps(act, expert_steps, SB, 2)

        @block.tensor
        def _(pe):
            mm = pe.matmul
            pe.wait_ge(consts, 22)
            pe.wait_ge(counted, 1)
            mm(bank(0, P, 0, T), lhsT=upper[:, :], rhs=per_part[:, :], start=True, stop=True)
            mm(bank(1, 128, 0, T), lhsT=ones[0:P, :], rhs=per_part[:, :], start=True, stop=True).then_inc(totals_ps, 1)
            pe.wait_ge(starts, 1)
            pe.transpose(bank(2, T + 1, 0, 128), start[:, :], ident[:, :]).then_inc(starts_ps, 1)
            pe.wait_ge(w_loaded, 16 * 15)
            mm(ps[EA:EA + 1, 3 * BANK:3 * BANK + HID], lhsT=u0[:, :], rhs=w1u[:, :], start=True, stop=True).then_inc(brow_ps, 1)
            pe.wait_ge(geg_ready, 1)
            mm(bank(2, 128, 0, NG), lhsT=ones[0:T, :], rhs=geg[:, :], start=True, stop=True).then_inc(groups_ps, 1)
            pe.wait_ge(groups_read, 1)
            pe.wait_ge(bias_spread, 48)
            for b in (3, 4, 5, 6, 7):
                mm(bank(b), lhsT=zeros[:, 0:128], rhs=zeros[:, 0:BANK], start=True, stop=False, skip_group_check=True)

            def xT_of(t, u):
                if not inside(t):
                    return
                wait(pe, xn_ready, t + 1)
                wait(pe, xT_ready, t)
                for k in range(KC):
                    m = pe.transpose(bank(0, 128, k * P, (k + 1) * P), xn[:, u, k * 128:(k + 1) * 128], ident[0:P, 0:P])
                m.then_inc(xT_ps, 1)

            def project(dst, xt, c0, width):
                for k in range(KC):
                    mm(dst, lhsT=xt[:, k, :], rhs=wqkv[:, k, c0:c0 + width], start=(k == 0), stop=False)
                return mm(dst, lhsT=ones3[:, :], rhs=bias3[:, c0 // C:(c0 + width) // C, :].rearrange("p a c -> p (a c)"), start=False, stop=True)

            def sums(t, u):
                if not inside(t):
                    return
                wait(pe, vr_ready, t + 1)
                wait(pe, phi_ready, t + 1)
                wait(pe, ksq_ready, t + 1)
                for h in range(H):
                    a = VW * (h % 2)
                    mm(ps[a:a + VW, (4 + h // 2) * BANK:(5 + h // 2) * BANK], lhsT=vr[:, u, h, :],
                       rhs=phi[:, u, h, :, :].rearrange("p o d -> p (o d)"), start=False, stop=False, skip_group_check=True)
                wait(pe, last_ready, t + 1)
                for g in range(H // 2):
                    m = mm(bank(3, 2 * LF, g * 2 * VE, (g + 1) * 2 * VE),
                           lhsT=last[:, u, 2 * g:2 * g + 2, :].rearrange("p h f -> p (h f)"),
                           rhs=vn[:, u, 2 * g:2 * g + 2, 0:VE], start=False, stop=False, skip_group_check=True)
                m.then_inc(m_added, 1)

            def pass1(t, u, k):
                if inside(t):
                    wait(pe, xT_ready, t + 1)
                    wait(pe, kn_ready, t - 1)
                    wait(pe, vn_ready, t - 1)
                    project(bank(1 + u, P), xT[:, u], C, 2 * C).then_inc(kv_ps, 1)
                    xT_of(t + 1, 1 - u)
                sums(t - 1, 1 - u)
            xT_of(0, 0)
            tiles(pe, pass1, 3, 1, 1)

            def queries(t, u):
                if not inside(t):
                    return
                wait(pe, xr_ready, t + 1)
                wait(pe, qdup_ready, t - 1)
                project(bank((0, 6)[u], P, 0, C), xT[:, u], 0, C).then_inc(q_ps, 1)

            pe.wait_ge(xT_ready, T)
            queries(0, 0)

            for g in range(H // 2):
                pe.wait_ge(m_copied, g + 1)
                if g >= 2:
                    pe.wait_ge(mT_taken, g - 1)
                for c in range(QC):
                    m = pe.transpose(bank(1 + g % 2, 128, c * 128, (c + 1) * 128), phi_m[:, g, c * 128:(c + 1) * 128], ident[:, :])
                m.then_inc(mT_ps, 1)

            pe.wait_ge(m_copied, H // 2)

            def group(t, u, j):
                if j == 0:
                    wait(pe, qphi_ready[0], t + 1)
                if j == H // 2:
                    wait(pe, qphi_ready[1], t + 1)
                if j == H:
                    wait(pe, qlast_ready, t + 1)
                wait(pe, grp_ready[j % 2], split(t, j) - 1)
                if j < H:
                    for c in range(QC):
                        m = pe.transpose(bank(1 + j % 2, 128, c * P, (c + 1) * P),
                                         phi[:, u, j, c * 4:(c + 1) * 4, :].rearrange("p o d -> p (o d)"), ident[0:P, 0:P])
                elif j == H:
                    for g in range(H // 2):
                        m = pe.transpose(bank(1 + j % 2, 2 * LF, g * P, (g + 1) * P),
                                         last[:, u, 2 * g:2 * g + 2, :].rearrange("p h f -> p (h f)"), ident[0:P, 0:P])
                else:
                    for c in range(MC):
                        for kk in range(KC):
                            m = mm(bank(1 + j % 2, 128, c * P, (c + 1) * P), lhsT=w1x[:, kk, c * 128:(c + 1) * 128],
                                   rhs=xT_all[:, kk, bass.ds(t * P, P)], start=(kk == 0), stop=(kk == KC - 1))
                m.then_inc(grp_ps[j % 2], 1)

            def outputs(t, u, j):
                if isinstance(t, int) and t == 0 and j == 0:
                    pe.wait_ge(m_ready, 1)
                wait(pe, grp_ready[j % 2], split(t, j))
                if j == 0:
                    wait(pe, yT_ready, t - 1)

                def y(h):
                    a = VW * (h % 2)
                    return ps[a:a + VW, (3 + u) * BANK + (h // 2) * P:(3 + u) * BANK + (h // 2 + 1) * P]
                if j < H:
                    for c in range(QC):
                        m = mm(y(j), lhsT=mq[:, j // 2, c, (j % 2) * VW:(j % 2 + 1) * VW], rhs=phT[:, j % 2, c * P:(c + 1) * P],
                               start=(j < 2 and c == 0), stop=False, skip_group_check=True)
                else:
                    for h in range(H):
                        m = mm(y(h), lhsT=ml[:, h // 2, (h % 2) * VW:(h % 2 + 1) * VW],
                               rhs=phT[0:2 * LF, j % 2, (h // 2) * P:(h // 2 + 1) * P], start=False, stop=(h >= H - 2),
                               skip_group_check=True)
                m.then_inc(y_added[j % 2], 1)

            def y_T(t, u):
                if not inside(t):
                    return
                wait(pe, yT_ready, t + 1)
                wait(pe, attn_ready, t)
                for g in range(H // 2):
                    m = pe.transpose(bank(5, P, g * 2 * VW, (g + 1) * 2 * VW), yT[:, g * P:(g + 1) * P], ident[:, :])
                m.then_inc(y_ps, 1)

            def attn_T(t, u):
                if not inside(t):
                    return
                wait(pe, attn_ready, t + 1)
                wait(pe, x1_ready, t)
                for k in range(KC):
                    m = pe.transpose(bank(7, 128, k * P, (k + 1) * P), attn[:, u, k * 128:(k + 1) * 128], ident[0:P, 0:P])
                m.then_inc(attnT_ps, 1)

            def proj(t, u):
                if not inside(t):
                    return
                wait(pe, attnT_ready, t + 1)
                dst = bank(7, P, 256, 256 + C)
                for k in range(KC):
                    mm(dst, lhsT=attnT[:, u, k, :], rhs=wproj[:, k, :], start=(k == 0), stop=False)
                mm(dst, lhsT=ones3[:, :], rhs=bias3[:, 3, :], start=False, stop=True).then_inc(proj_ps, 1)

            def pass2(t, u, k):
                if inside(t):
                    for j in range(NJ):
                        group(t, u, j)
                        if j == 1:
                            queries(t + 2, u)
                        if j == 3:
                            y_T(t - 1, 1 - u)
                        if j == 5:
                            attn_T(t - 1, 1 - u)
                        if j == 7:
                            proj(t - 1, 1 - u)
                        if j >= 1:
                            outputs(t, u, j - 1)
                else:
                    y_T(t - 1, 1 - u)
                    attn_T(t - 1, 1 - u)
                    proj(t - 1, 1 - u)
            queries(1, 1)
            tiles(pe, pass2, 4, 3, 2)

            pe.wait_ge(x1_ready, T)
            for b in range(NBK):
                mm(bank(b, EA + 1), lhsT=zeros[:, 0:EA + 1], rhs=zeros[:, 0:BANK], start=True, stop=False, skip_group_check=True)

            pe.wait_ge(offs_ready, 1)

            def offset(c, g):
                return pe.value_load(off_i[0:1, bass.ds(c * RG + g, 1)], min_val=0,
                                     max_val=(T - 1) // BPB * BANK + (T - 1) % BPB * P)

            def add_rows(chunks):
                off = offset(chunks[0][0], 0)
                for n_, (c, h, o, nth) in enumerate(chunks):
                    wait(pe, rows_loaded[h], nth * 16)
                    hold(pe, onehot_ready, c + 1)
                    for g in range(RG):
                        here = off
                        if g + 1 < RG:
                            off = offset(c, g + 1)
                        elif n_ + 1 < len(chunks):
                            off = offset(chunks[n_ + 1][0], 0)
                        for k in range(GT):
                            m = mm(ps[0:EA + 1, bass.ds(here, P)], lhsT=srt[:, h, g * GT + k, 0:EA + 1],
                                   rhs=oh[:, o, g * GT + k, :], start=False, stop=False, skip_group_check=True)
                    m.then_inc(rows_used, 1)
            add_rows([(c, c, c % 2, 1) for c in range(3)])
            with pe.Fori(0, (NR - 3) // RB) as i:
                add_rows([(i * RB + (3 + k), (3 + k) % RB, (3 + k) % 2, i + (3 + k) // RB + 1) for k in range(RB)])
            for t in range(T):
                if t % BPB == 0:
                    pe.wait_ge(cnt_copied, t // BPB + 1)
                m = mm(bank(7, P, t, t + 1), lhsT=cnt[EA:EA + 1, t * P:(t + 1) * P], rhs=ones[EA:EA + 1, 0:1],
                       start=True, stop=True)
            m.then_inc(cnt_ps, 1)
            pe.wait_ge(inv_ready, 1)
            for b in range(NBK):
                pe.wait_ge(sums_copied, NBK)
                for t in range(b * BPB, min((b + 1) * BPB, T)):
                    m = mm(bank((b - 1) % 8, EA, t % BPB * P, (t % BPB + 1) * P), lhsT=cinv[:, t:t + 1].to_broadcast([P, EA]),
                           rhs=ident[0:P, 0:P], start=True, stop=True)
                m.then_inc(inv_ps, 1)

            pe.wait_ge(mean_ready, NBK)
            pe.wait_ge(agg_one, 1)

            def ha(t, u):
                if not inside(t):
                    return
                wait(pe, hsum_ready, t - 1)
                for m in range(MC):
                    z = mm(bank(1 + u, 128, m * P, (m + 1) * P), lhsT=w1a[:, m * 128:(m + 1) * 128], rhs=aggT[:, bass.ds(t * P, P)],
                           start=True, stop=True)
                z.then_inc(ha_ps, 1)

            def layer2(t, u):
                if not inside(t):
                    return
                wait(pe, hs_ready, t + 1)
                wait(pe, x2_ready, t - 1)
                for m in range(MC):
                    z = mm(bank(3 + u, P, 0, C), lhsT=hs[:, u, m * P:(m + 1) * P], rhs=w2s[:, m, :], start=(m == 0),
                           stop=(m == MC - 1))
                z.then_inc(gnn_ps, 1)

            def tok_T(t, u):
                if not inside(t):
                    return
                wait(pe, xl_ready, t + 1)
                wait(pe, tokr_ready, t)
                for k in range(KC):
                    m = pe.transpose(bank(5, 128, k * P, (k + 1) * P), xl[:, u, k * 128:(k + 1) * 128], ident[0:P, 0:P])
                m.then_inc(tok_ps, 1)

            def router(t, u):
                if not inside(t):
                    return
                wait(pe, tokr_ready, t + 1)
                wait(pe, lg_ready, t)
                for k in range(KC):
                    m = mm(bank(6, P, 0, E), lhsT=tokr[:, u, k * P:(k + 1) * P], rhs=wr[:, k, :], start=(k == 0), stop=(k == KC - 1))
                m.then_inc(lg_ps, 1)

            def gnn(t, u, k):
                ha(t, u)
                layer2(t - 1, 1 - u)
                tok_T(t - 3, 1 - u)
                router(t - 4, u)

            def ranks(b):
                t0, t1 = BATCHES[b]
                pe.wait_ge(mask_ready, b + 1)
                mm(bank(0, P, 0, (t1 - t0) * E), lhsT=upper[:, :], rhs=both[:, t0:t1, :].rearrange("p t e -> p (t e)"),
                   start=True, stop=True)
                mm(bank(7, 128, 0, (t1 - t0) * E), lhsT=ones[0:P, :], rhs=both[:, t0:t1, :].rearrange("p t e -> p (t e)"),
                   start=True, stop=True).then_inc(ranks_ps, 1)
            tiles(pe, gnn, 6, 3, 4, ((18, lambda: ranks(0)), (24, lambda: ranks(1))))
            ranks(2)

            pe.wait_ge(table_ready, 1)
            pe.wait_ge(ew_loaded, 16 * 2 * KC)

            def xs_T(st):
                if not some(st):
                    return
                s, h, nth = st
                wait(pe, xs_loaded[h], nth * 16 + 16)
                wait(pe, xsT_ready, s - 1)
                for k in range(KC):
                    m = pe.transpose(bank(h % 2, 128, k * 128, (k + 1) * 128), xs[:, h, k * 128:(k + 1) * 128], ident[:, :])
                m.then_inc(xs_ps, 1)

            def layer(dst, xt, w, bias_row, col):
                for k in range(KC):
                    mm(dst, lhsT=xt[:, k * 128:(k + 1) * 128], rhs=w[:, k, bass.ds(col, C)], start=(k == 0), stop=False)
                return mm(dst, lhsT=ones3w[:, :], rhs=bias3[:, bias_row:bias_row + E, :].rearrange("p e c -> p (e c)")[:, bass.ds(col, C)],
                          start=False, stop=True)

            def expert_of(st):
                return pe.value_load(exp_i[0:1, bass.ds(st[0], 1)], min_val=0, max_val=(E - 1) * C) if some(st) else None

            def hidden(st, col):
                if not some(st):
                    return
                s, h, nth = st
                wait(pe, xsT_ready, s + 1)
                hold(pe, hg_ready, s - 1)
                layer(bank(2 + h % 2, 128, 0, C), xsT[:, h % 2, :], ew1_s, 4, col).then_inc(eh_ps, 1)

            def hidden_T(st):
                if not some(st):
                    return
                s, h, nth = st
                wait(pe, hg_ready, s + 1)
                wait(pe, hT_ready, s - 1)
                for k in range(KC):
                    m = pe.transpose(bank(4 + h % 2, 128, k * 128, (k + 1) * 128), hg[:, h % 2, k * 128:(k + 1) * 128], ident[:, :])
                m.then_inc(hg_ps, 1)

            def output(st, col):
                if not some(st):
                    return
                s, h, nth = st
                wait(pe, hT_ready, s + 1)
                hold(pe, ys_ready, s - 1)
                layer(bank(6 + h % 2, 128, 0, C), hT[:, h % 2, :], ew2_s, 4 + E, col).then_inc(ey_ps, 1)

            def expert_steps(sts):
                cols = [expert_of(step_at(sts[0], -1)), expert_of(sts[0])]
                for st in sts:
                    xs_T(step_at(st, 2))
                    cols.append(expert_of(step_at(st, 1)))
                    hidden(step_at(st, 1), cols[-1])
                    hidden_T(st)
                    output(step_at(st, -1), cols[-3])
            xs_T((0, 0, 0))
            xs_T((1, 1, 0))
            hidden((0, 0, 0), expert_of((0, 0, 0)))
            steps(pe, expert_steps, SB, 2)

        @block.vector
        def _(v):
            n = [0]

            def link(ins):
                n[0] += 1
                ins.then_inc(dve_step, 1)
                v.wait_ge(dve_step, n[0])

            v.wait_ge(src_loaded, 16)
            v.wait_ge(consts, 17)
            link(v.tensor_copy(src_f[:, :], src_i[:, :]))
            link(v.memset(clast[:, 0:1], 0.0))
            link(v.memset(start[:, 0:1], 0.0))
            link(v.memset(ones_b[:, :], 1.0))
            link(v.tensor_tensor(ge, src_f[:, :].unsqueeze(1).to_broadcast([P, T + 1, ET]),
                                 thr[:, :].unsqueeze(2).to_broadcast([P, T + 1, ET]), ALU.is_ge))
            link(v.tensor_tensor(oneh, ge[:, 0:T, :], ge[:, 1:T + 1, :], ALU.subtract))
            link(v.tensor_tensor_scan(cum.rearrange("p b j -> p (b j)"), ones_b[:, 0:1].to_broadcast([P, T * ET]),
                                      oneh.rearrange("p b j -> p (b j)"), 0.0, ALU.mult, ALU.add))
            link(v.tensor_copy(clast[:, 1:T + 1], cum[:, :, ET - 1]))
            v.tensor_tensor(per_part[:, :], clast[:, 1:T + 1], clast[:, 0:T], ALU.subtract).then_inc(counted, 1)
            v.wait_ge(totals_ps, 1)
            link(v.tensor_scalar(tot_i[:, :], bank(1, 128, 0, T), float(S * GT - 1), None, ALU.add))
            link(v.tensor_scalar(tot_i[:, :], tot_i[:, :], -S * GT, None, ALU.bitwise_and))
            link(v.tensor_copy(padded[:, :], tot_i[:, :]))
            v.tensor_tensor_scan(start[:, 1:T + 1], ones[:, 0:T], padded[:, :], 0.0, ALU.mult, ALU.add).then_inc(starts, 1)
            v.wait_ge(starts, 1)
            link(v.tensor_tensor(base[:, :], bank(0, P, 0, T), clast[:, 0:T], ALU.subtract))
            link(v.scalar_tensor_tensor(base[:, :], base[:, :], -1.0, start[0:P, 0:T], ALU.add, ALU.add))
            for b in range(T):
                v.scalar_tensor_tensor(cum[:, b, :], cum[:, b, :], base[:, b:b + 1], oneh[:, b, :], ALU.add,
                                       ALU.mult).then_inc(dve_step, 1)
                n[0] += 1
            v.wait_ge(dve_step, n[0])
            link(v.tensor_reduce(pos, cum.rearrange("p b j -> p j b"), AX.X, ALU.add))
            link(v.tensor_copy(pos_i, pos))
            link(v.tensor_scalar(slot_t, pos_i, 7, None, ALU.arith_shift_right))
            link(v.tensor_scalar(slot_p, pos_i, S - 1, None, ALU.bitwise_and))
            v.scalar_tensor_tensor(addr[:, :], slot_p, float(ST), slot_t, ALU.mult, ALU.add).then_inc(addr_ready, 1)
            v.wait_ge(starts_ps, 1)
            link(v.tensor_copy(startT[:, :], bank(2, T, 0, 1)))
            v.tensor_scalar(geg[:, :], iota_g[:, :], startT[:, 0:1], None, ALU.is_ge).then_inc(geg_ready, 1)
            v.wait_ge(brow_ps, 1)
            link(v.tensor_tensor(w1a[EA:EA + 1, :], ps[EA:EA + 1, 3 * BANK:3 * BANK + HID], w1a[EA:EA + 1, :], ALU.add))
            link(v.tensor_scalar(temp[:, :], temp[:, :], SC2, None, ALU.mult))
            v.wait_ge(groups_ps, 1)
            v.tensor_scalar(bt[:, :], bank(2, 128, 0, NG), -1.0, None, ALU.add).then_inc(groups_read, 1)

            def bucket_offsets():
                v.wait_ge(groups_read, 1)
                link(v.tensor_scalar(off_f[:, :], bt[0:1, :], float(P), None, ALU.mult))
                for m in range(1, (T - 1) // BPB + 1):
                    link(v.tensor_scalar(off_g[:, :], bt[0:1, :], float(BPB * m), float(GAP), ALU.is_ge, ALU.mult))
                    link(v.tensor_tensor(off_f[:, :], off_f[:, :], off_g[:, :], ALU.add))
                link(v.tensor_copy(off_i[:, :], off_f[:, :]))
                v.tensor_scalar(bt[:, :], bt[:, :], float(P), None, ALU.mult).then_inc(offs_ready, 1)

            v.wait_ge(std_ready, 1)
            link(v.reciprocal(rstd[:, :], rstd[:, :]))
            def xn_of(t, u):
                if not inside(t):
                    return
                wait(v, xT_ps, t - 1)
                v.tensor_scalar(xn[:, u, :], x_res[:, bass.ds(t, 1), :].rearrange("p a c -> p (a c)"),
                                neg_mean[:, bass.ds(t, 1)], rstd[:, bass.ds(t, 1)], ALU.add, ALU.mult).then_inc(xn_ready, 1)

            def heads(ap, w):
                return ap.rearrange("p (h d) -> p h d", h=H) if w is None else ap.unsqueeze(2).to_broadcast([P, H, w])

            def keys(t, u):
                if not inside(t):
                    return
                kb = heads(bank(1 + u, P, 0, C), None)
                wait(v, ksq_ready, t + 1)
                v.tensor_reduce(ssq[:, u, :], phi[:, u, :, 0, :], AX.X, ALU.add).then_inc(ssq_ready, 1)
                wait(v, ssq_ready, t + 1)
                v.tensor_scalar(nm[:, u, :], ssq[:, u, :], EPS2, 1.0 / SC2, ALU.max, ALU.mult).then_inc(nm_ready, 1)
                wait(v, nm_ready, t + 1)
                v.reciprocal(r2[:, u, :], nm[:, u, :]).then_inc(rk2_ready, 1)
                wait(v, rk2_ready, t + 1)
                wait(v, vn_ready, t + 1)
                wait(v, m_added, t - 1)
                v.tensor_tensor(vr[:, u, :, 0:VE], vn[:, u, :, 0:VE], heads(r2[:, u, :], VE), ALU.mult).then_inc(vr_ready, 1)
                wait(v, kdup_ready, t + 1)
                v.tensor_tensor(phi[:, u, :, 1:, :], kb.unsqueeze(2).to_broadcast([P, H, OFF - 1, D]),
                                overlapped(kdup, u, 0, H, 1), ALU.mult).then_inc(phi_ready, 1)
                wait(v, rk_ready, t + 1)
                v.tensor_tensor(last[:, u, :, 16:16 + D], kb, heads(rr[:, u, :], D), ALU.mult).then_inc(kn_ready, 1)
                wait(v, kn_ready, t + 1)
                v.tensor_tensor(last[:, u, :, 0:16], last[:, u, :, 16:32], last[:, u, :, 32:48], ALU.mult).then_inc(last_ready, 1)

            def pass1(t, u, k):
                xn_of(t + 1, 1 - u)
                keys(t - 1, 1 - u)
            xn_of(0, 0)
            v.wait_ge(mix_init, 4)
            tiles(v, pass1, 3, 1, 1)

            def xr(t, u):
                if not inside(t):
                    return
                hold(v, q_ps, t - 1)
                v.tensor_copy(xT[:, u, :, :], xT_all[:, :, bass.ds(t * P, P)]).then_inc(xr_ready, 1)

            def norm_a(t, u):
                if not inside(t):
                    return
                wait(v, qsq_ready, t + 1)
                v.tensor_reduce(ssq[:, u, :], heads(sqs[:, u, :], None), AX.X, ALU.add).then_inc(qssq_ready, 1)
                wait(v, qssq_ready, t + 1)
                v.tensor_scalar(nm[:, u, :], ssq[:, u, :], SC2, EPS2, ALU.mult, ALU.max).then_inc(qnm_ready, 1)
                wait(v, qnm_ready, t + 1)
                v.reciprocal(r2[:, u, :], nm[:, u, :]).then_inc(qinv_ready, 1)

            def norm_b(t, u):
                if not inside(t):
                    return
                wait(v, qroot_ready, t + 1)
                v.tensor_tensor(rq[:, u, :], rr[:, u, :], temp[:, :], ALU.mult).then_inc(rq_ready, 1)
                wait(v, rq_ready, t + 1)
                v.tensor_tensor(kdup[:, u, :, :].rearrange("p h (a d) -> p h a d", a=2),
                                heads(bank((0, 6)[u], P, 0, C), None).unsqueeze(2).to_broadcast([P, H, 2, D]),
                                rq[:, u, :].unsqueeze(2).unsqueeze(2).to_broadcast([P, H, 2, D]), ALU.mult).then_inc(qdup_ready, 1)

            def products(t, u, g):
                if not inside(t):
                    return
                qb = kdup[:, u, :, 0:D]
                if g == 0:
                    wait(v, qdup_ready, t + 1)
                    wait(v, grp_ps[0], (t - 2) * (NJ // 2) + (H // 2 + 1))
                hh = slice(g * H // 2, (g + 1) * H // 2)
                v.tensor_tensor(phi[:, u, hh], qb[:, hh].unsqueeze(2).to_broadcast([P, H // 2, OFF, D]),
                                overlapped(kdup, u, g * H // 2, H // 2, 0), ALU.mult).then_inc(qphi_ready[g], 1)

            def pairs(t, u):
                if not inside(t):
                    return
                wait(v, qlin_ready, t + 1)
                v.tensor_tensor(last[:, u, :, 0:16], last[:, u, :, 16:32], last[:, u, :, 32:48], ALU.mult).then_inc(qlast_ready, 1)

            def x1(t, u):
                if not inside(t):
                    return
                wait(v, proj_ps, t + 1)
                xv = x_res[:, bass.ds(t, 1), :].rearrange("p a c -> p (a c)")
                v.tensor_tensor(xv, bank(7, P, 256, 256 + C), xv, ALU.add).then_inc(x1_ready, 1)

            def yT_copy(t, u):
                if not inside(t):
                    return
                wait(v, y_added[0], (t + 1) * (H // 2 + 1))
                wait(v, y_ps, t)
                v.tensor_copy(yT[:, :], bank(3 + u, 128, 0, (H // 2) * P)).then_inc(yT_ready, 1)

            def normalise(t, u):
                if not inside(t):
                    return
                wait(v, y_ps, t + 1)
                yv = bank(5, P).rearrange("p (h e) -> p h e", h=H)
                v.reciprocal(ry[:, u, :], yv[:, :, D:VE].rearrange("p h e -> p (h e)")).then_inc(ry_ready, 1)
                wait(v, ry_ready, t + 1)
                wait(v, attnT_ps, t - 1)
                v.tensor_tensor(heads(attn[:, u, :], None), yv[:, :, 0:D], heads(ry[:, u, :], D), ALU.mult).then_inc(attn_ready, 1)

            def pass2(t, u, k):
                products(t + 1, 1 - u, 0)
                yT_copy(t - 1, 1 - u)
                x1(t - 2, u)
                normalise(t - 1, 1 - u)
                norm_a(t + 2, u)
                products(t + 1, 1 - u, 1)
                norm_b(t + 2, u)
                pairs(t + 1, 1 - u)
                xr(t + 3, 1 - u)
            v.wait_ge(kv_ps, T)
            v.wait_ge(xT_kept, T)
            xr(0, 0)
            xr(1, 1)
            v.wait_ge(m_added, T)
            for g in range(H // 2):
                v.tensor_copy(phi_m[:, g, :], bank(4 + g)).then_inc(m_copied, 1)
            norm_a(0, 0)
            for g in range(H // 2):
                v.wait_ge(mT_ps, g + 1)
                v.tensor_scalar(mq[:, g, 0, :], bank(1 + g % 2, 128, 0, 128), sq_half[:, 0:1], None, ALU.mult)
                v.tensor_copy(mq[:, g, 1:QC, :], bank(1 + g % 2, 128, 128, QC * 128).rearrange("p (c e) -> p c e", c=QC - 1)).then_inc(mT_taken, 1)
            norm_b(0, 0)
            products(0, 0, 0)
            link(v.memset(ml, 0.0))
            v.tensor_tensor(ml.rearrange("p g (a e) -> p g a e", a=2)[:, :, :, 0:VE],
                            bank(3, 2 * LF, 0, H * VE).rearrange("p (g a e) -> p g a e", g=H // 2, a=2),
                            mask[:, :].rearrange("p (a e) -> p a e", a=2).unsqueeze(1).to_broadcast([2 * LF, H // 2, 2, VE]),
                            ALU.mult).then_inc(m_ready, 1)
            products(0, 0, 1)
            pairs(0, 0)
            norm_a(1, 1)
            norm_b(1, 1)
            xr(2, 0)

            tiles(v, pass2, 4, 3, 2, ((4, bucket_offsets),))
            v.wait_ge(offs_ready, 1)

            def onehots(c, h, o, nth):
                wait(v, rows_loaded[h], nth * 16)
                wait(v, rows_used, c - 1)
                v.tensor_tensor(key[:, o, :].rearrange("p (g k) -> p g k", g=RG),
                                srt[:, h, :, EA + 1].rearrange("p (g k) -> p g k", g=RG),
                                bt[:, bass.ds(c * RG, RG)].unsqueeze(2).to_broadcast([128, RG, GT]),
                                ALU.subtract).then_inc(key_ready, 1)
                hold(v, key_ready, c + 1)
                v.tensor_tensor(oh[:, o, :, :], iota_c[:, :].unsqueeze(1).to_broadcast([128, RT, P]),
                                key[:, o, :].unsqueeze(2).to_broadcast([128, RT, P]), ALU.is_equal).then_inc(onehot_ready, 1)
            for c in range(3):
                onehots(c, c, c % 2, 1)
            with v.Fori(0, (NR - 3) // RB) as i:
                for k in range(RB):
                    onehots(i * RB + (3 + k), (3 + k) % RB, (3 + k) % 2, i + (3 + k) // RB + 1)
            v.wait_ge(rows_used, NR)

            for b in range(NBK):
                nb = min(BPB, T - b * BPB) * P
                v.tensor_copy(aggT[0:EA, b * BPB * P:b * BPB * P + nb], bank(b, EA, 0, nb)).then_inc(sums_copied, 1)
            v.wait_ge(cnt_ps, 1)
            link(v.tensor_scalar(cmax, bank(7, P, 0, T), 1.0, None, ALU.max))
            link(v.reciprocal(cinv, cmax))
            v.sem_inc(inv_ready)
            for b in range(NBK):
                nb = min(BPB, T - b * BPB) * P
                v.wait_ge(inv_ps, b + 1)
                v.wait_ge(sums_copied, b + 1)
                v.tensor_tensor(aggT[0:EA, b * BPB * P:b * BPB * P + nb], bank((b - 1) % 8, EA, 0, nb),
                                aggT[0:EA, b * BPB * P:b * BPB * P + nb], ALU.mult).then_inc(mean_ready, 1)

            def hsum(t, u, k):
                if not inside(t):
                    return
                wait(v, ha_ps, t + 1)
                wait(v, hpre_back[u], k * 16 + 16)
                wait(v, gnn_ps, t - 1)
                v.tensor_tensor(hs[:, u, :], bank(1 + u, 128, 0, MC * P), hpre2[:, u, :], ALU.add).then_inc(hsum_ready, 1)

            def x2_of(t, u):
                if not inside(t):
                    return
                wait(v, gnn_ps, t + 1)
                wait(v, res_ready, t - 1)
                v.tensor_tensor(x2[:, u, :], bank(3 + u, P, 0, C), x_res[:, bass.ds(t, 1), :].rearrange("p a c -> p (a c)"),
                                ALU.add).then_inc(x2_ready, 1)
                wait(v, x2_ready, t + 1)
                v.bn_stats(st2[:, u, :], x2[:, u, :]).then_inc(st2_ready, 1)
                hold(v, st2_ready, t + 1)
                v.bn_aggr(mv2[:, u, :], st2[:, u, :]).then_inc(mv2_ready, 1)
                wait(v, mv2_ready, t + 1)
                v.tensor_scalar(sd2[:, u, :], mv2[:, u, 1:2], LN_EPS, None, ALU.add).then_inc(ve2_ready, 1)

            def xl_of(t, u):
                if not inside(t):
                    return
                wait(v, sd2_ready, t + 1)
                v.reciprocal(rs2[:, u, :], sd2[:, u, :]).then_inc(rs2_ready, 1)
                wait(v, rs2_ready, t + 1)
                wait(v, tok_ps, t - 1)
                wait(v, xl_kept, t - 1)
                v.tensor_scalar(xl[:, u, :], x2[:, u, :], mv2[:, u, 0:1], rs2[:, u, :], ALU.subtract, ALU.mult).then_inc(xl_ready, 1)
                wait(v, xl_ready, t + 1)
                v.tensor_tensor(x_res[:, bass.ds(t, 1), :].rearrange("p a c -> p (a c)"), x2[:, u, :], xl[:, u, :],
                                ALU.add).then_inc(res_ready, 1)

            def lg_of(t, u):
                if not inside(t):
                    return
                hold(v, lg_ps, t + 1)
                v.tensor_copy(lg[:, bass.ds(t, 1), :].rearrange("p a c -> p (a c)"), bank(6, P, 0, E)).then_inc(lg_ready, 1)

            def gnn(t, u, k):
                hsum(t, u, k)
                x2_of(t - 1, 1 - u)
                xl_of(t - 2, u)
                lg_of(t - 4, u)

            def wide(a):
                return a.unsqueeze(2).to_broadcast([P, a.shape[1], E])

            def choose(b):
                soften(b)
                pick_one(b, 0)
                pick_one(b, 1)
                weights(b)

            def soften(b):
                t0, t1 = BATCHES[b]
                n_ = t1 - t0
                p_, w_, k_, r_ = pr[:, t0:t1, :], pw[:, 0:n_, :], pick[:, 0:n_, :], red[:, 0:n_]
                v.wait_ge(lg_ready, t1)
                link(v.tensor_reduce(r_, lg[:, t0:t1, :], AX.X, ALU.max))
                v.tensor_tensor(p_, lg[:, t0:t1, :], wide(r_), ALU.subtract).then_inc(sh_ready, 1)
                v.wait_ge(ex_ready, b + 1)
                link(v.tensor_reduce(r_, p_, AX.X, ALU.add))
                link(v.reciprocal(r_, r_))
                link(v.tensor_tensor(p_, p_, wide(r_), ALU.mult))

            def pick_one(b, m):
                t0, t1 = BATCHES[b]
                n_ = t1 - t0
                p_, w_, k_, r_ = pr[:, t0:t1, :], pw[:, 0:n_, :], pick[:, 0:n_, :], red[:, 0:n_]
                best = top[:, m, t0:t1]
                eq = (first, second)[m][:, t0:t1, :]
                at_ = (p_, w_)[m]
                link(v.tensor_reduce(best, at_, AX.X, ALU.max))
                link(v.tensor_tensor(eq, at_, wide(best), ALU.is_equal))
                link(v.scalar_tensor_tensor(k_, rank8[:, :].unsqueeze(1).to_broadcast([P, n_, E]), float(E), eq,
                                            ALU.add, ALU.mult))
                link(v.tensor_reduce(r_, k_, AX.X, ALU.max))
                link(v.tensor_tensor(eq, k_, wide(r_), ALU.is_equal))
                if m == 0:
                    link(v.scalar_tensor_tensor(w_, eq, -2.0, p_, ALU.mult, ALU.add))
                else:
                    v.tensor_tensor(both[:, t0:t1, :], first[:, t0:t1, :], eq, ALU.add).then_inc(mask_ready, 1)

            def weights(b):
                t0, t1 = BATCHES[b]
                r_ = red[:, 0:t1 - t0]
                link(v.tensor_tensor(r_, top[:, 0, t0:t1], top[:, 1, t0:t1], ALU.add))
                link(v.tensor_scalar(r_, r_, 1e-12, None, ALU.max))
                link(v.reciprocal(r_, r_))
                link(v.tensor_tensor(meta[:, :, t0:t1, 0], top[:, :, t0:t1], r_.unsqueeze(1).to_broadcast([P, 2, t1 - t0]),
                                     ALU.mult))

            def place(b):
                t0, t1 = BATCHES[b]
                n_ = t1 - t0
                keep = keeps[n_]
                tot = tot_b[:, 0:E * n_].rearrange("p (e t) -> p e t", e=E)
                cumt = cumt_b[:, 0:E * n_].rearrange("p (e t) -> p e t", e=E)
                sl = slot[:, 0:n_, :]
                v.wait_ge(ranks_ps, b + 1)
                link(v.tensor_copy(tot, bank(7, 128, 0, n_ * E).rearrange("p (t e) -> p e t", e=E)))
                link(v.tensor_tensor_scan(cumt_b[:, 0:E * n_], keep.rearrange("p e t -> p (e t)"), tot_b[:, 0:E * n_],
                                          0.0, ALU.mult, ALU.add))
                link(v.tensor_tensor(sl, bank(0, P, 0, n_ * E).rearrange("p (t e) -> p t e", e=E),
                                     cumt[0:P].rearrange("p e t -> p t e"), ALU.add))
                link(v.tensor_tensor(sl, sl, tot[0:P].rearrange("p e t -> p t e"), ALU.subtract))
                link(v.tensor_tensor(sl, sl, carry[0:P, :].unsqueeze(1).to_broadcast([P, n_, E]), ALU.add))
                link(v.tensor_tensor(carry[:, :], carry[:, :], cumt[:, :, n_ - 1], ALU.add))
                if t1 == T:
                    link(v.tensor_tensor(e_n, reg_part[:, :], carry, ALU.add))
                    v.tensor_copy(pad_idx[:, :], e_n).then_inc(pads_ready, 1)
                for m in range(2):
                    link(v.tensor_tensor(pick[:, 0:n_, :], sl, (first, second)[m][:, t0:t1, :], ALU.mult))
                    link(v.tensor_reduce(red[:, 0:n_], pick[:, 0:n_, :], AX.X, ALU.add))
                    link(v.tensor_copy(row_idx[:, m, t0:t1], red[:, 0:n_]))
                v.sem_inc(meta_ready)

            for keep in keeps.values():
                link(v.memset(keep, 1.0))
                link(v.memset(keep[:, :, 0:1], 0.0))
            link(v.tensor_copy(carry, reg_start[:, :]))
            link(v.tensor_copy(meta[:, 0, :, 1], dst_row[:, :]))
            link(v.tensor_scalar(meta[:, 1, :, 1], dst_row[:, :], float(N), None, ALU.add))
            tiles(v, gnn, 6, 3, 4, (
                (12, lambda: soften(0)), (14, lambda: pick_one(0, 0)), (16, lambda: (pick_one(0, 1), weights(0))),
                (18, lambda: place(0)), (20, lambda: soften(1)), (22, lambda: pick_one(1, 0)),
                (23, lambda: (pick_one(1, 1), weights(1))), (25, lambda: place(1))))
            choose(2)
            place(2)
            link(v.tensor_tensor(e_n, carry, reg_start[:, :], ALU.subtract))
            link(v.tensor_scalar(e_i, e_n, 127.0, None, ALU.add))
            link(v.tensor_scalar(e_i, e_i, -128, None, ALU.bitwise_and))
            link(v.tensor_copy(e_pad, e_i[0:1, :]))
            link(v.tensor_tensor_scan(e_end, ones[0:1, 0:E], e_pad, 0.0, ALU.mult, ALU.add))
            link(v.tensor_tensor(past, step_row[:, :].unsqueeze(2).to_broadcast([1, NS, E]),
                                 e_end.unsqueeze(1).to_broadcast([1, NS, E]), ALU.is_ge))
            link(v.tensor_reduce(exp_f, past, AX.X, ALU.add))
            link(v.tensor_tensor(pasts, past, e_pad.unsqueeze(1).to_broadcast([1, NS, E]), ALU.mult))
            link(v.tensor_reduce(row_f, pasts, AX.X, ALU.add))
            link(v.tensor_tensor(row_f, step_row[:, :], row_f, ALU.subtract))
            link(v.scalar_tensor_tensor(row_f, exp_f, float(REG), row_f, ALU.mult, ALU.add))
            link(v.tensor_scalar(row_f, row_f, float(E * REG), None, ALU.min))
            link(v.tensor_copy(row_i[:, :], row_f))
            link(v.tensor_scalar(exp_f, exp_f, float(E - 1), float(C), ALU.min, ALU.mult))
            v.tensor_copy(exp_i[:, :], exp_f).then_inc(table_ready, 1)
            def hT_copy(st):
                if not some(st):
                    return
                s, h, nth = st
                wait(v, hg_ps, s + 1)
                wait(v, ey_ps, s - 1)
                v.tensor_copy(hT[:, h % 2, :], bank(4 + h % 2, 128, 0, C)).then_inc(hT_ready, 1)

            def output_rows(st):
                if not some(st):
                    return
                s, h, nth = st
                wait(v, xs_loaded[h], nth * 16 + 16)
                wait(v, ys_stored[h], nth * 16)
                v.tensor_copy(y_idx[:, h:h + 1], xs[:, h, C + 1:XF]).then_inc(idx_ready, 1)

            def weigh(st):
                if not some(st):
                    return
                s, h, nth = st
                wait(v, ey_ps, s + 1)
                wait(v, ys_stored[h], nth * 16)
                v.tensor_scalar(ys[:, h, :], bank(6 + h % 2, 128, 0, C), xs[:, h, C:C + 1], None, ALU.mult).then_inc(ys_ready, 1)

            def expert_steps(sts):
                for st in sts:
                    hT_copy(st)
                    output_rows(st)
                    weigh(step_at(st, -1))
            steps(v, expert_steps, SB, 2)

            v.wait_ge(res_ready, T)
            for g in range(T // FT):
                xv = x_res[:, g * FT:(g + 1) * FT, :]
                v.wait_ge(yb_loaded[g], 32)
                link(v.tensor_tensor(xv, xv, outputs_of(g)[:, 0, :, :], ALU.add))
                v.tensor_tensor(xv, xv, outputs_of(g)[:, 1, :, :], ALU.add).then_inc(yb_added, 1)


def kernel(**inputs):
    import numpy as _np
    import concourse.bacc as _bacc
    from concourse import mybir as _mybir
    from concourse.bass_utils import run_bass_kernel_spmd as _run

    f = {k: _np.asarray(a) for k, a in inputs.items()}
    laid = [
        ("x", f["x"]), ("src", f["src"]), ("edge_attr", f["edge_attr_64"]), ("u", f["L0_gnn_u"]),
        ("W1", f["L0_gnn_W1"]), ("b1", f["L0_gnn_b1"]), ("W2", f["L0_gnn_W2"]), ("b2", f["L0_gnn_b2"]),
        ("WqkvT", f["L0_mix_Wqkv"].T), ("bqkv", f["L0_mix_bqkv"]), ("WprojT", f["L0_mix_Wproj"].T),
        ("bproj", f["L0_mix_bproj"]), ("temperature", f["L0_mix_temperature"].reshape(-1)),
        ("routerT", f["L0_ffn_router_w"].T), ("ew1", f["L0_ffn_w1"]), ("eb1", f["L0_ffn_b1"]),
        ("ew2", f["L0_ffn_w2"]), ("eb2", f["L0_ffn_b2"]),
    ]
    nc = _bacc.Bacc("TRN2", target_bir_lowering=False, num_devices=1)
    arrays, args = {}, []
    for name, a in laid:
        a = _np.ascontiguousarray(a)
        arrays[f"in_{name}"] = a
        args.append(nc.dram_tensor(f"in_{name}", a.shape, _mybir.dt.from_np(a.dtype), kind="ExternalInput").ap())
    args.append(nc.dram_tensor("out_x", f["x"].shape, _mybir.dt.float32, kind="ExternalOutput").ap())
    gps_layer(nc, *args)
    r = _run(nc, [arrays], core_ids=[0])
    return r.results[0]["out_x"]
```
